# Optimizing a Trainium2 kernel written in Bass

```python
import numpy as np
import jax
import jax.numpy as jnp

def _softmax(x, axis=-1):
    return jax.nn.softmax(x, axis=axis)

def _gelu(x):
    return jax.nn.gelu(x, approximate=True)

def _silu(x):
    return jax.nn.silu(x)

def _sigmoid(x):
    return jax.nn.sigmoid(x)

def _layernorm(x, axis=-1, eps=1e-05):
    m = jnp.mean(x, axis=axis, keepdims=True)
    v = jnp.var(x, axis=axis, keepdims=True)
    return (x - m) / jnp.sqrt(v + eps)

def _scatter_add(tgt, idx, src, axis=0):
    return tgt.at[idx].add(src)

def _segment_sum(src, seg, n):
    return jax.ops.segment_sum(src, seg, n)
kernel_name = 'mk_prb_d2_jaxref_r8_b3cfeb'

def setup_inputs(seed: int=0):
    np.random.seed(seed)
    _w = jnp.asarray

    def _L0_attn_setup():
        import jax, jax.numpy as jnp
        import numpy as np
        N_HEADS = 16

        def _alibi_causal_mask(T, n_heads, dtype):
            slopes = (1.0 / jnp.power(2.0, jnp.arange(1, n_heads + 1, dtype=dtype)))[:, None, None]
            idx = jnp.arange(T)
            rel = (idx[None, :] - idx[:, None]).astype(dtype)
            alibi = jnp.tril(rel)
            causal = jnp.where(idx[None, :] > idx[:, None], -jnp.inf, 0.0).astype(dtype)
            return (alibi + causal)[None, :, :] * slopes
        key = jax.random.key(seed)
        ks = jax.random.split(key, 5)
        B, T, C = (2, 256, 128)
        scale = 0.02
        return {'x': jax.random.normal(ks[0], (B, T, C), dtype=jnp.float32), 'W_attn': jax.random.normal(ks[1], (C, 3 * C), dtype=jnp.float32) * scale, 'b_attn': jax.random.normal(ks[2], (3 * C,), dtype=jnp.float32) * scale, 'W_proj': jax.random.normal(ks[3], (C, C), dtype=jnp.float32) * scale, 'b_proj': jax.random.normal(ks[4], (C,), dtype=jnp.float32) * scale}
    _L0_attn_in = _L0_attn_setup()

    def _L0_ffn_setup():
        import jax, jax.numpy as jnp
        import numpy as np
        LN_EPS = 0.001
        EPS = 1e-05
        QB = 128.0

        def ste_round(x):
            return x + jax.lax.stop_gradient(jnp.round(x) - x)
        key = jax.random.key(seed)
        k1, k2 = jax.random.split(key)
        x = jax.random.normal(k1, (4, 1024, 128), dtype=jnp.float32)
        weight = jax.random.normal(k2, (128, 128), dtype=jnp.float32) * 0.02
        ln_gamma = jnp.ones((128,), dtype=jnp.float32)
        ln_beta = jnp.zeros((128,), dtype=jnp.float32)
        return {'x': x, 'weight': weight, 'ln_gamma': ln_gamma, 'ln_beta': ln_beta}
    _L0_ffn_in = _L0_ffn_setup()

    def _L1_attn_setup():
        import jax, jax.numpy as jnp
        import numpy as np
        B, S, DIM = (2, 1024, 128)
        NH, NKV, HD = (16, 4, 64)
        GROUPS = NH // NKV
        CHUNK = 128
        THETA = 10000.0

        def _slopes(h):
            return jnp.asarray([2.0 ** (-8.0 / h * (i + 1)) for i in range(h)], dtype=jnp.float32)

        def _rope_tables(s, d):
            inv = 1.0 / THETA ** (np.arange(0, d, 2, dtype=np.float64) / d)
            freqs = np.outer(np.arange(s, dtype=np.float64), inv)
            emb = np.concatenate([freqs, freqs], axis=-1)
            return (jnp.asarray(np.cos(emb), jnp.float32), jnp.asarray(np.sin(emb), jnp.float32))

        def _apply_rope(x, cos, sin):
            x1, x2 = jnp.split(x, 2, axis=-1)
            rot = jnp.concatenate([-x2, x1], axis=-1)
            return x * cos + rot * sin

        def _lightning_attn(q, k, v, slopes, chunk):
            b, h, s, d = q.shape
            nc = s // chunk
            t = jnp.arange(chunk, dtype=jnp.float32)
            sl = slopes[:, None, None]
            mask = jnp.where(t[:, None] >= t[None, :], jnp.exp(-sl * (t[:, None] - t[None, :])), 0.0)
            q_dec = jnp.exp(-slopes[:, None] * (t + 1.0))[..., None]
            k_dec = jnp.exp(-slopes[:, None] * (chunk - 1.0 - t))[..., None]
            blk_dec = jnp.exp(-slopes * chunk)[None, :, None, None]

            def to_chunks(x):
                return x.reshape(b, h, nc, chunk, d).transpose(2, 0, 1, 3, 4)
            qc, kc, vc = (to_chunks(q), to_chunks(k), to_chunks(v))

            def step(kv, inp):
                qi, ki, vi = inp
                scores = jnp.einsum('bhtd,bhsd->bhts', qi, ki) * mask
                o = jnp.einsum('bhts,bhsd->bhtd', scores, vi) + jnp.einsum('bhtd,bhde->bhte', qi * q_dec, kv)
                kv = blk_dec * kv + jnp.einsum('bhtd,bhte->bhde', ki * k_dec, vi)
                return (kv, o)
            kv0 = jnp.zeros((b, h, d, d), q.dtype)
            _, outs = jax.lax.scan(step, kv0, (qc, kc, vc))
            return outs.transpose(1, 2, 0, 3, 4).reshape(b, h, s, d)
        key = jax.random.key(seed)
        k0, k1, k2, k3, k4 = jax.random.split(key, 5)
        x = jax.random.normal(k0, (B, S, DIM), jnp.float32)
        Wq = jax.random.normal(k1, (NH * HD, DIM), jnp.float32) * 0.02
        Wk = jax.random.normal(k2, (NKV * HD, DIM), jnp.float32) * 0.02
        Wv = jax.random.normal(k3, (NKV * HD, DIM), jnp.float32) * 0.02
        Wo = jax.random.normal(k4, (DIM, NH * HD), jnp.float32) * 0.02
        return {'x': x, 'Wq': Wq, 'Wk': Wk, 'Wv': Wv, 'Wo': Wo}
    _L1_attn_in = _L1_attn_setup()

    def _L1_ffn_setup():
        import jax, jax.numpy as jnp
        import numpy as np
        B, S, D, O, E, R = (8, 256, 128, 128, 8, 4)
        TOP_K = 2
        SCALING = 4.0 / 4.0
        key = jax.random.key(seed)
        k0, k1, k2, k3, k4 = jax.random.split(key, 5)
        hidden_states = jax.random.normal(k0, (B, S, D), dtype=jnp.float32)
        W_lin = jax.random.normal(k1, (O, D), dtype=jnp.float32) * 0.02
        b_lin = jnp.zeros((O,), dtype=jnp.float32)
        gate_w = jax.random.normal(k2, (E, D), dtype=jnp.float32) * 0.02
        left = jax.random.normal(k3, (E, D, R), dtype=jnp.float32) * 0.02
        right = jax.random.normal(k4, (E, R, O), dtype=jnp.float32) * 0.02
        return {'hidden_states': hidden_states, 'W_lin': W_lin, 'b_lin': b_lin, 'gate_w': gate_w, 'left': left, 'right': right}
    _L1_ffn_in = _L1_ffn_setup()
    _d = {'L0_attn_x': _L0_attn_in['x'], 'L0_attn_W_attn': _L0_attn_in['W_attn'], 'L0_attn_b_attn': _L0_attn_in['b_attn'], 'L0_attn_W_proj': _L0_attn_in['W_proj'], 'L0_attn_b_proj': _L0_attn_in['b_proj'], 'L0_ffn_weight': _L0_ffn_in['weight'], 'L0_ffn_ln_gamma': _L0_ffn_in['ln_gamma'], 'L0_ffn_ln_beta': _L0_ffn_in['ln_beta'], 'L1_attn_Wq': _L1_attn_in['Wq'], 'L1_attn_Wk': _L1_attn_in['Wk'], 'L1_attn_Wv': _L1_attn_in['Wv'], 'L1_attn_Wo': _L1_attn_in['Wo'], 'L1_ffn_W_lin': _L1_ffn_in['W_lin'], 'L1_ffn_b_lin': _L1_ffn_in['b_lin'], 'L1_ffn_gate_w': _L1_ffn_in['gate_w'], 'L1_ffn_left': _L1_ffn_in['left'], 'L1_ffn_right': _L1_ffn_in['right']}
    _x0 = _d['L0_attn_x']
    _d['L0_attn_x'] = jax.random.normal(jax.random.fold_in(jax.random.key(seed), 1), (2, 1024, 128), dtype=_x0.dtype)
    del _x0
    return _d

def reference(L0_attn_x, L0_attn_W_attn, L0_attn_b_attn, L0_attn_W_proj, L0_attn_b_proj, L0_ffn_weight, L0_ffn_ln_gamma, L0_ffn_ln_beta, L1_attn_Wq, L1_attn_Wk, L1_attn_Wv, L1_attn_Wo, L1_ffn_W_lin, L1_ffn_b_lin, L1_ffn_gate_w, L1_ffn_left, L1_ffn_right):

    def _L0_attn_ref(x, W_attn, b_attn, W_proj, b_proj):
        import jax, jax.numpy as jnp
        import numpy as np
        N_HEADS = 16

        def _alibi_causal_mask(T, n_heads, dtype):
            slopes = (1.0 / jnp.power(2.0, jnp.arange(1, n_heads + 1, dtype=dtype)))[:, None, None]
            idx = jnp.arange(T)
            rel = (idx[None, :] - idx[:, None]).astype(dtype)
            alibi = jnp.tril(rel)
            causal = jnp.where(idx[None, :] > idx[:, None], -jnp.inf, 0.0).astype(dtype)
            return (alibi + causal)[None, :, :] * slopes
        B, T, C = x.shape
        H = N_HEADS
        D = C // H
        qkv = x @ W_attn + b_attn
        q, k, v = jnp.split(qkv, 3, axis=-1)
        q = q.reshape(B, T, H, D).transpose(0, 2, 1, 3)
        k = k.reshape(B, T, H, D).transpose(0, 2, 1, 3)
        v = v.reshape(B, T, H, D).transpose(0, 2, 1, 3)
        att = jnp.einsum('bhtd,bhsd->bhts', q, k) / jnp.sqrt(jnp.asarray(D, x.dtype))
        att = att + _alibi_causal_mask(T, H, x.dtype)[None]
        att = jax.nn.softmax(att, axis=-1)
        y = jnp.einsum('bhts,bhsd->bhtd', att, v)
        y = y.transpose(0, 2, 1, 3).reshape(B, T, C)
        return y @ W_proj + b_proj

    def _L0_ffn_ref(x, weight, ln_gamma, ln_beta):
        import jax, jax.numpy as jnp
        import numpy as np
        LN_EPS = 0.001
        EPS = 1e-05
        QB = 128.0

        def ste_round(x):
            return x + jax.lax.stop_gradient(jnp.round(x) - x)
        mu = jnp.mean(x, axis=-1, keepdims=True)
        var = jnp.var(x, axis=-1, keepdims=True)
        xn = (x - mu) * jax.lax.rsqrt(var + LN_EPS) * ln_gamma + ln_beta
        beta = jnp.mean(jnp.abs(weight))
        w_q = jnp.clip(ste_round(weight / (beta + EPS)), -1.0, 1.0)
        gamma = jnp.max(jnp.abs(xn))
        xq = jnp.clip(xn * QB / gamma, -QB + EPS, QB - EPS)
        y = jnp.einsum('bsd,du->bsu', xq, w_q)
        return y * (gamma * beta / QB)

    def _L1_attn_ref(x, Wq, Wk, Wv, Wo):
        import jax, jax.numpy as jnp
        import numpy as np
        B, S, DIM = (2, 1024, 128)
        NH, NKV, HD = (16, 4, 64)
        GROUPS = NH // NKV
        CHUNK = 128
        THETA = 10000.0

        def _slopes(h):
            return jnp.asarray([2.0 ** (-8.0 / h * (i + 1)) for i in range(h)], dtype=jnp.float32)

        def _rope_tables(s, d):
            inv = 1.0 / THETA ** (np.arange(0, d, 2, dtype=np.float64) / d)
            freqs = np.outer(np.arange(s, dtype=np.float64), inv)
            emb = np.concatenate([freqs, freqs], axis=-1)
            return (jnp.asarray(np.cos(emb), jnp.float32), jnp.asarray(np.sin(emb), jnp.float32))

        def _apply_rope(x, cos, sin):
            x1, x2 = jnp.split(x, 2, axis=-1)
            rot = jnp.concatenate([-x2, x1], axis=-1)
            return x * cos + rot * sin

        def _lightning_attn(q, k, v, slopes, chunk):
            b, h, s, d = q.shape
            nc = s // chunk
            t = jnp.arange(chunk, dtype=jnp.float32)
            sl = slopes[:, None, None]
            mask = jnp.where(t[:, None] >= t[None, :], jnp.exp(-sl * (t[:, None] - t[None, :])), 0.0)
            q_dec = jnp.exp(-slopes[:, None] * (t + 1.0))[..., None]
            k_dec = jnp.exp(-slopes[:, None] * (chunk - 1.0 - t))[..., None]
            blk_dec = jnp.exp(-slopes * chunk)[None, :, None, None]

            def to_chunks(x):
                return x.reshape(b, h, nc, chunk, d).transpose(2, 0, 1, 3, 4)
            qc, kc, vc = (to_chunks(q), to_chunks(k), to_chunks(v))

            def step(kv, inp):
                qi, ki, vi = inp
                scores = jnp.einsum('bhtd,bhsd->bhts', qi, ki) * mask
                o = jnp.einsum('bhts,bhsd->bhtd', scores, vi) + jnp.einsum('bhtd,bhde->bhte', qi * q_dec, kv)
                kv = blk_dec * kv + jnp.einsum('bhtd,bhte->bhde', ki * k_dec, vi)
                return (kv, o)
            kv0 = jnp.zeros((b, h, d, d), q.dtype)
            _, outs = jax.lax.scan(step, kv0, (qc, kc, vc))
            return outs.transpose(1, 2, 0, 3, 4).reshape(b, h, s, d)
        b, s, _ = x.shape
        q = (x @ Wq.T).reshape(b, s, NH, HD).transpose(0, 2, 1, 3)
        k = (x @ Wk.T).reshape(b, s, NKV, HD).transpose(0, 2, 1, 3)
        v = (x @ Wv.T).reshape(b, s, NKV, HD).transpose(0, 2, 1, 3)
        cos, sin = _rope_tables(s, HD)
        q = _apply_rope(q, cos, sin)
        k = _apply_rope(k, cos, sin)
        k = jnp.repeat(k, GROUPS, axis=1)
        v = jnp.repeat(v, GROUPS, axis=1)
        out = _lightning_attn(q, k, v, _slopes(NH), CHUNK)
        out = out.transpose(0, 2, 1, 3).reshape(b, s, NH * HD)
        return out @ Wo.T

    def _L1_ffn_ref(hidden_states, W_lin, b_lin, gate_w, left, right):
        import jax, jax.numpy as jnp
        import numpy as np
        B, S, D, O, E, R = (8, 256, 128, 128, 8, 4)
        TOP_K = 2
        SCALING = 4.0 / 4.0
        bsz, seq, d_in = hidden_states.shape
        x = hidden_states.reshape(-1, d_in)
        logits = x @ gate_w.T
        scores = jax.nn.softmax(logits, axis=-1)
        weights, idx = jax.lax.top_k(scores, TOP_K)
        base = x @ W_lin.T + b_lin
        left_sel = left[idx]
        right_sel = right[idx]
        t = jnp.einsum('nd,nkdr->nkr', x, left_sel)
        out_k = jnp.einsum('nkr,nkro->nko', t, right_sel)
        lora = jnp.sum(weights[..., None] * out_k, axis=1) * SCALING
        return (base + lora).reshape(bsz, seq, -1)
    x = L0_attn_x
    xn = _layernorm(x, axis=-1)
    x = x + _L0_attn_ref(xn, L0_attn_W_attn, L0_attn_b_attn, L0_attn_W_proj, L0_attn_b_proj) + _L0_ffn_ref(xn, L0_ffn_weight, L0_ffn_ln_gamma, L0_ffn_ln_beta)
    xn = _layernorm(x, axis=-1)
    x = x + _L1_attn_ref(xn, L1_attn_Wq, L1_attn_Wk, L1_attn_Wv, L1_attn_Wo) + _L1_ffn_ref(xn, L1_ffn_W_lin, L1_ffn_b_lin, L1_ffn_gate_w, L1_ffn_left, L1_ffn_right)
    return x

_drawn_inputs = setup_inputs


def setup_inputs(seed=0):
    import zlib

    import numpy as np

    out = dict(_drawn_inputs(seed))
    spreads = {'L0_ffn_ln_gamma': (1.0, 0.2), 'L0_ffn_ln_beta': (0.0, 0.474), 'L1_ffn_b_lin': (0.0, 0.1)}
    factors = {'L0_attn_W_attn': 5.699,
     'L0_attn_b_attn': 8.0,
     'L0_attn_W_proj': 5.06,
     'L0_attn_b_proj': 2.756,
     'L1_ffn_gate_w': 8.0,
     'L1_ffn_left': 8.0,
     'L1_ffn_right': 8.0}
    for name, (base, spread) in spreads.items():
        noise = np.random.default_rng([zlib.crc32(name.encode()), seed]).standard_normal(out[name].shape)
        drawn = base * np.exp(spread * noise) if base else spread * noise
        out[name] = jnp.asarray(drawn.astype(out[name].dtype))
    for name, factor in factors.items():
        out[name] = (out[name] * factor).astype(out[name].dtype)
    return out
```

```python
from contextlib import ExitStack

import concourse.bass as bass
from concourse import mybir

F32 = mybir.dt.float32
BF16 = mybir.dt.bfloat16
ALU = mybir.AluOpType
ACT = mybir.ActivationFunctionType
AX = mybir.AxisListType
RED = bass.bass_isa.ReduceOp

P = 128
B, T, C = 2, 1024, 128
NT = B * T // P
TPB = T // P
SPAN = 512
NSPAN = B * T // SPAN
TPS = SPAN // P

H0, D0 = 16, 8
GH = 4
NG = H0 // GH
GROUPS = [(b, g) for b in range(B) for g in range(NG)]
ALIBI_ROWS = 4
QK_ROWS = 9 * D0
MAX_K = 96
EXP_K = MAX_K + 3
VW = 16
STRIP = 32

H1, KV1, D1 = 16, 4, 64
QT = H1 * D1 // P

E1, R1, TOPK = 8, 4, 2
GL = E1 + E1 * R1

WCOLS = {}
_at = 0
for _name, _n in [("attn", 3 * C), ("proj", C), ("ffn0", C), ("q1", H1 * D1), ("q1rot", H1 * D1),
                  ("k1", KV1 * D1), ("k1rot", KV1 * D1), ("v1", KV1 * D1), ("wo1", QT * C), ("lin1", C),
                  ("gl1", GL), ("bq", 1), ("bk", 1), ("bproj", 1), ("lng", 1), ("lnb", 1), ("blin", 1),
                  ("bv", C)]:
    WCOLS[_name] = (_at, _at + _n)
    _at += _n
NW = _at
CCOLS = {}
_at = 0
for _name, _n in [("cos", T), ("sin", T), ("decay", H1 * P), ("qdec", QT * P), ("kdec", H1),
                  ("blkdec", QT * P), ("ident", P)]:
    CCOLS[_name] = (_at, _at + _n)
    _at += _n
NC_ = _at

UNITS = [(0, [(0, 0, 512)]), (0, [(1, 1, 384), (3, 3, 128)]), (0, [(2, 2, 256)]),
         (1, [(0, 4, 512)]), (1, [(1, 4, 512)]), (1, [(2, 4, 512)]), (1, [(3, 4, 512)]),
         (1, [(4, 4, 512)]), (1, [(5, 5, 384), (7, 7, 128)]), (1, [(6, 6, 256)])]
NU = len(UNITS)
NSTEP = NU * len(GROUPS)
UNIT_W = [sum(n for _, _, n in segs) for _, segs in UNITS]
MAXU = [[(h, a, 0)] + ([(h, b_, a + 1)] if b_ is not None else [])
        for h in range(GH) for a, b_ in ((7, None), (6, 0), (5, 1), (4, 2))]
MAXU += [[(h, 3, 0), (h + 1, 3, 4)] for h in (0, 2)]
NMAX = len(MAXU)
P_SLOTS = 3
ST_BANKS = 3
OP_SLOTS = 3
LEAD = 15


def item_stream():
    out = []
    for n in range(len(GROUPS)):
        for u in range(NMAX):
            out.append(("max", n, u))
            if u == 1 and n:
                out.append(("turn", n - 1, 0))
    return out + [("turn", len(GROUPS) - 1, 0)]


ITEMS = item_stream()
_per = (NMAX + 1) / NU
TURN_AT = {n: k for k, (kind, n, _) in enumerate(ITEMS) if kind == "turn"}
TRI = []
for _s in range(NSTEP):
    TRI.append((TRI[-1] if TRI else 0) + sum(i0 == j for j, i0, _ in UNITS[_s % NU][1]))


def items_of_step(s):
    lo = 0 if s == 0 else min(len(ITEMS), int((s + LEAD) * _per))
    hi = min(len(ITEMS), int((s + 1 + LEAD) * _per)) if s < NSTEP - 1 else len(ITEMS)
    return range(lo, hi)


def build(nc, x, w, wright, consts, alibi_q, alibi_k, masks, out):
    alibi_q, alibi_k, masks = (v.bitcast(BF16) for v in (alibi_q, alibi_k, masks))
    with ExitStack() as ctx:
        def sb(name, shape, dt=F32, c=ctx):
            return c.enter_context(nc.sbuf_tensor(name, shape, dt))

        def sem(name):
            return ctx.enter_context(nc.semaphore(name))

        PS = ctx.enter_context(nc.psum_tensor("PS", [P, 8, 512], F32))

        x_sb = sb("x_sb", [P, NT, C])
        w_sb = sb("w_sb", [P, NW])
        c_sb = sb("c_sb", [P, NC_])
        right_sb = sb("right_sb", [E1 * R1, C])
        W = {n: w_sb[:, a:b] for n, (a, b) in WCOLS.items()}
        K = {n: c_sb[:, a:b] for n, (a, b) in CCOLS.items()}
        masks_sb = sb("masks_sb", [P, 2, P], BF16)
        ident_b, causal_b = masks_sb[:, 0, :], masks_sb[:, 1, :]
        xn = sb("xn", [P, NT, C])
        xnT = sb("xnT", [P, B * T])
        stats = sb("stats", [P, NT, 6])
        mv = sb("mv", [P, NT, 2])
        std = sb("std", [P, NT])
        rstd = sb("rstd", [P, NT])

        l0 = ExitStack()
        xn2T = sb("xn2T", [P, B * T], c=l0)
        split = ExitStack()
        part = sb("part", [P, 2, 3, SPAN], BF16, split)
        rest = sb("rest", [P, 3, SPAN], F32, split)
        split.close()
        yacc = sb("yacc", [P, len(GROUPS), T], F32, l0)
        mrow = sb("mrow", [P, 2, T], BF16, l0)
        sT = sb("sT", [P, 2, SPAN], F32, l0)
        y = xnT[:, :].rearrange("p (a n c) -> p a n c", n=TPS, c=C)
        yT = xn[:, 4:12, :].rearrange("p (a n) c -> p a (n c)", a=2)
        wq_a, wq_b, wq_c = xn[:, 0, :], xn[:, 1, :], xn[:, 2, :]
        vaug = sb("vaug", [P, NT, H0, VW], F32, l0)
        q_op = sb("q_op", [P, OP_SLOTS, GH, T], BF16, l0)
        k_op = sb("k_op", [P, OP_SLOTS, GH, T], BF16, l0)
        prob = sb("prob", [P, P_SLOTS, GH, SPAN], F32, l0)
        pmax = sb("pmax", [P, NMAX, TPB], F32, l0)
        rmax = sb("rmax", [P, GH, TPB], F32, l0)
        rleft = sb("rleft", [P, 2, GH, TPB], F32, l0)
        mpart = sb("mpart", [P, TPB, GH, 3], BF16, l0)
        rden = sb("rden", [P, 2, TPS, GH], F32, l0)
        small = sb("small", [P, 8], F32, l0)
        l0.close()

        l1 = ExitStack()
        gates = ExitStack()
        gl_sb = sb("gl_sb", [P, NT, GL], F32, gates)
        ex = sb("ex", [P, NT, E1], F32, gates)
        sc = sb("sc", [P, NT, 2 * E1], F32, gates)
        col = sb("col", [P, 3, NT], F32, gates)
        top = sb("top", [P, NT, 8], F32, gates)
        kept = sb("kept", [P, NT, 2 * E1], F32, gates)
        tw = sb("tw", [P, NT, E1 * R1], F32, gates)
        gates.close()
        twT = xn[0:E1 * R1, :, :].rearrange("p n c -> p (n c)")
        faded = sb("faded", [P, QT, P], F32, l1)
        rope_a = sb("rope_a", [P, 2, SPAN], F32, l1)
        rope_b = sb("rope_b", [P, 2, SPAN], F32, l1)
        qr = sb("qr", [P, 2, QT, SPAN], F32, l1)
        kr = sb("kr", [P, 2, 2, SPAN], F32, l1)
        kz = sb("kz", [P, 2, KV1, 2, SPAN], F32, l1)
        kt_sb = sb("kt_sb", [P, 2, 2, P], F32, l1)
        v_sb = sb("v_sb", [P, 2, KV1 * D1], F32, l1)
        vdec = sb("vdec", [P, 2, KV1, H1 // KV1, D1], F32, l1)
        qd = sb("qd", [P, 2, QT, P], F32, l1)
        sm = sb("sm", [P, 2, SPAN], F32, l1)
        state = sb("state", [P, 2, QT, P], F32, l1)
        oT = sb("oT", [P, QT, SPAN], F32, l1)
        fT = sb("fT", [P, 2, SPAN], F32, l1)
        l1.close()

        q_scr = nc.dram_tensor("q_scr", [B, H0, 3 * D0, T], BF16, kind="Internal").ap()
        k_scr = nc.dram_tensor("k_scr", [B, H0, 3 * D0, T], BF16, kind="Internal").ap()

        s_load = sem("s_load")
        s_x = [sem(f"s_x{i}") for i in range(NSPAN)]
        dve = sem("dve")
        s_clear = sem("s_clear")
        s_var = sem("s_var")
        s_std = sem("s_std")
        s_xn = sem("s_xn")
        fillA, freeA = sem("fillA"), sem("freeA")
        fillD, freeD = sem("fillD"), sem("freeD")
        s_part = sem("s_part")
        s_scr = [sem(f"s_scr{i}") for i in range(2)]
        s_op = [sem(f"s_op{i}") for i in range(OP_SLOTS)]
        s_vaug = sem("s_vaug")
        s_gmax = sem("s_gmax")
        s_gall = sem("s_gall")
        s_ffn = sem("s_ffn")
        s_item, s_item_used = sem("s_item"), sem("s_item_used")
        s_mpart = sem("s_mpart")
        s_mop = [sem(f"s_mop{i}") for i in range(2)]
        s_st = sem("s_st")
        s_exp = sem("s_exp")
        s_tri = sem("s_tri")
        s_pv = sem("s_pv")
        s_acc = sem("s_acc")
        s_out = sem("s_out")
        s_glx = sem("s_glx"); s_ex = sem("s_ex"); s_tw = sem("s_tw")
        s_zero = sem("s_zero")
        s_pj, s_pj_free = sem("s_pj"), sem("s_pj_free")
        s_qr = sem("s_qr"); s_kr = sem("s_kr")
        s_ks = [sem(f"s_ks{i}") for i in range(2)]
        s_v = sem("s_v"); s_vd = sem("s_vd"); s_qd = sem("s_qd")
        s_sc, s_sm = sem("s_sc"), sem("s_sm")
        s_kv = sem("s_kv")
        s_state, s_faded = sem("s_state"), sem("s_faded")
        s_o, s_oT = sem("s_o"), sem("s_oT")

        RA, RD = [], []
        for i in range(NSPAN):
            RA.append(("xnT", i))
        for i in range(NSPAN):
            RA.append(("xn2T", i))
            RD += [("q", i), ("k", i), ("v", i)]
        A1 = len(RA)
        D1_ = len(RD)
        for i in range(NSPAN):
            RD += [("yt", i, g) for g in range(NG)] + [("back", i)]
            RA += [("yT", i), ("proj", i)]
        A2, D2 = len(RA), len(RD)
        for i in range(NSPAN):
            RA.append(("xn1T", i))
        for i in range(NSPAN):
            RD.append(("gl", i))
        for i in range(NSPAN):
            RA.append(("twT", i))
        PJ_SPAN = 2 * (2 + QT) + TPS + 2

        def sums(c):
            return c - c // TPB

        def states(c):
            return 2 * sums(c)

        A_at = {n: i for i, n in enumerate(RA)}
        D_at = {n: i for i, n in enumerate(RD)}

        block = ctx.enter_context(nc.Block())

        @block.sync
        def _(sp):
            xt = x.rearrange("(n p) c -> p n c", p=P)
            for i in range(NSPAN):
                sp.dma_start(x_sb[:, TPS * i:TPS * i + TPS, :], xt[:, TPS * i:TPS * i + TPS, :]).then_inc(s_x[i], 16)
                if i == 0:
                    sp.dma_start(w_sb[:, :], w).then_inc(s_load, 16)
                    sp.dma_start(masks_sb[:, :, :], masks).then_inc(s_load, 16)
                    sp.dma_start(c_sb[:, :], consts).then_inc(s_load, 16)
                    sp.dma_start(right_sb[:, :], wright).then_inc(s_load, 16)

            def load_ops(n):
                b, g = GROUPS[n]
                slot = n % OP_SLOTS
                if n >= OP_SLOTS:
                    sp.wait_ge(s_st, GH * NU * (n - OP_SLOTS + 1))
                for h in range(GH):
                    hh = g * GH + h
                    sp.dma_start(q_op[ALIBI_ROWS:ALIBI_ROWS + QK_ROWS, slot, h, :],
                                 q_scr[b, hh].rearrange("(o r) t -> o r t", o=1).broadcast_to([3, 3 * D0, T])).then_inc(s_op[slot], 16)
                    for c3 in range(3):
                        r0 = ALIBI_ROWS + 3 * D0 * c3
                        sp.dma_start(k_op[r0:r0 + 3 * D0, slot, h, :],
                                     k_scr[b, hh, D0 * c3:D0 * c3 + D0].rearrange("(o d) t -> o d t", o=1)
                                     .broadcast_to([3, D0, T])).then_inc(s_op[slot], 16)
                    sp.dma_start(q_op[0:ALIBI_ROWS, slot, h, :], alibi_q[hh]).then_inc(s_op[slot], 16)

            def load_m(n):
                slot = n % OP_SLOTS
                sp.wait_ge(s_item_used, TURN_AT[n] + 1)
                for h in range(GH):
                    sp.dma_start(q_op[MAX_K:MAX_K + 3, slot, h, :],
                                 mrow[MAX_K + 3 * h:MAX_K + 3 * h + 3, n % 2, :]).then_inc(s_mop[n % 2], 16)

            for i in range(2 * NSPAN):
                sp.wait_ge(s_part, i + 1)
                scr = q_scr if i % 2 == 0 else k_scr
                b, half = divmod(i // 2, 2)
                for a in range(3):
                    sp.dma_start(scr[b, :, D0 * a:D0 * a + D0, SPAN * half:SPAN * half + SPAN],
                                 part[:, i % 2, a, :]).then_inc(s_scr[i % 2], 16)
            for i in range(2):
                sp.wait_ge(s_scr[i], 3 * 16 * NSPAN)
            sp.wait_ge(s_clear, 2)
            for slot in range(OP_SLOTS):
                for h in range(GH):
                    sp.dma_start(k_op[0:ALIBI_ROWS, slot, h, :], alibi_k[0:ALIBI_ROWS]).then_inc(s_op[slot], 16)
                    sp.dma_start(k_op[MAX_K:EXP_K, slot, h, :], alibi_k[ALIBI_ROWS:ALIBI_ROWS + 3]).then_inc(s_op[slot], 16)
            for n in range(OP_SLOTS):
                load_ops(n)
            load_m(0)
            load_m(1)
            for n in range(2, len(GROUPS)):
                if n + 1 < len(GROUPS):
                    load_ops(n + 1)
                load_m(n)

            for i in range(NSPAN):
                for pr in range(2):
                    sp.wait_ge(s_kr, 2 * i + pr + 1)
                    if i >= 2:
                        sp.wait_ge(s_o, KV1 * TPS * (i - 1))
                        sp.wait_ge(s_kv, sums(TPS * (i - 1)))
                    for half in range(2):
                        g = 2 * pr + half
                        src = kr[64 * half:64 * half + 64, i % 2, pr, :]
                        for q in range(2):
                            sp.dma_start(kz[64 * q:64 * q + 64, i % 2, g, q, :], src).then_inc(s_ks[i % 2], 16)
            ot = out.rearrange("(n p) c -> p n c", p=P)
            for i in range(NSPAN):
                sp.wait_ge(s_pj_free, PJ_SPAN * (i + 1))
                sp.dma_start(ot[:, TPS * i:TPS * i + TPS, :], x_sb[:, TPS * i:TPS * i + TPS, :]).then_inc(s_out, 16)
            sp.wait_ge(s_out, 16 * NSPAN)

        OP_FIRST = 16 * GH * 2
        OP_EACH = 16 * GH * 5

        @block.tensor
        def _(pe):
            mm, tr = nc.tensor.matmul, nc.tensor.transpose

            def unit_a(name):
                k = A_at[name]
                if k >= 4:
                    pe.wait_ge(freeA, k - 3)
                return PS[:, k % 4, :]

            def unit_d(name):
                k = D_at[name]
                if k >= 4:
                    pe.wait_ge(freeD, k - 3)
                return PS[:, 4 + k % 4, :]

            pe.wait_ge(s_load, 64)
            for i in range(NSPAN):
                ps = unit_a(("xnT", i))
                pe.wait_ge(s_xn, TPS * (i + 1))
                for j in range(TPS):
                    last = tr(ps[:, P * j:P * j + P], xn[:, TPS * i + j, :], K["ident"])
                last.then_inc(fillA, 1)
            for i in range(NSPAN):
                pe.wait_ge(freeA, i + 1)
                cs = slice(SPAN * i, SPAN * i + SPAN)
                for n, name in enumerate("qk"):
                    mm(unit_d((name, i)), W["attn"][:, C * n:C * n + C], xnT[:, cs], start=True, stop=True).then_inc(fillD, 1)
                ps = unit_d(("v", i))
                for j in range(TPS):
                    last = mm(ps[:, P * j:P * j + P], xnT[:, SPAN * i + P * j:SPAN * i + P * j + P],
                              W["attn"][:, 2 * C:3 * C], start=True, stop=True)
                last.then_inc(fillD, 1)
            for i in range(NSPAN):
                ps = unit_a(("xn2T", i))
                pe.wait_ge(s_xn, NT + TPS * (i + 1))
                for j in range(TPS):
                    last = tr(ps[:, P * j:P * j + P], xn[:, TPS * i + j, :], K["ident"])
                last.then_inc(fillA, 1)

            pe.wait_ge(freeA, A1)
            pe.wait_ge(freeD, D1_)

            def item(k):
                kind, n, u = ITEMS[k]
                if k >= 2:
                    pe.wait_ge(s_item_used, k - 1)
                ring = 3 + 2 * (k % 2)
                if kind == "max":
                    slot = n % OP_SLOTS
                    if u == 0:
                        pe.wait_ge(s_op[slot], OP_FIRST + OP_EACH * (n // OP_SLOTS + 1))
                    for h, i, at in MAXU[u]:
                        j = 0
                        while j <= i:
                            c0 = at + j
                            nb = min(i + 1 - j, 4 - c0 % 4)
                            o = PS[:, ring + c0 // 4, P * (c0 % 4):P * (c0 % 4 + nb)]
                            diag = j + nb == i + 1
                            last = mm(o, q_op[0:MAX_K, slot, h, P * i:P * i + P], k_op[0:MAX_K, slot, h, P * j:P * (j + nb)],
                                      start=True, stop=not diag, skip_group_check=True)
                            if diag:
                                last = mm(o[:, P * (nb - 1):P * nb], ident_b, causal_b, start=False, stop=True,
                                          skip_group_check=True)
                            j += nb
                    last.then_inc(s_item, 1)
                else:
                    pe.wait_ge(s_mpart, n + 1)
                    o = PS[MAX_K:MAX_K + 3 * GH, ring, :].bitcast(BF16)
                    for i in range(TPB):
                        last = tr(o[:, P * i:P * i + P], mpart[:, i, :, :].rearrange("p h a -> p (h a)"), ident_b)
                    last.then_inc(s_item, 1)

            def scores(s):
                n, u = divmod(s, NU)
                slot = n % OP_SLOTS
                if u == 0:
                    pe.wait_ge(s_mop[n % 2], 16 * GH * (n // 2 + 1))
                for h in range(GH):
                    k = GH * s + h
                    if k >= ST_BANKS:
                        pe.wait_ge(s_exp, k - ST_BANKS + 1)
                    at = 0
                    for j, i0, nn in UNITS[u][1]:
                        last = mm(PS[:, k % ST_BANKS, at:at + nn], k_op[0:EXP_K, slot, h, P * j:P * j + P],
                                  q_op[0:EXP_K, slot, h, P * i0:P * i0 + nn], start=True, stop=True)
                        at += nn
                    last.then_inc(s_st, 1)

            def pv(s):
                n, u = divmod(s, NU)
                b, g = GROUPS[n]
                half, segs = UNITS[u]
                pe.wait_ge(s_exp, GH * (s + 1))
                pe.wait_ge(s_tri, TRI[s])
                if u in (0, 3):
                    pe.wait_ge(s_acc, 1 + 2 * n + (u == 3))
                at = 0
                for j, i0, nn in segs:
                    c0 = P * i0 - SPAN * half
                    for h in range(GH):
                        last = mm(PS[STRIP * h:STRIP * h + VW, 7, c0:c0 + nn], vaug[:, TPB * b + j, g * GH + h, :],
                                  prob[:, s % P_SLOTS, h, at:at + nn], start=(j == 0),
                                  stop=(u in (2, 9)), skip_group_check=True)
                    at += nn
                last.then_inc(s_pv, 1)

            for k in items_of_step(0):
                item(k)
            for s in range(NSTEP + 1):
                if s < NSTEP:
                    scores(s)
                if 0 < s < NSTEP:
                    for k in items_of_step(s):
                        item(k)
                if s:
                    pv(s - 1)

            pe.wait_ge(s_exp, GH * NSTEP)
            pe.wait_ge(s_item_used, len(ITEMS))
            pe.wait_ge(s_acc, 1 + 2 * len(GROUPS))
            pe.wait_ge(s_ffn, 1 + NSPAN)

            def turn_heads(i):
                b, half = divmod(i, 2)
                for g in range(NG):
                    ps = unit_d(("yt", i, g))
                    for j in range(TPS):
                        last = tr(ps[:, P * j:P * j + P],
                                  yacc[:, NG * b + g, SPAN * half + P * j:SPAN * half + P * j + P], K["ident"])
                    last.then_inc(fillD, 1)

            def project(i):
                ps = unit_a(("yT", i))
                pe.wait_ge(freeD, D_at[("yt", i, NG - 1)] + 1)
                for j in range(TPS):
                    last = tr(ps[:, P * j:P * j + P], y[:, i % 2, j, :], K["ident"])
                last.then_inc(fillA, 1)
                ps = unit_a(("proj", i))
                mm(ps, wq_c[:, :], xn2T[:, SPAN * i:SPAN * i + SPAN], start=True, stop=False)
                pe.wait_ge(freeA, A_at[("yT", i)] + 1)
                mm(ps, W["proj"], yT[:, i % 2, :], start=False, stop=True).then_inc(fillA, 1)

            def back(i):
                pe.wait_ge(freeA, A_at[("proj", i)] + 1)
                ps = unit_d(("back", i))
                for j in range(TPS):
                    last = tr(ps[:, P * j:P * j + P], sT[:, i % 2, P * j:P * j + P], K["ident"])
                last.then_inc(fillD, 1)

            for i in range(NSPAN):
                turn_heads(i)
                project(i)
                back(i)

            for i in range(NSPAN):
                ps = unit_a(("xn1T", i))
                pe.wait_ge(s_xn, 2 * NT + TPS * (i + 1))
                for j in range(TPS):
                    last = tr(ps[:, P * j:P * j + P], xn[:, TPS * i + j, :], K["ident"])
                last.then_inc(fillA, 1)
            for i in range(NSPAN):
                pe.wait_ge(freeA, A_at[("xn1T", i)] + 1)
                ps = unit_d(("gl", i))
                for j in range(TPS):
                    last = mm(ps[:, GL * j:GL * j + GL], xnT[:, SPAN * i + P * j:SPAN * i + P * j + P], W["gl1"],
                              start=True, stop=True)
                last.then_inc(fillD, 1)
            for i in range(NSPAN):
                ps = unit_a(("twT", i))
                pe.wait_ge(s_tw, 1)
                for j in range(TPS):
                    last = tr(ps[0:E1 * R1, P * j:P * j + P], tw[:, TPS * i + j, :], K["ident"])
                last.then_inc(fillA, 1)

            pe.wait_ge(freeA, len(RA))
            pe.wait_ge(freeD, len(RD))

            pj = [0]

            def proj_bank():
                k = pj[0]
                pj[0] += 1
                if k >= 2:
                    pe.wait_ge(s_pj_free, k - 1)
                return PS[:, k % 2, :]

            def span_proj(i):
                cs = slice(SPAN * i, SPAN * i + SPAN)
                for pr in range(2):
                    for name in ("k1", "k1rot"):
                        mm(proj_bank(), W[name][:, P * pr:P * pr + P], xnT[:, cs], start=True, stop=True).then_inc(s_pj, 1)
                for kt in range(QT):
                    for name in ("q1", "q1rot"):
                        mm(proj_bank(), W[name][:, P * kt:P * kt + P], xnT[:, cs], start=True, stop=True).then_inc(s_pj, 1)

            def chunk_kv(c):
                i, ch = divmod(c, TPS)
                ps = proj_bank()
                mm(ps[:, 0:KV1 * D1], xnT[:, P * c:P * c + P], W["v1"], start=True, stop=True)
                if ch == 0:
                    pe.wait_ge(s_kr, 2 * (i + 1))
                for pr in range(2):
                    last = tr(ps[:, 256 + P * pr:256 + P * pr + P], kr[:, i % 2, pr, P * ch:P * ch + P], K["ident"])
                last.then_inc(s_pj, 1)

            def chunk_attn(c):
                i, ch = divmod(c, TPS)
                first = c % TPB == 0
                last_c = c % TPB == TPB - 1
                pe.wait_ge(s_qr, QT * (i + 1))
                if ch == 0:
                    pe.wait_ge(s_ks[i % 2], 16 * 8 * (i // 2 + 1))
                    if c == 0:
                        pe.wait_ge(s_zero, 2)

                def score(g):
                    m = KV1 * c + g
                    if m >= 2:
                        pe.wait_ge(s_sm, m - 1)
                    for q in range(2):
                        last = mm(PS[:, 2 + m % 2, 256 * q:256 * q + 256].rearrange("p (a t) -> p a t", a=2),
                                  kz[:, i % 2, g, q, P * ch:P * ch + P],
                                  qr[:, i % 2, 2 * g:2 * g + 2, P * ch:P * ch + P], start=True, stop=True,
                                  skip_group_check=True)
                    last.then_inc(s_sc, 1)

                def mix(g):
                    m = KV1 * c + g
                    if g % 2 == 0 and c:
                        pe.wait_ge(s_oT, 2 * (c - 1) + g // 2 + 1)
                    if g == 0:
                        pe.wait_ge(s_pj_free, PJ_SPAN * i + 2 * (2 + QT) + ch + 1)
                    pe.wait_ge(s_sm, m + 1)
                    o = PS[:, 4 + g // 2, 256 * (g % 2):256 * (g % 2) + 256]
                    for q in range(2):
                        last = mm(o[64 * q:64 * q + 64, :], v_sb[:, c % 2, D1 * g:D1 * g + D1],
                                  sm[:, m % 2, 256 * q:256 * q + 256], start=True, stop=first, skip_group_check=True)
                    if not first:
                        if g == 0:
                            pe.wait_ge(s_qd, c + 1)
                            pe.wait_ge(s_state, states(c))
                        for a in range(2):
                            last = mm(o[:, P * a:P * a + P], state[:, c % 2, 2 * g + a, :], qd[:, c % 2, 2 * g + a, :],
                                      start=False, stop=True, skip_group_check=True)
                    last.then_inc(s_o, 1)

                score(0)
                for g in range(KV1):
                    if g + 1 < KV1:
                        score(g + 1)
                    mix(g)
                if not last_c:
                    pe.wait_ge(s_vd, KV1 * (c + 1))
                    if c:
                        pe.wait_ge(s_state, states(c))
                    for g in range(KV1):
                        kk = kt_sb[:, c % 2, g // 2, D1 * (g % 2):D1 * (g % 2) + D1]
                        o = PS[:, 6 + g // 2, 256 * (g % 2):256 * (g % 2) + 256]
                        for q in range(2):
                            last = mm(o[64 * q:64 * q + 64, :], kk,
                                      vdec[:, c % 2, g, :, :].rearrange("p h e -> p (h e)"), start=True, stop=True,
                                      skip_group_check=True)
                    last.then_inc(s_kv, 1)

            def span_out(i):
                ps = proj_bank()
                pe.wait_ge(s_oT, 2 * TPS * (i + 1))
                cs = slice(SPAN * i, SPAN * i + SPAN)
                mm(ps, W["lin1"], xnT[:, cs], start=True, stop=False)
                mm(ps, right_sb[:, :], twT[:, cs], start=False, stop=False)
                for kt in range(QT):
                    last = mm(ps, W["wo1"][:, C * kt:C * kt + C], oT[:, kt, :], start=False, stop=(kt == QT - 1))
                last.then_inc(s_pj, 1)
                pe.wait_ge(s_pj_free, PJ_SPAN * (i + 1) - 1)
                ps = proj_bank()
                for j in range(TPS):
                    last = tr(ps[:, P * j:P * j + P], fT[:, i % 2, P * j:P * j + P], K["ident"])
                last.then_inc(s_pj, 1)

            for i in range(NSPAN):
                span_proj(i)
                for ch in range(TPS):
                    chunk_kv(TPS * i + ch)
                    chunk_attn(TPS * i + ch)
                span_out(i)


        @block.vector
        def _(v):
            n_dve = [0]
            vec = nc.vector

            def link(ins):
                n_dve[0] += 1
                ins.then_inc(dve, 1)
                v.wait_ge(dve, n_dve[0])

            def note(ins):
                n_dve[0] += 1
                return ins.then_inc(dve, 1)

            def settle():
                v.wait_ge(dve, n_dve[0])

            def layer_norm(src, dst, eps, turn):
                for i in range(NT):
                    if turn == 0 and i % TPS == 0:
                        v.wait_ge(s_x[i // TPS], 16)
                    note(vec.bn_stats(out=stats[:, i, :], in_=src[:, i, :]))
                settle()
                for i in range(NT):
                    note(vec.bn_aggr(out=mv[:, i, :], in_=stats[:, i, :]))
                settle()
                n_dve[0] += 1
                vec.tensor_scalar(std[:, :], mv[:, :, 1], eps, None, ALU.add).then_inc(s_var, 1)
                n_dve[0] -= 1
                v.wait_ge(s_std, turn + 1)
                link(vec.reciprocal(rstd[:, :], rstd[:, :]))
                for i in range(NT):
                    vec.tensor_scalar(dst[:, i, :], src[:, i, :], mv[:, i, 0:1], rstd[:, i:i + 1],
                                      ALU.subtract, ALU.mult).then_inc(s_xn, 1)
                v.wait_ge(s_xn, NT * (turn + 1))

            def wait_d(name):
                k = D_at[name]
                v.wait_ge(fillD, k + 1)
                return PS[:, 4 + k % 4, :]

            link(vec.memset(vaug[:, :, :, :], 0.0))
            vec.memset(vaug[:, :, :, D0:D0 + 1], 1.0).then_inc(s_vaug, 1)
            layer_norm(x_sb, xn, 1e-5, 0)
            v.wait_ge(s_load, 64)
            v.wait_ge(s_vaug, 1)
            for i in range(NSPAN):
                for n, name in enumerate("qk"):
                    k = 2 * i + n
                    ps = wait_d((name, i))
                    if n == 0:
                        ins = vec.tensor_scalar(rest[:, 0, :], ps, W["bq"], float(D0) ** -0.5, ALU.add, ALU.mult)
                    else:
                        ins = vec.tensor_scalar(rest[:, 0, :], ps, W["bk"], None, ALU.add)
                    ins.then_inc(freeD, 1)
                    v.wait_ge(freeD, D_at[(name, i)] + 1)
                    if k >= 2:
                        v.wait_ge(s_scr[n], 3 * 16 * i)
                    link(vec.tensor_copy(part[:, n, 0, :], rest[:, 0, :]))
                    link(vec.tensor_tensor(rest[:, 1, :], rest[:, 0, :], part[:, n, 0, :], ALU.subtract))
                    link(vec.tensor_copy(part[:, n, 1, :], rest[:, 1, :]))
                    link(vec.tensor_tensor(rest[:, 2, :], rest[:, 1, :], part[:, n, 1, :], ALU.subtract))
                    vec.tensor_copy(part[:, n, 2, :], rest[:, 2, :]).then_inc(s_part, 1)
                    v.wait_ge(s_part, k + 1)
                ps = wait_d(("v", i))
                ins = vec.tensor_tensor(vaug[:, TPS * i:TPS * i + TPS, :, 0:D0],
                                        ps.rearrange("p (n h d) -> p n h d", n=TPS, d=D0),
                                        W["bv"].rearrange("p (a h d) -> p a h d", a=1, d=D0).broadcast_to([P, TPS, H0, D0]), ALU.add)
                ins.then_inc(freeD, 1)
                v.wait_ge(freeD, D_at[("v", i)] + 1)
            v.wait_ge(fillA, NSPAN)
            layer_norm(xn, xn, 1e-3, 1)
            link(vec.tensor_reduce(small[:, 0:1], W["ffn0"], AX.X, ALU.add, apply_absolute_value=True))
            v.wait_ge(freeA, A1)
            vec.tensor_reduce(small[:, 1:2], xn2T[:, :], AX.X, ALU.max, apply_absolute_value=True).then_inc(s_gmax, 1)
            v.wait_ge(s_gall, 2)
            link(vec.tensor_scalar(small[:, 0:1], small[:, 2:3], 1.0 / (C * C), None, ALU.mult))
            link(vec.tensor_scalar(small[:, 4:5], small[:, 0:1], 1e-5, None, ALU.add))
            link(vec.reciprocal(small[:, 4:5], small[:, 4:5]))
            link(vec.tensor_scalar(wq_a[:, :], W["ffn0"], small[:, 4:5], None, ALU.mult))
            link(vec.tensor_scalar(wq_b[:, :], wq_a[:, :], 0.5, None, ALU.is_gt))
            link(vec.tensor_scalar(wq_a[:, :], wq_a[:, :], -0.5, None, ALU.is_lt))
            link(vec.tensor_tensor(wq_b[:, :], wq_b[:, :], wq_a[:, :], ALU.subtract))
            link(vec.reciprocal(small[:, 5:6], small[:, 3:4]))
            link(vec.tensor_scalar(small[:, 6:7], small[:, 3:4], small[:, 0:1], 1.0 / 128.0, ALU.mult, ALU.mult))
            link(vec.tensor_scalar(small[:, 5:6], small[:, 5:6], 128.0, None, ALU.mult))
            vec.tensor_scalar(wq_c[:, :], wq_b[:, :], small[:, 6:7], None, ALU.mult).then_inc(s_ffn, 1)
            top_q = 128.0 - 1e-5
            for i in range(NSPAN):
                cs = slice(SPAN * i, SPAN * i + SPAN)
                link(vec.tensor_scalar(xn2T[:, cs], xn2T[:, cs], small[:, 5:6], top_q, ALU.mult, ALU.min))
                vec.tensor_scalar(xn2T[:, cs], xn2T[:, cs], -top_q, None, ALU.max).then_inc(s_ffn, 1)

            v.wait_ge(freeD, D1_)
            vec.memset(PS[:, 7, :], 0.0).then_inc(s_acc, 1)

            def item(k):
                kind, n, u = ITEMS[k]
                v.wait_ge(s_item, k + 1)
                ring = 3 + 2 * (k % 2)
                if kind == "max":
                    vec.tensor_reduce(pmax[:, u, :], PS[:, ring:ring + 2, :].rearrange("p a (b c) -> p (a b) c", c=P),
                                      AX.X, ALU.max).then_inc(s_item_used, 1)
                    if u == NMAX - 1:
                        v.wait_ge(s_item_used, k + 1)
                        four = pmax[:, 0:4 * GH, :].rearrange("p (h u) b -> p h u b", u=4)
                        for uu, (a, b_) in enumerate(((7, None), (6, 0), (5, 1), (4, 2))):
                            note(vec.tensor_reduce(rmax[:, :, a], four[:, :, uu, 0:a + 1], AX.X, ALU.max, negate=True))
                            if b_ is not None:
                                note(vec.tensor_reduce(rmax[:, :, b_], four[:, :, uu, a + 1:8], AX.X, ALU.max, negate=True))
                        note(vec.tensor_reduce(rmax[:, :, 3], pmax[:, 4 * GH:, :].rearrange("p u (h b) -> p (u h) b", h=2),
                                               AX.X, ALU.max, negate=True))
                        settle()
                        mp = mpart[:, :, :, :].rearrange("p i h a -> p h i a")
                        link(vec.tensor_copy(mp[:, :, :, 0], rmax[:, :, :]))
                        link(vec.tensor_tensor(rleft[:, 0], rmax[:, :, :], mp[:, :, :, 0], ALU.subtract))
                        link(vec.tensor_copy(mp[:, :, :, 1], rleft[:, 0]))
                        link(vec.tensor_tensor(rleft[:, 1], rleft[:, 0], mp[:, :, :, 1], ALU.subtract))
                        vec.tensor_copy(mp[:, :, :, 2], rleft[:, 1]).then_inc(s_mpart, 1)
                        v.wait_ge(s_mpart, n + 1)
                else:
                    if n >= 2:
                        v.wait_ge(s_mop[n % 2], 16 * GH * (n // 2))
                    src = PS[MAX_K:MAX_K + 3 * GH, ring, :].bitcast(BF16)
                    vec.tensor_copy(mrow[MAX_K:MAX_K + 3 * GH, n % 2, :], src).then_inc(s_item_used, 1)

            def acc(s):
                n, u = divmod(s, NU)
                if u in (2, 9):
                    v.wait_ge(s_pv, s + 1)
                    half = UNITS[u][0]
                    vec.tensor_copy(yacc[:, n, SPAN * half:SPAN * half + SPAN], PS[:, 7, :]).then_inc(s_acc, 1)

            for k in items_of_step(0):
                item(k)
            for s in range(NSTEP + 1):
                if 0 < s < NSTEP:
                    for k in items_of_step(s):
                        item(k)
                if s:
                    acc(s - 1)

            for i in range(NSPAN):
                if i >= 2:
                    v.wait_ge(freeA, A_at[("yT", i - 2)] + 1)
                for g in range(NG):
                    ps = wait_d(("yt", i, g)).rearrange("p (n h w) -> p n h w", n=TPS, w=STRIP)
                    link(vec.reciprocal(rden[:, g % 2], ps[:, :, :, D0]))
                    vec.tensor_tensor(y[:, i % 2, :, GH * D0 * g:GH * D0 * (g + 1)].rearrange("p n (h d) -> p n h d", d=D0),
                                      ps[:, :, :, 0:D0],
                                      rden[:, g % 2].rearrange("p n (h a) -> p n h a", a=1).broadcast_to([P, TPS, GH, D0]),
                                      ALU.mult).then_inc(freeD, 1)
                    v.wait_ge(freeD, D_at[("yt", i, g)] + 1)
                ps = wait_d(("back", i)).rearrange("p (n c) -> p n c", n=TPS)
                xs = x_sb[:, TPS * i:TPS * i + TPS, :]
                vec.tensor_tensor(xs, ps, xs, ALU.add).then_inc(freeD, 1)
            v.wait_ge(freeD, D2)
            layer_norm(x_sb, xn, 1e-5, 2)

            for i in range(NSPAN):
                ps = wait_d(("gl", i))
                vec.tensor_copy(gl_sb[:, TPS * i:TPS * i + TPS, :], ps[:, 0:TPS * GL].rearrange("p (n c) -> p n c", n=TPS)).then_inc(freeD, 1)
            v.wait_ge(freeD, len(RD))
            wide = lambda a: a.rearrange("p (n o) -> p n o", o=1).broadcast_to([P, NT, E1])
            link(vec.tensor_reduce(col[:, 0, :], gl_sb[:, :, 0:E1], AX.X, ALU.max))
            vec.tensor_tensor(ex[:, :, :], gl_sb[:, :, 0:E1], wide(col[:, 0, :]), ALU.subtract).then_inc(s_glx, 1)
            v.wait_ge(s_ex, 1)
            link(vec.tensor_reduce(col[:, 1, :], ex[:, :, :], AX.X, ALU.add))
            link(vec.reciprocal(col[:, 2, :], col[:, 1, :]))
            link(vec.memset(sc[:, :, E1:], -1.0))
            link(vec.tensor_tensor(sc[:, :, 0:E1], ex[:, :, :], wide(col[:, 2, :]), ALU.mult))
            for i in range(NT):
                note(vec.max(top[:, i, :], sc[:, i, :]))
            settle()
            link(vec.memset(top[:, :, TOPK:8], -1.0))
            for i in range(NT):
                note(vec.match_replace(kept[:, i, :], top[:, i, :], sc[:, i, :], 0.0))
            settle()
            link(vec.tensor_tensor(kept[:, :, 0:E1], sc[:, :, 0:E1], kept[:, :, 0:E1], ALU.subtract))
            vec.tensor_tensor(tw[:, :, :].rearrange("p n (e r) -> p n e r", r=R1),
                              gl_sb[:, :, E1:].rearrange("p n (e r) -> p n e r", r=R1),
                              kept[:, :, 0:E1].rearrange("p n (e o) -> p n e o", o=1).broadcast_to([P, NT, E1, R1]),
                              ALU.mult).then_inc(s_tw, 1)

            pj = [0]

            def rope(i, m, is_k):
                cosT = K["cos"][:, SPAN * (i % 2):SPAN * (i % 2) + SPAN]
                sinT = K["sin"][:, SPAN * (i % 2):SPAN * (i % 2) + SPAN]
                r = (2 + QT) * i + m
                if r >= 2:
                    v.wait_ge(s_qr, QT * ((r - 2) // (2 + QT)) + max(0, (r - 2) % (2 + QT) - 1))
                    v.wait_ge(s_kr, 2 * ((r - 2) // (2 + QT)) + min(2, (r - 2) % (2 + QT) + 1))
                for dst, tab in ((rope_a, cosT), (rope_b, sinT)):
                    k = pj[0]
                    pj[0] += 1
                    v.wait_ge(s_pj, k + 1)
                    vec.tensor_tensor(dst[:, r % 2, :], PS[:, k % 2, :], tab, ALU.mult).then_inc(s_pj_free, 1)
                v.wait_ge(s_pj_free, pj[0])

            def chunk_kv(c):
                k = pj[0]
                pj[0] += 1
                v.wait_ge(s_pj, k + 1)
                if c >= 2:
                    v.wait_ge(s_o, KV1 * (c - 1))
                    v.wait_ge(s_kv, sums(c - 1))
                    v.wait_ge(s_vd, KV1 * (c - 1))
                vec.tensor_copy(v_sb[:, c % 2, :], PS[:, k % 2, 0:256]).then_inc(s_v, 1)
                vec.tensor_copy(kt_sb[:, c % 2, :, :].rearrange("p a s -> p (a s)"), PS[:, k % 2, 256:512]).then_inc(s_pj_free, 1)
                v.wait_ge(s_pj_free, k + 1)

            def masked(c, g):
                m = KV1 * c + g
                v.wait_ge(s_sc, m + 1)
                if m >= 2:
                    v.wait_ge(s_o, m - 1)
                vec.tensor_tensor(sm[:, m % 2, :], PS[:, 2 + m % 2, :], K["decay"][:, SPAN * g:SPAN * g + SPAN], ALU.mult).then_inc(s_sm, 1)

            def advance(c):
                if c % TPB == TPB - 1:
                    return
                v.wait_ge(s_kv, sums(c + 1))
                v.wait_ge(s_faded, c + 1)
                if c == 0:
                    v.wait_ge(s_zero, 2)
                for q in range(2):
                    rows, cols = slice(64 * q, 64 * q + 64), slice(64 * q, 64 * q + 64)
                    new = PS[rows, 6:8, :].rearrange("p a (k q e) -> p (a k) q e", q=2, e=D1)[:, :, q, :]
                    dst = state[rows, (c + 1) % 2, :, cols]
                    if c % TPB == 0:
                        vec.tensor_copy(dst, new).then_inc(s_state, 1)
                    else:
                        vec.tensor_tensor(dst, new, faded[rows, :, cols], ALU.add).then_inc(s_state, 1)
                v.wait_ge(s_state, states(c + 1))

            for i in range(NSPAN):
                for m in range(2 + QT):
                    rope(i, m, m < 2)
                for ch in range(TPS):
                    c = TPS * i + ch
                    chunk_kv(c)
                    for g in range(KV1):
                        masked(c, g)
                    advance(c)
                pj[0] += 1
                k = pj[0]
                pj[0] += 1
                v.wait_ge(s_pj, k + 1)
                xs = x_sb[:, TPS * i:TPS * i + TPS, :]
                vec.tensor_tensor(xs, PS[:, k % 2, :].rearrange("p (n c) -> p n c", n=TPS), xs, ALU.add).then_inc(s_pj_free, 1)

        @block.scalar
        def _(a):
            sca = nc.scalar

            def wait_a(name):
                k = A_at[name]
                a.wait_ge(fillA, k + 1)
                return PS[:, k % 4, :]

            def root(turn):
                a.wait_ge(s_var, turn + 1)
                sca.activation(rstd[:, :], std[:, :], ACT.Sqrt).then_inc(s_std, 1)

            root(0)
            for i in range(NSPAN):
                sca.copy(xnT[:, SPAN * i:SPAN * i + SPAN], wait_a(("xnT", i))).then_inc(freeA, 1)
            root(1)
            a.wait_ge(s_load, 64)
            for i in range(NSPAN):
                sca.activation(xn2T[:, SPAN * i:SPAN * i + SPAN], wait_a(("xn2T", i)), ACT.Identity,
                               bias=W["lnb"], scale=W["lng"]).then_inc(freeA, 1)
            for s in range(NSTEP):
                u = s % NU
                if s >= P_SLOTS:
                    a.wait_ge(s_pv, s - P_SLOTS + 1)
                for h in range(GH):
                    k = GH * s + h
                    a.wait_ge(s_st, k + 1)
                    sca.activation(prob[:, s % P_SLOTS, h, 0:UNIT_W[u]], PS[:, k % ST_BANKS, 0:UNIT_W[u]],
                                   ACT.Exp).then_inc(s_exp, 1)
            for i in range(NSPAN):
                ps = wait_a(("yT", i))
                if i >= 2:
                    a.wait_ge(fillA, A_at[("proj", i - 2)] + 1)
                sca.copy(yT[:, i % 2, :], ps).then_inc(freeA, 1)
                ps = wait_a(("proj", i))
                if i >= 2:
                    a.wait_ge(fillD, D_at[("back", i - 2)] + 1)
                sca.activation(sT[:, i % 2, :], ps, ACT.Identity, bias=W["bproj"]).then_inc(freeA, 1)
            root(2)
            for i in range(NSPAN):
                sca.copy(xnT[:, SPAN * i:SPAN * i + SPAN], wait_a(("xn1T", i))).then_inc(freeA, 1)
            a.wait_ge(s_glx, 1)
            sca.activation(ex[:, :, :], ex[:, :, :], ACT.Exp).then_inc(s_ex, 1)
            for i in range(NSPAN):
                ps = wait_a(("twT", i))
                sca.copy(twT[:, SPAN * i:SPAN * i + SPAN], ps[0:E1 * R1, :]).then_inc(freeA, 1)
            for i in range(NSPAN):
                for ch in range(TPS):
                    c = TPS * i + ch
                    for r in range(2):
                        a.wait_ge(s_o, KV1 * c + 2 * r + 2)
                        if i and ch == 0 and r == 0:
                            a.wait_ge(s_pj, PJ_SPAN * i - 1)
                        sca.copy(oT[:, 4 * r:4 * r + 4, P * ch:P * ch + P],
                                 PS[:, 4 + r, :].rearrange("p (k t) -> p k t", k=4)).then_inc(s_oT, 1)
                k = PJ_SPAN * (i + 1) - 2
                a.wait_ge(s_pj, k + 1)
                if i >= 2:
                    a.wait_ge(s_pj, PJ_SPAN * (i - 1))
                sca.activation(fT[:, i % 2, :], PS[:, k % 2, :], ACT.Identity, bias=W["blin"]).then_inc(s_pj_free, 1)

        @block.gpsimd
        def _(g_):
            po = nc.gpsimd
            po.memset(q_op[:, :, :, :], 0.0).then_inc(s_clear, 1)
            po.memset(k_op[:, :, :, :], 0.0).then_inc(s_clear, 1)
            g_.wait_ge(s_gmax, 1)
            po.partition_all_reduce(small[:, 2:3], small[:, 0:1], P, RED.add).then_inc(s_gall, 1)
            po.partition_all_reduce(small[:, 3:4], small[:, 1:2], P, RED.max).then_inc(s_gall, 1)
            for s in range(NSTEP):
                at = 0
                for j, i0, nn in UNITS[s % NU][1]:
                    if i0 == j:
                        if at == 0:
                            g_.wait_ge(s_exp, GH * (s + 1))
                        blk = prob[:, s % P_SLOTS, :, at:at + P]
                        po.affine_select(out=blk, in_=blk, compare_op=ALU.is_ge, fill=0.0, base=0,
                                         pattern=[[0, GH], [1, P]], channel_multiplier=-1).then_inc(s_tri, 1)
                    at += nn
            g_.wait_ge(s_tw, 1)
            po.memset(kz[:, :, :, :, :], 0.0).then_inc(s_zero, 1)
            po.memset(state[:, :, :, :], 0.0).then_inc(s_zero, 1)

            def prepare(c):
                i, ch = divmod(c, TPS)
                kdec = K["kdec"].rearrange("p (g h o) -> p g h o", g=KV1, o=1)
                g_.wait_ge(s_v, c + 1)
                if c >= 2:
                    g_.wait_ge(s_o, KV1 * (c - 1))
                    g_.wait_ge(s_kv, sums(c - 1))
                for g in range(KV1):
                    ins = po.tensor_tensor(vdec[:, c % 2, g, :, :],
                                           v_sb[:, c % 2, D1 * g:D1 * g + D1].rearrange("p (o e) -> p o e", o=1).broadcast_to([P, H1 // KV1, D1]),
                                           kdec[:, g, :, :].broadcast_to([P, H1 // KV1, D1]), ALU.mult)
                    ins.then_inc(s_vd, 1)
                g_.wait_ge(s_vd, KV1 * (c + 1))
                po.tensor_tensor(qd[:, c % 2, :, :], qr[:, i % 2, :, P * ch:P * ch + P],
                                 K["qdec"].rearrange("p (k t) -> p k t", k=QT), ALU.mult).then_inc(s_qd, 1)
                g_.wait_ge(s_qd, c + 1)
                if c:
                    g_.wait_ge(s_state, states(c))
                else:
                    g_.wait_ge(s_zero, 2)
                po.tensor_tensor(faded[:, :, :], state[:, c % 2, :, :], K["blkdec"].rearrange("p (k t) -> p k t", k=QT),
                                 ALU.mult).then_inc(s_faded, 1)
                g_.wait_ge(s_faded, c + 1)

            for i in range(NSPAN):
                for m in range(2 + QT):
                    r = (2 + QT) * i + m
                    g_.wait_ge(s_pj_free, PJ_SPAN * i + 2 * m + 2)
                    if m == 0 and i >= 2:
                        g_.wait_ge(s_o, KV1 * TPS * (i - 1))
                        g_.wait_ge(s_kv, sums(TPS * (i - 1)))
                    if m < 2 and i >= 2:
                        g_.wait_ge(s_ks[i % 2], 16 * 8 * (i // 2))
                    if m < 2:
                        po.tensor_tensor(kr[:, i % 2, m, :], rope_a[:, r % 2, :], rope_b[:, r % 2, :], ALU.add).then_inc(s_kr, 1)
                    else:
                        po.tensor_tensor(qr[:, i % 2, m - 2, :], rope_a[:, r % 2, :], rope_b[:, r % 2, :], ALU.add).then_inc(s_qr, 1)
                g_.wait_ge(s_qr, QT * (i + 1))
                for ch in range(TPS):
                    prepare(TPS * i + ch)


def _layer_1_constants():
    import numpy as np
    inv = 1.0 / 10000.0 ** (np.arange(0, D1, 2, dtype=np.float64) / D1)
    angle = np.outer(inv, np.arange(T, dtype=np.float64))
    cos = np.tile(np.cos(angle), (4, 1))
    sin = np.sin(angle)
    sin = np.tile(np.concatenate([-sin, sin]), (2, 1))
    slope = (2.0 ** (-8.0 / H1 * np.arange(1, H1 + 1))).astype(np.float32).astype(np.float64)
    t = np.arange(P, dtype=np.float64)
    late = t[None, :] - t[:, None]
    head = np.arange(H1).reshape(KV1, 2, 2)
    order = head.transpose(0, 2, 1).reshape(-1)
    decay = np.concatenate([np.where(late >= 0, np.exp(-slope[h] * np.maximum(late, 0)), 0.0) for h in order], axis=1)
    tiles = np.arange(H1).reshape(QT, 2)
    qdec = np.concatenate([np.repeat(np.exp(-slope[tiles[k]][:, None] * (t + 1.0)), D1, axis=0) for k in range(QT)], axis=1)
    kdec = np.exp(-slope[None, :] * (P - 1.0 - t)[:, None])
    fade = np.repeat(np.exp(-slope * P).reshape(QT, 2), D1, axis=1)
    blkdec = np.broadcast_to(fade.reshape(1, -1), (P, QT * P))
    parts = {"cos": cos, "sin": sin, "decay": decay, "qdec": qdec, "kdec": kdec, "blkdec": blkdec, "ident": np.eye(P)}
    return np.concatenate([parts[n].astype(np.float32) for n in CCOLS], axis=1)


def _layer_0_constants():
    import numpy as np
    bf = lambda v: (v.astype(np.float32).view(np.uint32) >> 16).astype(np.uint16)
    t = np.arange(T)
    coarse, fine = t // 4 * 4, t % 4
    one = np.ones(T)
    k_rows = np.stack([coarse, fine, one, one, one, one, one])
    q_rows = np.stack([[s * one, s * one, -s * coarse, -s * fine] for s in 0.5 ** np.arange(1, H0 + 1)])
    row = np.arange(P)
    masks = np.stack([np.eye(P), np.where(row[None, :] > row[:, None], -1e30, 0.0)], axis=1)
    return bf(q_rows), bf(k_rows), bf(masks)


def kernel(**inputs):
    import numpy as np
    import concourse.bacc as bacc
    from concourse.bass_utils import run_bass_kernel_spmd

    a = {k: np.asarray(v) for k, v in inputs.items()}
    wq, wk, wv, wo = (a["L1_attn_" + n] for n in ("Wq", "Wk", "Wv", "Wo"))

    def turned(wt, heads):
        return wt.reshape(heads, 2, D1 // 2, C)[:, ::-1].reshape(heads * D1, C)

    col = lambda v: v.reshape(C, 1)
    parts = {
        "attn": a["L0_attn_W_attn"], "proj": a["L0_attn_W_proj"], "ffn0": a["L0_ffn_weight"],
        "q1": wq.T, "q1rot": turned(wq, H1).T, "k1": wk.T, "k1rot": turned(wk, KV1).T, "v1": wv.T,
        "wo1": wo.T.reshape(QT, P, C).transpose(1, 0, 2).reshape(P, QT * C),
        "lin1": a["L1_ffn_W_lin"].T,
        "gl1": np.concatenate([a["L1_ffn_gate_w"].T, a["L1_ffn_left"].transpose(1, 0, 2).reshape(C, E1 * R1)], axis=1),
        "bq": col(a["L0_attn_b_attn"][:C]), "bk": col(a["L0_attn_b_attn"][C:2 * C]),
        "bproj": col(a["L0_attn_b_proj"]), "lng": col(a["L0_ffn_ln_gamma"]), "lnb": col(a["L0_ffn_ln_beta"]),
        "blin": col(a["L1_ffn_b_lin"]), "bv": np.broadcast_to(a["L0_attn_b_attn"][2 * C:], (P, C)),
    }
    q_rows, k_rows, masks = _layer_0_constants()
    arrays = {
        "x_dram": np.ascontiguousarray(a["L0_attn_x"].reshape(B * T, C)),
        "w_dram": np.ascontiguousarray(np.concatenate([parts[n] for n in WCOLS], axis=1)),
        "right_dram": np.ascontiguousarray(a["L1_ffn_right"].reshape(E1 * R1, C)),
        "const_dram": _layer_1_constants(), "alibi_q_dram": q_rows, "alibi_k_dram": k_rows, "masks_dram": masks,
    }
    nc = bacc.Bacc("TRN2", target_bir_lowering=False, num_devices=1)
    args = [nc.dram_tensor(n, v.shape, mybir.dt.from_np(v.dtype), kind="ExternalInput").ap() for n, v in arrays.items()]
    args.append(nc.dram_tensor("out_dram", (B * T, C), F32, kind="ExternalOutput").ap())
    build(nc, *args)
    r = run_bass_kernel_spmd(nc, [arrays], core_ids=[0])
    return r.results[0]["out_dram"].reshape(B, T, C)
```

```python
from contextlib import ExitStack

import concourse.bass as bass
from concourse import mybir

F32 = mybir.dt.float32
BF16 = mybir.dt.bfloat16
ALU = mybir.AluOpType
ACT = mybir.ActivationFunctionType
AX = mybir.AxisListType
RED = bass.bass_isa.ReduceOp

P = 128
B, T, C = 2, 1024, 128
NT = B * T // P
TPB = T // P
SPAN = 512
NSPAN = B * T // SPAN
TPS = SPAN // P

H0, D0 = 16, 8
GH = 4
NG = H0 // GH
GROUPS = [(b, g) for b in range(B) for g in range(NG)]
ALIBI_ROWS = 4
QK_ROWS = 9 * D0
MAX_K = 96
EXP_K = MAX_K + 3
VW = 16
STRIP = 32

H1, KV1, D1 = 16, 4, 64
HPG = H1 // KV1
QT = H1 * D1 // P
NCH = B * T // P
PROJ = 2 * (2 + QT)
PPC = PROJ // TPS

E1, R1, TOPK = 8, 4, 2
GL = E1 + E1 * R1

WCOLS = {}
_at = 0
for _name, _n in [("attn", 3 * C), ("proj", C), ("ffn0", C), ("q1", H1 * D1), ("q1rot", H1 * D1),
                  ("k1", KV1 * D1), ("k1rot", KV1 * D1), ("v1", KV1 * D1), ("wo1", QT * C), ("lin1", C),
                  ("gl1", GL), ("bq", 1), ("bk", 1), ("bproj", 1), ("lng", 1), ("lnb", 1), ("blin", 1),
                  ("bv", C)]:
    WCOLS[_name] = (_at, _at + _n)
    _at += _n
NW = _at
CCOLS = {}
_at = 0
for _name, _n in [("cos", T), ("sin", T), ("decay", H1 * P), ("qdec", QT * P), ("kdec", H1),
                  ("blkdec", QT * P), ("ident", P)]:
    CCOLS[_name] = (_at, _at + _n)
    _at += _n
NC_ = _at

UNITS = [(0, [(0, 0, 512)]), (0, [(1, 1, 384), (3, 3, 128)]), (0, [(2, 2, 256)]),
         (1, [(0, 4, 512)]), (1, [(1, 4, 512)]), (1, [(2, 4, 512)]), (1, [(3, 4, 512)]),
         (1, [(4, 4, 512)]), (1, [(5, 5, 384), (7, 7, 128)]), (1, [(6, 6, 256)])]
NU = len(UNITS)
NSTEP = NU * len(GROUPS)
UNIT_W = [sum(n for _, _, n in segs) for _, segs in UNITS]
MAXU = [[(h, a, 0)] + ([(h, b_, a + 1)] if b_ is not None else [])
        for h in range(GH) for a, b_ in ((7, None), (6, 0), (5, 1), (4, 2))]
MAXU += [[(h, 3, 0), (h + 1, 3, 4)] for h in (0, 2)]
NMAX = len(MAXU)
P_SLOTS = 3
ST_BANKS = 3
OP_SLOTS = 3
LEAD = 15


def item_stream():
    out = []
    for n in range(len(GROUPS)):
        for u in range(NMAX):
            out.append(("max", n, u))
            if u == 1 and n:
                out.append(("turn", n - 1, 0))
    return out + [("turn", len(GROUPS) - 1, 0)]


ITEMS = item_stream()
_per = (NMAX + 1) / NU
TURN_AT = {n: k for k, (kind, n, _) in enumerate(ITEMS) if kind == "turn"}
TRI = []
for _s in range(NSTEP):
    TRI.append((TRI[-1] if TRI else 0) + sum(i0 == j for j, i0, _ in UNITS[_s % NU][1]))


def items_of_step(s):
    lo = 0 if s == 0 else min(len(ITEMS), int((s + LEAD) * _per))
    hi = min(len(ITEMS), int((s + 1 + LEAD) * _per)) if s < NSTEP - 1 else len(ITEMS)
    return range(lo, hi)


def build(nc, x, w, wright, consts, alibi_q, alibi_k, masks, out):
    alibi_q, alibi_k, masks = (v.bitcast(BF16) for v in (alibi_q, alibi_k, masks))
    with ExitStack() as ctx:
        def sb(name, shape, dt=F32, c=ctx):
            return c.enter_context(nc.sbuf_tensor(name, shape, dt))

        def sem(name):
            return ctx.enter_context(nc.semaphore(name))

        PS = ctx.enter_context(nc.psum_tensor("PS", [P, 8, 512], F32))

        x_sb = sb("x_sb", [P, NT, C])
        w_sb = sb("w_sb", [P, NW])
        c_sb = sb("c_sb", [P, NC_])
        right_sb = sb("right_sb", [E1 * R1, C])
        W = {n: w_sb[:, a:b] for n, (a, b) in WCOLS.items()}
        K = {n: c_sb[:, a:b] for n, (a, b) in CCOLS.items()}
        masks_sb = sb("masks_sb", [P, 2, P], BF16)
        ident_b, causal_b = masks_sb[:, 0, :], masks_sb[:, 1, :]
        xn = sb("xn", [P, NT, C])
        xnT = sb("xnT", [P, B * T])
        stats = sb("stats", [P, NT, 6])
        mv = sb("mv", [P, NT, 2])
        std = sb("std", [P, NT])
        rstd = sb("rstd", [P, NT])

        l0 = ExitStack()
        xn2T = sb("xn2T", [P, B * T], c=l0)
        split = ExitStack()
        part = sb("part", [P, 2, 3, SPAN], BF16, split)
        rest = sb("rest", [P, 3, SPAN], F32, split)
        split.close()
        yacc = sb("yacc", [P, len(GROUPS), T], F32, l0)
        mrow = sb("mrow", [P, 2, T], BF16, l0)
        sT = sb("sT", [P, 2, SPAN], F32, l0)
        y = xnT[:, :].rearrange("p (a n c) -> p a n c", n=TPS, c=C)
        yT = xn[:, 4:12, :].rearrange("p (a n) c -> p a (n c)", a=2)
        wq_a, wq_b, wq_c = xn[:, 0, :], xn[:, 1, :], xn[:, 2, :]
        vaug = sb("vaug", [P, NT, H0, VW], F32, l0)
        q_op = sb("q_op", [P, OP_SLOTS, GH, T], BF16, l0)
        k_op = sb("k_op", [P, OP_SLOTS, GH, T], BF16, l0)
        prob = sb("prob", [P, P_SLOTS, GH, SPAN], F32, l0)
        pmax = sb("pmax", [P, NMAX, TPB], F32, l0)
        rmax = sb("rmax", [P, GH, TPB], F32, l0)
        rleft = sb("rleft", [P, 2, GH, TPB], F32, l0)
        mpart = sb("mpart", [P, TPB, GH, 3], BF16, l0)
        rden = sb("rden", [P, 2, TPS, GH], F32, l0)
        small = sb("small", [P, 8], F32, l0)
        l0.close()

        l1 = ExitStack()
        gates = ExitStack()
        gl_sb = sb("gl_sb", [P, NT, GL], F32, gates)
        ex = sb("ex", [P, NT, E1], F32, gates)
        sc = sb("sc", [P, NT, 2 * E1], F32, gates)
        col = sb("col", [P, 3, NT], F32, gates)
        top = sb("top", [P, NT, 8], F32, gates)
        kept = sb("kept", [P, NT, 2 * E1], F32, gates)
        tw = sb("tw", [P, NT, E1 * R1], F32, gates)
        gates.close()
        twT = xn[0:E1 * R1, :, :].rearrange("p n c -> p (n c)")
        faded = sb("faded", [P, QT, P], F32, l1)
        rope_a = sb("rope_a", [P, 2, SPAN], F32, l1)
        rope_b = sb("rope_b", [P, 2, SPAN], F32, l1)
        qr = sb("qr", [P, 2, QT, SPAN], F32, l1)
        kr = sb("kr", [P, 2, 2, SPAN], F32, l1)
        kz = sb("kz", [P, 2, 2, 2, SPAN], F32, l1)
        vk = sb("vk", [P, 2, 2 * KV1 * D1], F32, l1)
        vdec = sb("vdec", [P, 2, KV1, HPG, D1], F32, l1)
        qd = sb("qd", [P, 2, QT, P], F32, l1)
        sm = sb("sm", [P, 4, SPAN], F32, l1)
        state = sb("state", [P, 2, QT, P], F32, l1)
        oT = sb("oT", [P, 2, QT, SPAN], F32, l1)
        fT = sb("fT", [P, SPAN], F32, l1)
        l1.close()

        q_scr = nc.dram_tensor("q_scr", [B, H0, 3 * D0, T], BF16, kind="Internal").ap()
        k_scr = nc.dram_tensor("k_scr", [B, H0, 3 * D0, T], BF16, kind="Internal").ap()

        s_load = sem("s_load")
        s_x = [sem(f"s_x{i}") for i in range(NSPAN)]
        dve = sem("dve")
        s_clear = sem("s_clear")
        s_var = sem("s_var")
        s_std = sem("s_std")
        s_xn = sem("s_xn")
        fillA, freeA = sem("fillA"), sem("freeA")
        fillD, freeD = sem("fillD"), sem("freeD")
        s_part = sem("s_part")
        s_scr = [sem(f"s_scr{i}") for i in range(2)]
        s_op = [sem(f"s_op{i}") for i in range(OP_SLOTS)]
        s_vaug = sem("s_vaug")
        s_gmax = sem("s_gmax")
        s_gall = sem("s_gall")
        s_ffn = sem("s_ffn")
        s_item, s_item_used = sem("s_item"), sem("s_item_used")
        s_mpart = sem("s_mpart")
        s_mop = [sem(f"s_mop{i}") for i in range(2)]
        s_st = sem("s_st")
        s_exp = sem("s_exp")
        s_tri = sem("s_tri")
        s_pv = sem("s_pv")
        s_acc = sem("s_acc")
        s_out = sem("s_out")
        s_glx = sem("s_glx"); s_ex = sem("s_ex"); s_tw = sem("s_tw")
        s_zero = sem("s_zero")
        s_pj, s_pj_free = sem("s_pj"), sem("s_pj_free")
        s_qr = sem("s_qr"); s_kr = sem("s_kr"); s_kz = sem("s_kz")
        s_z, s_zf = sem("s_z"), sem("s_zf")
        s_vd = sem("s_vd"); s_qd = sem("s_qd")
        s_sc, s_sm = sem("s_sc"), sem("s_sm")
        s_kv = sem("s_kv")
        s_state, s_faded = sem("s_state"), sem("s_faded")
        s_o, s_oT = sem("s_o"), sem("s_oT")

        RA, RD = [], []
        for i in range(NSPAN):
            RA.append(("xnT", i))
        for i in range(NSPAN):
            RA.append(("xn2T", i))
            RD += [("q", i), ("k", i), ("v", i)]
        A1 = len(RA)
        D1_ = len(RD)
        for i in range(NSPAN):
            RD += [("yt", i, g) for g in range(NG)] + [("back", i)]
            RA += [("yT", i), ("proj", i)]
        A2, D2 = len(RA), len(RD)
        for i in range(NSPAN):
            RA.append(("xn1T", i))
        for i in range(NSPAN):
            RD.append(("gl", i))
        for i in range(NSPAN):
            RA.append(("twT", i))
        PJ = [("p", 0, m) for m in range(PROJ)]
        Z = [("vk", 0)]
        for c in range(NCH):
            i, ch = divmod(c, TPS)
            if i + 1 < NSPAN:
                PJ += [("p", i + 1, m) for m in range(PPC * ch, PPC * ch + PPC)]
            if ch == 0 and i:
                Z.append(("out", i - 1))
            if ch == 1 and i:
                PJ.append(("back", i - 1))
            if c + 1 < NCH:
                Z.append(("vk", c + 1))
        Z.append(("out", NSPAN - 1))
        PJ.append(("back", NSPAN - 1))
        PJ_at = {n: k for k, n in enumerate(PJ)}
        Z_at = {n: k for k, n in enumerate(Z)}

        def sums(c):
            return c - c // TPB

        def later(c):
            return c - (c + TPB - 1) // TPB

        def fades(c):
            return c - (c + TPB - 1) // TPB - c // TPB

        def states(c):
            return 2 * sums(c)

        A_at = {n: i for i, n in enumerate(RA)}
        D_at = {n: i for i, n in enumerate(RD)}

        block = ctx.enter_context(nc.Block())

        @block.sync
        def _(sp):
            xt = x.rearrange("(n p) c -> p n c", p=P)
            for i in range(NSPAN):
                sp.dma_start(x_sb[:, TPS * i:TPS * i + TPS, :], xt[:, TPS * i:TPS * i + TPS, :]).then_inc(s_x[i], 16)
                if i == 0:
                    sp.dma_start(w_sb[:, :], w).then_inc(s_load, 16)
                    sp.dma_start(masks_sb[:, :, :], masks).then_inc(s_load, 16)
                    sp.dma_start(c_sb[:, :], consts).then_inc(s_load, 16)
                    sp.dma_start(right_sb[:, :], wright).then_inc(s_load, 16)

            def load_ops(n):
                b, g = GROUPS[n]
                slot = n % OP_SLOTS
                if n >= OP_SLOTS:
                    sp.wait_ge(s_st, GH * NU * (n - OP_SLOTS + 1))
                for h in range(GH):
                    hh = g * GH + h
                    sp.dma_start(q_op[ALIBI_ROWS:ALIBI_ROWS + QK_ROWS, slot, h, :],
                                 q_scr[b, hh].rearrange("(o r) t -> o r t", o=1).broadcast_to([3, 3 * D0, T])).then_inc(s_op[slot], 16)
                    for c3 in range(3):
                        r0 = ALIBI_ROWS + 3 * D0 * c3
                        sp.dma_start(k_op[r0:r0 + 3 * D0, slot, h, :],
                                     k_scr[b, hh, D0 * c3:D0 * c3 + D0].rearrange("(o d) t -> o d t", o=1)
                                     .broadcast_to([3, D0, T])).then_inc(s_op[slot], 16)
                    sp.dma_start(q_op[0:ALIBI_ROWS, slot, h, :], alibi_q[hh]).then_inc(s_op[slot], 16)

            def load_m(n):
                slot = n % OP_SLOTS
                sp.wait_ge(s_item_used, TURN_AT[n] + 1)
                for h in range(GH):
                    sp.dma_start(q_op[MAX_K:MAX_K + 3, slot, h, :],
                                 mrow[MAX_K + 3 * h:MAX_K + 3 * h + 3, n % 2, :]).then_inc(s_mop[n % 2], 16)

            for i in range(2 * NSPAN):
                sp.wait_ge(s_part, i + 1)
                scr = q_scr if i % 2 == 0 else k_scr
                b, half = divmod(i // 2, 2)
                for a in range(3):
                    sp.dma_start(scr[b, :, D0 * a:D0 * a + D0, SPAN * half:SPAN * half + SPAN],
                                 part[:, i % 2, a, :]).then_inc(s_scr[i % 2], 16)
            for i in range(2):
                sp.wait_ge(s_scr[i], 3 * 16 * NSPAN)
            sp.wait_ge(s_clear, 2)
            for slot in range(OP_SLOTS):
                for h in range(GH):
                    sp.dma_start(k_op[0:ALIBI_ROWS, slot, h, :], alibi_k[0:ALIBI_ROWS]).then_inc(s_op[slot], 16)
                    sp.dma_start(k_op[MAX_K:EXP_K, slot, h, :], alibi_k[ALIBI_ROWS:ALIBI_ROWS + 3]).then_inc(s_op[slot], 16)
            for n in range(OP_SLOTS):
                load_ops(n)
            load_m(0)
            load_m(1)
            for n in range(2, len(GROUPS)):
                if n + 1 < len(GROUPS):
                    load_ops(n + 1)
                load_m(n)

            ot = out.rearrange("(n p) c -> p n c", p=P)
            for i in range(NSPAN):
                sp.wait_ge(s_pj_free, PJ_at[("back", i)] + 1)
                sp.dma_start(ot[:, TPS * i:TPS * i + TPS, :], x_sb[:, TPS * i:TPS * i + TPS, :]).then_inc(s_out, 16)
            sp.wait_ge(s_out, 16 * NSPAN)

        OP_FIRST = 16 * GH * 2
        OP_EACH = 16 * GH * 5

        @block.tensor
        def _(pe):
            mm, tr = nc.tensor.matmul, nc.tensor.transpose

            def unit_a(name):
                k = A_at[name]
                if k >= 4:
                    pe.wait_ge(freeA, k - 3)
                return PS[:, k % 4, :]

            def unit_d(name):
                k = D_at[name]
                if k >= 4:
                    pe.wait_ge(freeD, k - 3)
                return PS[:, 4 + k % 4, :]

            pe.wait_ge(s_load, 64)
            for i in range(NSPAN):
                ps = unit_a(("xnT", i))
                pe.wait_ge(s_xn, TPS * (i + 1))
                for j in range(TPS):
                    last = tr(ps[:, P * j:P * j + P], xn[:, TPS * i + j, :], K["ident"])
                last.then_inc(fillA, 1)
            for i in range(NSPAN):
                pe.wait_ge(freeA, i + 1)
                cs = slice(SPAN * i, SPAN * i + SPAN)
                for n, name in enumerate("qk"):
                    mm(unit_d((name, i)), W["attn"][:, C * n:C * n + C], xnT[:, cs], start=True, stop=True).then_inc(fillD, 1)
                ps = unit_d(("v", i))
                for j in range(TPS):
                    last = mm(ps[:, P * j:P * j + P], xnT[:, SPAN * i + P * j:SPAN * i + P * j + P],
                              W["attn"][:, 2 * C:3 * C], start=True, stop=True)
                last.then_inc(fillD, 1)
            for i in range(NSPAN):
                ps = unit_a(("xn2T", i))
                pe.wait_ge(s_xn, NT + TPS * (i + 1))
                for j in range(TPS):
                    last = tr(ps[:, P * j:P * j + P], xn[:, TPS * i + j, :], K["ident"])
                last.then_inc(fillA, 1)

            pe.wait_ge(freeA, A1)
            pe.wait_ge(freeD, D1_)

            def item(k):
                kind, n, u = ITEMS[k]
                if k >= 2:
                    pe.wait_ge(s_item_used, k - 1)
                ring = 3 + 2 * (k % 2)
                if kind == "max":
                    slot = n % OP_SLOTS
                    if u == 0:
                        pe.wait_ge(s_op[slot], OP_FIRST + OP_EACH * (n // OP_SLOTS + 1))
                    for h, i, at in MAXU[u]:
                        j = 0
                        while j <= i:
                            c0 = at + j
                            nb = min(i + 1 - j, 4 - c0 % 4)
                            o = PS[:, ring + c0 // 4, P * (c0 % 4):P * (c0 % 4 + nb)]
                            diag = j + nb == i + 1
                            last = mm(o, q_op[0:MAX_K, slot, h, P * i:P * i + P], k_op[0:MAX_K, slot, h, P * j:P * (j + nb)],
                                      start=True, stop=not diag, skip_group_check=True)
                            if diag:
                                last = mm(o[:, P * (nb - 1):P * nb], ident_b, causal_b, start=False, stop=True,
                                          skip_group_check=True)
                            j += nb
                    last.then_inc(s_item, 1)
                else:
                    pe.wait_ge(s_mpart, n + 1)
                    o = PS[MAX_K:MAX_K + 3 * GH, ring, :].bitcast(BF16)
                    for i in range(TPB):
                        last = tr(o[:, P * i:P * i + P], mpart[:, i, :, :].rearrange("p h a -> p (h a)"), ident_b)
                    last.then_inc(s_item, 1)

            def scores(s):
                n, u = divmod(s, NU)
                slot = n % OP_SLOTS
                if u == 0:
                    pe.wait_ge(s_mop[n % 2], 16 * GH * (n // 2 + 1))
                for h in range(GH):
                    k = GH * s + h
                    if k >= ST_BANKS:
                        pe.wait_ge(s_exp, k - ST_BANKS + 1)
                    at = 0
                    for j, i0, nn in UNITS[u][1]:
                        last = mm(PS[:, k % ST_BANKS, at:at + nn], k_op[0:EXP_K, slot, h, P * j:P * j + P],
                                  q_op[0:EXP_K, slot, h, P * i0:P * i0 + nn], start=True, stop=True)
                        at += nn
                    last.then_inc(s_st, 1)

            def pv(s):
                n, u = divmod(s, NU)
                b, g = GROUPS[n]
                half, segs = UNITS[u]
                pe.wait_ge(s_exp, GH * (s + 1))
                pe.wait_ge(s_tri, TRI[s])
                if u in (0, 3):
                    pe.wait_ge(s_acc, 1 + 2 * n + (u == 3))
                at = 0
                for j, i0, nn in segs:
                    c0 = P * i0 - SPAN * half
                    for h in range(GH):
                        last = mm(PS[STRIP * h:STRIP * h + VW, 7, c0:c0 + nn], vaug[:, TPB * b + j, g * GH + h, :],
                                  prob[:, s % P_SLOTS, h, at:at + nn], start=(j == 0),
                                  stop=(u in (2, 9)), skip_group_check=True)
                    at += nn
                last.then_inc(s_pv, 1)

            for k in items_of_step(0):
                item(k)
            for s in range(NSTEP + 1):
                if s < NSTEP:
                    scores(s)
                if 0 < s < NSTEP:
                    for k in items_of_step(s):
                        item(k)
                if s:
                    pv(s - 1)

            pe.wait_ge(s_exp, GH * NSTEP)
            pe.wait_ge(s_item_used, len(ITEMS))
            pe.wait_ge(s_acc, 1 + 2 * len(GROUPS))
            pe.wait_ge(s_ffn, 1 + NSPAN)

            def turn_heads(i):
                b, half = divmod(i, 2)
                for g in range(NG):
                    ps = unit_d(("yt", i, g))
                    for j in range(TPS):
                        last = tr(ps[:, P * j:P * j + P],
                                  yacc[:, NG * b + g, SPAN * half + P * j:SPAN * half + P * j + P], K["ident"])
                    last.then_inc(fillD, 1)

            def project(i):
                ps = unit_a(("yT", i))
                pe.wait_ge(freeD, D_at[("yt", i, NG - 1)] + 1)
                for j in range(TPS):
                    last = tr(ps[:, P * j:P * j + P], y[:, i % 2, j, :], K["ident"])
                last.then_inc(fillA, 1)
                ps = unit_a(("proj", i))
                mm(ps, wq_c[:, :], xn2T[:, SPAN * i:SPAN * i + SPAN], start=True, stop=False)
                pe.wait_ge(freeA, A_at[("yT", i)] + 1)
                mm(ps, W["proj"], yT[:, i % 2, :], start=False, stop=True).then_inc(fillA, 1)

            def back(i):
                pe.wait_ge(freeA, A_at[("proj", i)] + 1)
                ps = unit_d(("back", i))
                for j in range(TPS):
                    last = tr(ps[:, P * j:P * j + P], sT[:, i % 2, P * j:P * j + P], K["ident"])
                last.then_inc(fillD, 1)

            for i in range(NSPAN):
                turn_heads(i)
                project(i)
                back(i)

            for i in range(NSPAN):
                ps = unit_a(("xn1T", i))
                pe.wait_ge(s_xn, 2 * NT + TPS * (i + 1))
                for j in range(TPS):
                    last = tr(ps[:, P * j:P * j + P], xn[:, TPS * i + j, :], K["ident"])
                last.then_inc(fillA, 1)
            for i in range(NSPAN):
                pe.wait_ge(freeA, A_at[("xn1T", i)] + 1)
                ps = unit_d(("gl", i))
                for j in range(TPS):
                    last = mm(ps[:, GL * j:GL * j + GL], xnT[:, SPAN * i + P * j:SPAN * i + P * j + P], W["gl1"],
                              start=True, stop=True)
                last.then_inc(fillD, 1)
            for i in range(NSPAN):
                ps = unit_a(("twT", i))
                pe.wait_ge(s_tw, 1)
                for j in range(TPS):
                    last = tr(ps[0:E1 * R1, P * j:P * j + P], tw[:, TPS * i + j, :], K["ident"])
                last.then_inc(fillA, 1)

            pe.wait_ge(freeA, len(RA))
            pe.wait_ge(freeD, len(RD))

            pe.wait_ge(s_zero, 2)

            def bank01(name):
                k = PJ_at[name]
                if k >= 2:
                    pe.wait_ge(s_pj_free, k - 1)
                return PS[:, k % 2, :]

            def bank7(name):
                k = Z_at[name]
                if k:
                    pe.wait_ge(s_zf, k)
                return PS[:, 7, :]

            def project1(i, ms):
                if i == NSPAN:
                    return
                for m in ms:
                    tile, twin = divmod(m, 2)
                    w = W["k1rot" if twin else "k1"][:, P * tile:P * tile + P] if tile < 2 else \
                        W["q1rot" if twin else "q1"][:, P * (tile - 2):P * (tile - 2) + P]
                    mm(bank01(("p", i, m)), w, xnT[:, SPAN * i:SPAN * i + SPAN], start=True, stop=True).then_inc(s_pj, 1)

            def chunk_vk(c):
                if c == NCH:
                    return
                i, ch = divmod(c, TPS)
                ps = bank7(("vk", c))
                mm(ps[:, 0:KV1 * D1], xnT[:, P * c:P * c + P], W["v1"], start=True, stop=True)
                pe.wait_ge(s_kr, 2 * (i + 1))
                for pr in range(2):
                    last = tr(ps[:, KV1 * D1 + P * pr:KV1 * D1 + P * pr + P], kr[:, i % 2, pr, P * ch:P * ch + P], K["ident"])
                last.then_inc(s_z, 1)

            def score(c, g):
                i, ch = divmod(c, TPS)
                m = KV1 * c + g
                if m >= 2:
                    pe.wait_ge(s_sm, m - 1)
                mm(PS[:, 2 + m % 2, :].rearrange("p (a t) -> p a t", a=HPG), kz[:, i % 2, g // 2, g % 2, P * ch:P * ch + P],
                   qr[:, i % 2, HPG * (g // 2):HPG * (g // 2) + HPG, P * ch:P * ch + P], start=True, stop=True).then_inc(s_sc, 1)

            def mix(c, pr):
                first = c % TPB == 0
                if c:
                    pe.wait_ge(s_oT, 2 * c + pr - 1)
                pe.wait_ge(s_zf, Z_at[("vk", c)] + 1)
                for q in range(2):
                    g = 2 * pr + q
                    m = KV1 * c + g
                    pe.wait_ge(s_sm, m + 1)
                    last = mm(PS[D1 * q:D1 * q + D1, 4 + pr, :], vk[:, c % 2, D1 * g:D1 * g + D1], sm[:, m % 4, :],
                              start=True, stop=first, skip_group_check=True)
                if not first:
                    pe.wait_ge(s_qd, later(c + 1))
                    pe.wait_ge(s_state, states(c))
                    for a in range(HPG):
                        last = mm(PS[:, 4 + pr, P * a:P * a + P], state[:, c % 2, HPG * pr + a, :],
                                  qd[:, c % 2, HPG * pr + a, :], start=False, stop=True, skip_group_check=True)
                last.then_inc(s_o, 1)

            def kv_sums(c):
                if c % TPB == TPB - 1:
                    return
                pe.wait_ge(s_vd, KV1 * (sums(c) + 1))
                if c:
                    pe.wait_ge(s_state, states(c))
                for g in range(KV1):
                    pr, q = divmod(g, 2)
                    last = mm(PS[D1 * q:D1 * q + D1, 6, 256 * pr:256 * pr + 256],
                              vk[:, c % 2, KV1 * D1 + D1 * g:KV1 * D1 + D1 * g + D1],
                              vdec[:, c % 2, g, :, :].rearrange("p h e -> p (h e)"), start=True, stop=True,
                              skip_group_check=True)
                last.then_inc(s_kv, 1)

            def span_out(i):
                ps = bank7(("out", i))
                cs = slice(SPAN * i, SPAN * i + SPAN)
                mm(ps, W["lin1"], xnT[:, cs], start=True, stop=False)
                mm(ps, right_sb[:, :], twT[:, cs], start=False, stop=False)
                pe.wait_ge(s_oT, 2 * TPS * (i + 1))
                for kt in range(QT):
                    last = mm(ps, W["wo1"][:, C * kt:C * kt + C], oT[:, i % 2, kt, :], start=False, stop=(kt == QT - 1))
                last.then_inc(s_z, 1)

            def span_back(i):
                ps = bank01(("back", i))
                pe.wait_ge(s_zf, Z_at[("out", i)] + 1)
                for j in range(TPS):
                    last = tr(ps[:, P * j:P * j + P], fT[:, P * j:P * j + P], K["ident"])
                last.then_inc(s_pj, 1)

            project1(0, range(PROJ))
            chunk_vk(0)
            for c in range(NCH):
                i, ch = divmod(c, TPS)
                f = PPC * ch
                if ch == 0:
                    pe.wait_ge(s_kz, 4 * (i + 1))
                    pe.wait_ge(s_qr, QT * (i + 1))
                score(c, 0)
                score(c, 1)
                if ch == 0 and i:
                    span_out(i - 1)
                project1(i + 1, (f, f + 1))
                score(c, 2)
                mix(c, 0)
                score(c, 3)
                project1(i + 1, (f + 2,))
                mix(c, 1)
                kv_sums(c)
                project1(i + 1, (f + 3, f + 4))
                if ch == 1 and i:
                    span_back(i - 1)
                chunk_vk(c + 1)
            span_out(NSPAN - 1)
            span_back(NSPAN - 1)

        @block.vector
        def _(v):
            n_dve = [0]
            vec = nc.vector

            def link(ins):
                n_dve[0] += 1
                ins.then_inc(dve, 1)
                v.wait_ge(dve, n_dve[0])

            def note(ins):
                n_dve[0] += 1
                return ins.then_inc(dve, 1)

            def settle():
                v.wait_ge(dve, n_dve[0])

            def layer_norm(src, dst, eps, turn):
                for i in range(NT):
                    if turn == 0 and i % TPS == 0:
                        v.wait_ge(s_x[i // TPS], 16)
                    note(vec.bn_stats(out=stats[:, i, :], in_=src[:, i, :]))
                settle()
                for i in range(NT):
                    note(vec.bn_aggr(out=mv[:, i, :], in_=stats[:, i, :]))
                settle()
                n_dve[0] += 1
                vec.tensor_scalar(std[:, :], mv[:, :, 1], eps, None, ALU.add).then_inc(s_var, 1)
                n_dve[0] -= 1
                v.wait_ge(s_std, turn + 1)
                link(vec.reciprocal(rstd[:, :], rstd[:, :]))
                for i in range(NT):
                    vec.tensor_scalar(dst[:, i, :], src[:, i, :], mv[:, i, 0:1], rstd[:, i:i + 1],
                                      ALU.subtract, ALU.mult).then_inc(s_xn, 1)
                v.wait_ge(s_xn, NT * (turn + 1))

            def wait_d(name):
                k = D_at[name]
                v.wait_ge(fillD, k + 1)
                return PS[:, 4 + k % 4, :]

            link(vec.memset(vaug[:, :, :, :], 0.0))
            vec.memset(vaug[:, :, :, D0:D0 + 1], 1.0).then_inc(s_vaug, 1)
            layer_norm(x_sb, xn, 1e-5, 0)
            v.wait_ge(s_load, 64)
            v.wait_ge(s_vaug, 1)
            for i in range(NSPAN):
                for n, name in enumerate("qk"):
                    k = 2 * i + n
                    ps = wait_d((name, i))
                    if n == 0:
                        ins = vec.tensor_scalar(rest[:, 0, :], ps, W["bq"], float(D0) ** -0.5, ALU.add, ALU.mult)
                    else:
                        ins = vec.tensor_scalar(rest[:, 0, :], ps, W["bk"], None, ALU.add)
                    ins.then_inc(freeD, 1)
                    v.wait_ge(freeD, D_at[(name, i)] + 1)
                    if k >= 2:
                        v.wait_ge(s_scr[n], 3 * 16 * i)
                    link(vec.tensor_copy(part[:, n, 0, :], rest[:, 0, :]))
                    link(vec.tensor_tensor(rest[:, 1, :], rest[:, 0, :], part[:, n, 0, :], ALU.subtract))
                    link(vec.tensor_copy(part[:, n, 1, :], rest[:, 1, :]))
                    link(vec.tensor_tensor(rest[:, 2, :], rest[:, 1, :], part[:, n, 1, :], ALU.subtract))
                    vec.tensor_copy(part[:, n, 2, :], rest[:, 2, :]).then_inc(s_part, 1)
                    v.wait_ge(s_part, k + 1)
                ps = wait_d(("v", i))
                ins = vec.tensor_tensor(vaug[:, TPS * i:TPS * i + TPS, :, 0:D0],
                                        ps.rearrange("p (n h d) -> p n h d", n=TPS, d=D0),
                                        W["bv"].rearrange("p (a h d) -> p a h d", a=1, d=D0).broadcast_to([P, TPS, H0, D0]), ALU.add)
                ins.then_inc(freeD, 1)
                v.wait_ge(freeD, D_at[("v", i)] + 1)
            v.wait_ge(fillA, NSPAN)
            layer_norm(xn, xn, 1e-3, 1)
            link(vec.tensor_reduce(small[:, 0:1], W["ffn0"], AX.X, ALU.add, apply_absolute_value=True))
            v.wait_ge(freeA, A1)
            vec.tensor_reduce(small[:, 1:2], xn2T[:, :], AX.X, ALU.max, apply_absolute_value=True).then_inc(s_gmax, 1)
            v.wait_ge(s_gall, 2)
            link(vec.tensor_scalar(small[:, 0:1], small[:, 2:3], 1.0 / (C * C), None, ALU.mult))
            link(vec.tensor_scalar(small[:, 4:5], small[:, 0:1], 1e-5, None, ALU.add))
            link(vec.reciprocal(small[:, 4:5], small[:, 4:5]))
            link(vec.tensor_scalar(wq_a[:, :], W["ffn0"], small[:, 4:5], None, ALU.mult))
            link(vec.tensor_scalar(wq_b[:, :], wq_a[:, :], 0.5, None, ALU.is_gt))
            link(vec.tensor_scalar(wq_a[:, :], wq_a[:, :], -0.5, None, ALU.is_lt))
            link(vec.tensor_tensor(wq_b[:, :], wq_b[:, :], wq_a[:, :], ALU.subtract))
            link(vec.reciprocal(small[:, 5:6], small[:, 3:4]))
            link(vec.tensor_scalar(small[:, 6:7], small[:, 3:4], small[:, 0:1], 1.0 / 128.0, ALU.mult, ALU.mult))
            link(vec.tensor_scalar(small[:, 5:6], small[:, 5:6], 128.0, None, ALU.mult))
            vec.tensor_scalar(wq_c[:, :], wq_b[:, :], small[:, 6:7], None, ALU.mult).then_inc(s_ffn, 1)
            top_q = 128.0 - 1e-5
            for i in range(NSPAN):
                cs = slice(SPAN * i, SPAN * i + SPAN)
                link(vec.tensor_scalar(xn2T[:, cs], xn2T[:, cs], small[:, 5:6], top_q, ALU.mult, ALU.min))
                vec.tensor_scalar(xn2T[:, cs], xn2T[:, cs], -top_q, None, ALU.max).then_inc(s_ffn, 1)

            v.wait_ge(freeD, D1_)
            vec.memset(PS[:, 7, :], 0.0).then_inc(s_acc, 1)

            def item(k):
                kind, n, u = ITEMS[k]
                v.wait_ge(s_item, k + 1)
                ring = 3 + 2 * (k % 2)
                if kind == "max":
                    vec.tensor_reduce(pmax[:, u, :], PS[:, ring:ring + 2, :].rearrange("p a (b c) -> p (a b) c", c=P),
                                      AX.X, ALU.max).then_inc(s_item_used, 1)
                    if u == NMAX - 1:
                        v.wait_ge(s_item_used, k + 1)
                        four = pmax[:, 0:4 * GH, :].rearrange("p (h u) b -> p h u b", u=4)
                        for uu, (a, b_) in enumerate(((7, None), (6, 0), (5, 1), (4, 2))):
                            note(vec.tensor_reduce(rmax[:, :, a], four[:, :, uu, 0:a + 1], AX.X, ALU.max, negate=True))
                            if b_ is not None:
                                note(vec.tensor_reduce(rmax[:, :, b_], four[:, :, uu, a + 1:8], AX.X, ALU.max, negate=True))
                        note(vec.tensor_reduce(rmax[:, :, 3], pmax[:, 4 * GH:, :].rearrange("p u (h b) -> p (u h) b", h=2),
                                               AX.X, ALU.max, negate=True))
                        settle()
                        mp = mpart[:, :, :, :].rearrange("p i h a -> p h i a")
                        link(vec.tensor_copy(mp[:, :, :, 0], rmax[:, :, :]))
                        link(vec.tensor_tensor(rleft[:, 0], rmax[:, :, :], mp[:, :, :, 0], ALU.subtract))
                        link(vec.tensor_copy(mp[:, :, :, 1], rleft[:, 0]))
                        link(vec.tensor_tensor(rleft[:, 1], rleft[:, 0], mp[:, :, :, 1], ALU.subtract))
                        vec.tensor_copy(mp[:, :, :, 2], rleft[:, 1]).then_inc(s_mpart, 1)
                        v.wait_ge(s_mpart, n + 1)
                else:
                    if n >= 2:
                        v.wait_ge(s_mop[n % 2], 16 * GH * (n // 2))
                    src = PS[MAX_K:MAX_K + 3 * GH, ring, :].bitcast(BF16)
                    vec.tensor_copy(mrow[MAX_K:MAX_K + 3 * GH, n % 2, :], src).then_inc(s_item_used, 1)

            def acc(s):
                n, u = divmod(s, NU)
                if u in (2, 9):
                    v.wait_ge(s_pv, s + 1)
                    half = UNITS[u][0]
                    vec.tensor_copy(yacc[:, n, SPAN * half:SPAN * half + SPAN], PS[:, 7, :]).then_inc(s_acc, 1)

            for k in items_of_step(0):
                item(k)
            for s in range(NSTEP + 1):
                if 0 < s < NSTEP:
                    for k in items_of_step(s):
                        item(k)
                if s:
                    acc(s - 1)

            for i in range(NSPAN):
                if i >= 2:
                    v.wait_ge(freeA, A_at[("yT", i - 2)] + 1)
                for g in range(NG):
                    ps = wait_d(("yt", i, g)).rearrange("p (n h w) -> p n h w", n=TPS, w=STRIP)
                    link(vec.reciprocal(rden[:, g % 2], ps[:, :, :, D0]))
                    vec.tensor_tensor(y[:, i % 2, :, GH * D0 * g:GH * D0 * (g + 1)].rearrange("p n (h d) -> p n h d", d=D0),
                                      ps[:, :, :, 0:D0],
                                      rden[:, g % 2].rearrange("p n (h a) -> p n h a", a=1).broadcast_to([P, TPS, GH, D0]),
                                      ALU.mult).then_inc(freeD, 1)
                    v.wait_ge(freeD, D_at[("yt", i, g)] + 1)
                ps = wait_d(("back", i)).rearrange("p (n c) -> p n c", n=TPS)
                xs = x_sb[:, TPS * i:TPS * i + TPS, :]
                vec.tensor_tensor(xs, ps, xs, ALU.add).then_inc(freeD, 1)
            v.wait_ge(freeD, D2)
            layer_norm(x_sb, xn, 1e-5, 2)

            for i in range(NSPAN):
                ps = wait_d(("gl", i))
                vec.tensor_copy(gl_sb[:, TPS * i:TPS * i + TPS, :], ps[:, 0:TPS * GL].rearrange("p (n c) -> p n c", n=TPS)).then_inc(freeD, 1)
            v.wait_ge(freeD, len(RD))
            wide = lambda a: a.rearrange("p (n o) -> p n o", o=1).broadcast_to([P, NT, E1])
            link(vec.tensor_reduce(col[:, 0, :], gl_sb[:, :, 0:E1], AX.X, ALU.max))
            vec.tensor_tensor(ex[:, :, :], gl_sb[:, :, 0:E1], wide(col[:, 0, :]), ALU.subtract).then_inc(s_glx, 1)
            v.wait_ge(s_ex, 1)
            link(vec.tensor_reduce(col[:, 1, :], ex[:, :, :], AX.X, ALU.add))
            link(vec.reciprocal(col[:, 2, :], col[:, 1, :]))
            link(vec.memset(sc[:, :, E1:], -1.0))
            link(vec.tensor_tensor(sc[:, :, 0:E1], ex[:, :, :], wide(col[:, 2, :]), ALU.mult))
            for i in range(NT):
                note(vec.max(top[:, i, :], sc[:, i, :]))
            settle()
            link(vec.memset(top[:, :, TOPK:8], -1.0))
            for i in range(NT):
                note(vec.match_replace(kept[:, i, :], top[:, i, :], sc[:, i, :], 0.0))
            settle()
            link(vec.tensor_tensor(kept[:, :, 0:E1], sc[:, :, 0:E1], kept[:, :, 0:E1], ALU.subtract))
            vec.tensor_tensor(tw[:, :, :].rearrange("p n (e r) -> p n e r", r=R1),
                              gl_sb[:, :, E1:].rearrange("p n (e r) -> p n e r", r=R1),
                              kept[:, :, 0:E1].rearrange("p n (e o) -> p n e o", o=1).broadcast_to([P, NT, E1, R1]),
                              ALU.mult).then_inc(s_tw, 1)

            def rope(i, ms):
                if i == NSPAN:
                    return
                for m in ms:
                    r, twin = divmod(m, 2)
                    n = (2 + QT) * i + r
                    k = PJ_at[("p", i, m)]
                    if n >= 2 and not twin:
                        i0, r0 = divmod(n - 2, 2 + QT)
                        v.wait_ge(s_kr, 2 * i0 + min(r0 + 1, 2))
                        if QT * i0 + max(r0 - 1, 0):
                            v.wait_ge(s_qr, QT * i0 + max(r0 - 1, 0))
                    v.wait_ge(s_pj, k + 1)
                    tab = K["sin" if twin else "cos"][:, SPAN * (i % 2):SPAN * (i % 2) + SPAN]
                    vec.tensor_tensor((rope_b if twin else rope_a)[:, n % 2, :], PS[:, k % 2, :], tab,
                                      ALU.mult).then_inc(s_pj_free, 1)

            def masked(c, g):
                m = KV1 * c + g
                v.wait_ge(s_sc, m + 1)
                if m >= 4:
                    v.wait_ge(s_o, (m - 4) // 2 + 1)
                vec.tensor_tensor(sm[:, m % 4, :], PS[:, 2 + m % 2, :], K["decay"][:, SPAN * g:SPAN * g + SPAN], ALU.mult).then_inc(s_sm, 1)

            def advance(c):
                if c % TPB == TPB - 1:
                    return
                v.wait_ge(s_kv, sums(c + 1))
                v.wait_ge(s_o, 2 * (c + 1))
                if c % TPB:
                    v.wait_ge(s_faded, fades(c + 1))
                elif c == 0:
                    v.wait_ge(s_zero, 2)
                for q in range(2):
                    rows = slice(D1 * q, D1 * q + D1)
                    new = PS[rows, 6, :].rearrange("p (k e) -> p k e", e=D1)
                    dst = state[rows, (c + 1) % 2, :, rows]
                    if c % TPB == 0:
                        vec.tensor_copy(dst, new).then_inc(s_state, 1)
                    else:
                        vec.tensor_tensor(dst, new, faded[rows, :, rows], ALU.add).then_inc(s_state, 1)

            def span_back(i):
                k = PJ_at[("back", i)]
                v.wait_ge(s_pj, k + 1)
                xs = x_sb[:, TPS * i:TPS * i + TPS, :]
                vec.tensor_tensor(xs, PS[:, k % 2, :].rearrange("p (n c) -> p n c", n=TPS), xs, ALU.add).then_inc(s_pj_free, 1)

            rope(0, range(PROJ))
            for c in range(NCH):
                i, ch = divmod(c, TPS)
                f = PPC * ch
                masked(c, 0)
                masked(c, 1)
                rope(i + 1, (f, f + 1))
                masked(c, 2)
                masked(c, 3)
                rope(i + 1, (f + 2,))
                advance(c)
                rope(i + 1, (f + 3, f + 4))
                if ch == 1 and i:
                    span_back(i - 1)
            span_back(NSPAN - 1)

        @block.scalar
        def _(a):
            sca = nc.scalar

            def wait_a(name):
                k = A_at[name]
                a.wait_ge(fillA, k + 1)
                return PS[:, k % 4, :]

            def root(turn):
                a.wait_ge(s_var, turn + 1)
                sca.activation(rstd[:, :], std[:, :], ACT.Sqrt).then_inc(s_std, 1)

            root(0)
            for i in range(NSPAN):
                sca.copy(xnT[:, SPAN * i:SPAN * i + SPAN], wait_a(("xnT", i))).then_inc(freeA, 1)
            root(1)
            a.wait_ge(s_load, 64)
            for i in range(NSPAN):
                sca.activation(xn2T[:, SPAN * i:SPAN * i + SPAN], wait_a(("xn2T", i)), ACT.Identity,
                               bias=W["lnb"], scale=W["lng"]).then_inc(freeA, 1)
            for s in range(NSTEP):
                u = s % NU
                if s >= P_SLOTS:
                    a.wait_ge(s_pv, s - P_SLOTS + 1)
                for h in range(GH):
                    k = GH * s + h
                    a.wait_ge(s_st, k + 1)
                    sca.activation(prob[:, s % P_SLOTS, h, 0:UNIT_W[u]], PS[:, k % ST_BANKS, 0:UNIT_W[u]],
                                   ACT.Exp).then_inc(s_exp, 1)
            for i in range(NSPAN):
                ps = wait_a(("yT", i))
                if i >= 2:
                    a.wait_ge(fillA, A_at[("proj", i - 2)] + 1)
                sca.copy(yT[:, i % 2, :], ps).then_inc(freeA, 1)
                ps = wait_a(("proj", i))
                if i >= 2:
                    a.wait_ge(fillD, D_at[("back", i - 2)] + 1)
                sca.activation(sT[:, i % 2, :], ps, ACT.Identity, bias=W["bproj"]).then_inc(freeA, 1)
            root(2)
            for i in range(NSPAN):
                sca.copy(xnT[:, SPAN * i:SPAN * i + SPAN], wait_a(("xn1T", i))).then_inc(freeA, 1)
            a.wait_ge(s_glx, 1)
            sca.activation(ex[:, :, :], ex[:, :, :], ACT.Exp).then_inc(s_ex, 1)
            for i in range(NSPAN):
                ps = wait_a(("twT", i))
                sca.copy(twT[:, SPAN * i:SPAN * i + SPAN], ps[0:E1 * R1, :]).then_inc(freeA, 1)
            def pad_k(i):
                if i == NSPAN:
                    return
                for pr in range(2):
                    a.wait_ge(s_kr, 2 * i + pr + 1)
                    if i == 0:
                        a.wait_ge(s_zero, 2)
                    for q in range(2):
                        rows = slice(D1 * q, D1 * q + D1)
                        sca.copy(kz[rows, i % 2, pr, q, :], kr[rows, i % 2, pr, :]).then_inc(s_kz, 1)

            def chunk_vk(c):
                if c == NCH:
                    return
                k = Z_at[("vk", c)]
                a.wait_ge(s_z, k + 1)
                if c >= 2:
                    a.wait_ge(s_vd, KV1 * sums(c - 1))
                    a.wait_ge(s_kv, sums(c - 1))
                    a.wait_ge(s_o, 2 * (c - 1))
                sca.copy(vk[:, c % 2, :], PS[:, 7, :]).then_inc(s_zf, 1)

            def span_out(i):
                k = Z_at[("out", i)]
                a.wait_ge(s_z, k + 1)
                if i:
                    a.wait_ge(s_pj, PJ_at[("back", i - 1)] + 1)
                sca.activation(fT[:, :], PS[:, 7, :], ACT.Identity, bias=W["blin"]).then_inc(s_zf, 1)

            pad_k(0)
            chunk_vk(0)
            for c in range(NCH):
                i, ch = divmod(c, TPS)
                if ch == 0 and i:
                    span_out(i - 1)
                for pr in range(2):
                    a.wait_ge(s_o, 2 * c + pr + 1)
                    if i >= 2 and ch == 0 and pr == 0:
                        a.wait_ge(s_z, Z_at[("out", i - 2)] + 1)
                    sca.copy(oT[:, i % 2, HPG * pr:HPG * pr + HPG, P * ch:P * ch + P],
                             PS[:, 4 + pr, :].rearrange("p (k t) -> p k t", k=HPG)).then_inc(s_oT, 1)
                chunk_vk(c + 1)
                if ch == 0:
                    pad_k(i + 1)
            span_out(NSPAN - 1)

        @block.gpsimd
        def _(g_):
            po = nc.gpsimd
            po.memset(q_op[:, :, :, :], 0.0).then_inc(s_clear, 1)
            po.memset(k_op[:, :, :, :], 0.0).then_inc(s_clear, 1)
            g_.wait_ge(s_gmax, 1)
            po.partition_all_reduce(small[:, 2:3], small[:, 0:1], P, RED.add).then_inc(s_gall, 1)
            po.partition_all_reduce(small[:, 3:4], small[:, 1:2], P, RED.max).then_inc(s_gall, 1)
            for s in range(NSTEP):
                at = 0
                for j, i0, nn in UNITS[s % NU][1]:
                    if i0 == j:
                        if at == 0:
                            g_.wait_ge(s_exp, GH * (s + 1))
                        blk = prob[:, s % P_SLOTS, :, at:at + P]
                        po.affine_select(out=blk, in_=blk, compare_op=ALU.is_ge, fill=0.0, base=0,
                                         pattern=[[0, GH], [1, P]], channel_multiplier=-1).then_inc(s_tri, 1)
                    at += nn
            g_.wait_ge(s_tw, 1)
            po.memset(kz[:, :, :, :, :], 0.0).then_inc(s_zero, 1)
            po.memset(state[:, :, :, :], 0.0).then_inc(s_zero, 1)

            def turn(i, ms):
                if i == NSPAN:
                    return
                for m in ms:
                    if m % 2 == 0:
                        continue
                    r = m // 2
                    n = (2 + QT) * i + r
                    g_.wait_ge(s_pj_free, PJ_at[("p", i, m)] + 1)
                    if i >= 2 and m == 1:
                        g_.wait_ge(s_o, 2 * TPS * (i - 1))
                        g_.wait_ge(s_z, Z_at[("vk", TPS * (i - 1) - 1)] + 1)
                        g_.wait_ge(s_kz, 4 * (i - 1))
                    if r < 2:
                        po.tensor_tensor(kr[:, i % 2, r, :], rope_a[:, n % 2, :], rope_b[:, n % 2, :], ALU.add).then_inc(s_kr, 1)
                    else:
                        po.tensor_tensor(qr[:, i % 2, r - 2, :], rope_a[:, n % 2, :], rope_b[:, n % 2, :], ALU.add).then_inc(s_qr, 1)

            def fade_q(c):
                if c % TPB == 0:
                    return
                i, ch = divmod(c, TPS)
                g_.wait_ge(s_qr, QT * (i + 1))
                if c >= 2:
                    g_.wait_ge(s_o, 2 * (c - 1))
                po.tensor_tensor(qd[:, c % 2, :, :], qr[:, i % 2, :, P * ch:P * ch + P],
                                 K["qdec"].rearrange("p (k t) -> p k t", k=QT), ALU.mult).then_inc(s_qd, 1)

            def fade_v(c):
                if c % TPB == TPB - 1:
                    return
                kdec = K["kdec"].rearrange("p (g h o) -> p g h o", g=KV1, o=1)
                g_.wait_ge(s_zf, Z_at[("vk", c)] + 1)
                if c >= 2:
                    g_.wait_ge(s_kv, sums(c - 1))
                for g in range(KV1):
                    po.tensor_tensor(vdec[:, c % 2, g, :, :],
                                     vk[:, c % 2, D1 * g:D1 * g + D1].rearrange("p (o e) -> p o e", o=1).broadcast_to([P, HPG, D1]),
                                     kdec[:, g, :, :].broadcast_to([P, HPG, D1]), ALU.mult).then_inc(s_vd, 1)

            def fade_state(c):
                if c % TPB in (0, TPB - 1):
                    return
                g_.wait_ge(s_state, states(c))
                po.tensor_tensor(faded[:, :, :], state[:, c % 2, :, :], K["blkdec"].rearrange("p (k t) -> p k t", k=QT),
                                 ALU.mult).then_inc(s_faded, 1)

            turn(0, range(PROJ))
            fade_v(0)
            for c in range(NCH):
                i, ch = divmod(c, TPS)
                turn(i + 1, range(PPC * ch, PPC * ch + PPC))
                if c + 1 < NCH:
                    fade_q(c + 1)
                    fade_v(c + 1)
                    fade_state(c + 1)


def _tile_heads():
    import numpy as np
    return np.arange(H1).reshape(KV1 // 2, 2, HPG).transpose(0, 2, 1).reshape(QT, 2)


def _layer_1_constants():
    import numpy as np
    inv = 1.0 / 10000.0 ** (np.arange(0, D1, 2, dtype=np.float64) / D1)
    angle = np.outer(inv, np.arange(T, dtype=np.float64))
    cos = np.tile(np.cos(angle), (4, 1))
    sin = np.sin(angle)
    sin = np.tile(np.concatenate([-sin, sin]), (2, 1))
    slope = (2.0 ** (-8.0 / H1 * np.arange(1, H1 + 1))).astype(np.float32).astype(np.float64)
    t = np.arange(P, dtype=np.float64)
    late = t[None, :] - t[:, None]
    decay = np.concatenate([np.where(late >= 0, np.exp(-slope[h] * np.maximum(late, 0)), 0.0) for h in range(H1)], axis=1)
    tiles = _tile_heads()
    qdec = np.concatenate([np.repeat(np.exp(-slope[tiles[k]][:, None] * (t + 1.0)), D1, axis=0) for k in range(QT)], axis=1)
    kdec = np.exp(-slope[None, :] * (P - 1.0 - t)[:, None])
    fade = np.repeat(np.exp(-slope * P)[tiles], D1, axis=1)
    blkdec = np.broadcast_to(fade.reshape(1, -1), (P, QT * P))
    parts = {"cos": cos, "sin": sin, "decay": decay, "qdec": qdec, "kdec": kdec, "blkdec": blkdec, "ident": np.eye(P)}
    return np.concatenate([parts[n].astype(np.float32) for n in CCOLS], axis=1)


def _layer_0_constants():
    import numpy as np
    bf = lambda v: (v.astype(np.float32).view(np.uint32) >> 16).astype(np.uint16)
    t = np.arange(T)
    coarse, fine = t // 4 * 4, t % 4
    one = np.ones(T)
    k_rows = np.stack([coarse, fine, one, one, one, one, one])
    q_rows = np.stack([[s * one, s * one, -s * coarse, -s * fine] for s in 0.5 ** np.arange(1, H0 + 1)])
    row = np.arange(P)
    masks = np.stack([np.eye(P), np.where(row[None, :] > row[:, None], -1e30, 0.0)], axis=1)
    return bf(q_rows), bf(k_rows), bf(masks)


def kernel(**inputs):
    import numpy as np
    import concourse.bacc as bacc
    from concourse.bass_utils import run_bass_kernel_spmd

    a = {k: np.asarray(v) for k, v in inputs.items()}
    wq, wk, wv, wo = (a["L1_attn_" + n] for n in ("Wq", "Wk", "Wv", "Wo"))

    def turned(wt, heads):
        return wt.reshape(heads, 2, D1 // 2, C)[:, ::-1].reshape(heads * D1, C)

    heads = _tile_heads().reshape(-1)
    by_tile = lambda wt: wt.reshape(H1, D1, -1)[heads].reshape(H1 * D1, -1)
    col = lambda v: v.reshape(C, 1)
    parts = {
        "attn": a["L0_attn_W_attn"], "proj": a["L0_attn_W_proj"], "ffn0": a["L0_ffn_weight"],
        "q1": by_tile(wq).T, "q1rot": by_tile(turned(wq, H1)).T, "k1": wk.T, "k1rot": turned(wk, KV1).T, "v1": wv.T,
        "wo1": by_tile(wo.T).reshape(QT, P, C).transpose(1, 0, 2).reshape(P, QT * C),
        "lin1": a["L1_ffn_W_lin"].T,
        "gl1": np.concatenate([a["L1_ffn_gate_w"].T, a["L1_ffn_left"].transpose(1, 0, 2).reshape(C, E1 * R1)], axis=1),
        "bq": col(a["L0_attn_b_attn"][:C]), "bk": col(a["L0_attn_b_attn"][C:2 * C]),
        "bproj": col(a["L0_attn_b_proj"]), "lng": col(a["L0_ffn_ln_gamma"]), "lnb": col(a["L0_ffn_ln_beta"]),
        "blin": col(a["L1_ffn_b_lin"]), "bv": np.broadcast_to(a["L0_attn_b_attn"][2 * C:], (P, C)),
    }
    q_rows, k_rows, masks = _layer_0_constants()
    arrays = {
        "x_dram": np.ascontiguousarray(a["L0_attn_x"].reshape(B * T, C)),
        "w_dram": np.ascontiguousarray(np.concatenate([parts[n] for n in WCOLS], axis=1)),
        "right_dram": np.ascontiguousarray(a["L1_ffn_right"].reshape(E1 * R1, C)),
        "const_dram": _layer_1_constants(), "alibi_q_dram": q_rows, "alibi_k_dram": k_rows, "masks_dram": masks,
    }
    nc = bacc.Bacc("TRN2", target_bir_lowering=False, num_devices=1)
    args = [nc.dram_tensor(n, v.shape, mybir.dt.from_np(v.dtype), kind="ExternalInput").ap() for n, v in arrays.items()]
    args.append(nc.dram_tensor("out_dram", (B * T, C), F32, kind="ExternalOutput").ap())
    build(nc, *args)
    r = run_bass_kernel_spmd(nc, [arrays], core_ids=[0])
    return r.results[0]["out_dram"].reshape(B, T, C)
```

```python
from contextlib import ExitStack

import concourse.bass as bass
from concourse import mybir

F32 = mybir.dt.float32
BF16 = mybir.dt.bfloat16
F32R = mybir.dt.float32r
ALU = mybir.AluOpType
ACT = mybir.ActivationFunctionType
AX = mybir.AxisListType
RED = bass.bass_isa.ReduceOp

P = 128
B, T, C = 2, 1024, 128
NT = B * T // P
TPB = T // P
SPAN = 512
NSPAN = B * T // SPAN
TPS = SPAN // P

H0, D0 = 16, 8
GH = 4
NG = H0 // GH
GROUPS = [(b, g) for b in range(B) for g in range(NG)]
ALIBI_ROWS = 4
QK_ROWS = 9 * D0
MAX_K = 96
EXP_K = MAX_K + 3
VW = 16
STRIP = 32

H1, KV1, D1 = 16, 4, 64
HPG = H1 // KV1
QT = H1 * D1 // P
NCH = B * T // P
PROJ = 2 + QT
PROJ_OF = [range(0, 4), range(4, 8), range(8, PROJ), range(0)]
SIN_SLOTS, TURN_SLOTS = 3, 4

E1, R1, TOPK = 8, 4, 2
GL = E1 + E1 * R1

WCOLS = {}
_at = 0
for _name, _n in [("ident", P), ("attn", 3 * C), ("bq", 1), ("bk", 1), ("bv", C), ("lng", 1), ("lnb", 1),
                  ("bproj", 1), ("ffn0", C), ("proj", C), ("q1", H1 * D1), 
                  ("k1", KV1 * D1), ("v1", KV1 * D1), ("wo1", QT * C), ("lin1", C),
                  ("gl1", GL), ("blin", 1)]:
    WCOLS[_name] = (_at, _at + _n)
    _at += _n
NW = _at
FRONT = WCOLS["q1"][0]
CCOLS = {}
_at = 0
for _name, _n in [("cos", T), ("sin", T), ("decay", H1 * P), ("qdec", QT * P), ("kdec", H1),
                  ("blkdec", 2 * QT)]:
    CCOLS[_name] = (_at, _at + _n)
    _at += _n
NC_ = _at

UNITS = [(0, [(0, 0, 512)]), (0, [(1, 1, 384), (3, 3, 128)]), (0, [(2, 2, 256)]),
         (1, [(0, 4, 512)]), (1, [(1, 4, 512)]), (1, [(2, 4, 512)]), (1, [(3, 4, 512)]),
         (1, [(4, 4, 512)]), (1, [(5, 5, 384), (7, 7, 128)]), (1, [(6, 6, 256)])]
NU = len(UNITS)
NSTEP = NU * len(GROUPS)
UNIT_W = [sum(n for _, _, n in segs) for _, segs in UNITS]
MAXU = [[(h, a, 0)] + ([(h, b_, a + 1)] if b_ is not None else [])
        for h in range(GH) for a, b_ in ((7, None), (6, 0), (5, 1), (4, 2))]
MAXU += [[(h, 3, 0), (h + 1, 3, 4)] for h in (0, 2)]
NMAX = len(MAXU)
EARLY = 5
P_SLOTS = 3
ST_BANKS = 3
OP_SLOTS = 3
FIRST_ITEMS = 24
ITEM_RATE = 2.5
LEAD = 16
TAIL_STEP = NSTEP - LEAD + 2


def item_stream():
    out = []
    for n in range(len(GROUPS)):
        for u in range(NMAX):
            out.append(("max", n, u))
            if u == 1 and n:
                out.append(("turn", n - 1, 0))
    out += [("xn2T", b, 0) for b in range(B)] + [("turn", len(GROUPS) - 1, 0)]
    return out, out + [("yt", 0, 0), ("yt", 0, 1), ("yt", 1, 0), ("yT", 0, 0), ("yt", 1, 1), ("proj", 0, 0),
                       ("yT", 1, 0), ("back", 0, 0), ("proj", 1, 0), ("back", 1, 0), ("xn1T", 0, 0)]


MAIN_ITEMS, ITEMS = item_stream()
TURN_AT = {n: k for k, (kind, n, _) in enumerate(ITEMS) if kind == "turn"}
ITEM_AT = {(kind, n): k for k, (kind, n, u) in enumerate(ITEMS) if u == 0}
TRI = []
for _s in range(NSTEP):
    TRI.append((TRI[-1] if TRI else 0) + sum(i0 == j for j, i0, _ in UNITS[_s % NU][1]))


TAIL = len(ITEMS) - len(MAIN_ITEMS)
LN1_STEP = TAIL_STEP + TAIL


def items_of_step(s):
    def upto(s):
        return min(len(MAIN_ITEMS), FIRST_ITEMS + int(ITEM_RATE * s), (s + LEAD) * len(MAIN_ITEMS) // NSTEP) \
            + (TAIL if s == NSTEP - 1 else min(TAIL - 1, max(0, s - TAIL_STEP)))
    return range(upto(s - 1) if s else 0, upto(s))


def step_of(k):
    return next(s for s in range(NSTEP) if k in items_of_step(s))


X2_STEP = NU
FFN_STEP = step_of(len(MAIN_ITEMS) - 1) + 1


def build(nc, x, w, wright, consts, alibi_q, alibi_k, masks, out):
    alibi_q, alibi_k, masks = (v.bitcast(BF16) for v in (alibi_q, alibi_k, masks))
    with ExitStack() as ctx:
        def sb(name, shape, dt=F32, c=ctx):
            return c.enter_context(nc.sbuf_tensor(name, shape, dt))

        def sem(name):
            return ctx.enter_context(nc.semaphore(name))

        PS = ctx.enter_context(nc.psum_tensor("PS", [P, 8, 512], F32))

        x_sb = sb("x_sb", [P, NT, C])
        w_sb = sb("w_sb", [P, NW])
        c_sb = sb("c_sb", [P, NC_])
        right_sb = sb("right_sb", [E1 * R1, C])
        W = {n: w_sb[:, a:b] for n, (a, b) in WCOLS.items()}
        K = {n: c_sb[:, a:b] for n, (a, b) in CCOLS.items()}
        xn = sb("xn", [P, NT, C])
        xnT = sb("xnT", [P, B * T])
        stats = sb("stats", [P, NT, 6])
        mv = sb("mv", [P, NT, 2])
        std = sb("std", [P, NT])
        rstd = sb("rstd", [P, NT])
        rstd2 = sb("rstd2", [P, NT])

        l0 = ExitStack()
        xn2T = sb("xn2T", [P, B * T], c=l0)
        split = ExitStack()
        part_a = sb("part_a", [P, NSPAN, 3, SPAN], BF16, split)
        rest = sb("rest", [P, NSPAN, SPAN], F32, split)
        part_b = sb("part_b", [P, 2, 3, T], BF16, split)
        split.close()
        yacc = sb("yacc", [P, len(GROUPS), T], F32, l0)
        mrow = sb("mrow", [P, 2, T], BF16, l0)
        sT = sb("sT", [P, 2, SPAN], F32, l0)
        y = xnT[:, T:2 * T].rearrange("p (a n c) -> p a n c", n=TPS, c=C)
        yT = xn[:, TPB:NT, :].rearrange("p (a n) c -> p a (n c)", a=2)
        wq_a, wq_b, wq_c = xn[:, 0, :], xn[:, 1, :], W["ffn0"]
        vaug = sb("vaug", [P, NT, H0, VW], F32, l0)
        q_op = sb("q_op", [P, OP_SLOTS, GH, T], BF16, l0)
        k_op = sb("k_op", [P, OP_SLOTS, GH, T], BF16, l0)
        prob = sb("prob", [P, P_SLOTS, GH, SPAN], F32, l0)
        pmax = sb("pmax", [P, NMAX, TPB], F32, l0)
        rmax = sb("rmax", [P, GH, TPB], F32, l0)
        rleft = sb("rleft", [P, 2, GH, TPB], F32, l0)
        mpart = sb("mpart", [P, TPB, GH, 3], BF16, l0)
        rden = sb("rden", [P, 2, TPS * GH], F32, l0)
        masks_sb = sb("masks_sb", [P, 2, P], BF16, l0)
        ident_b, causal_b = masks_sb[:, 0, :], masks_sb[:, 1, :]
        small = sb("small", [P, 8], F32, l0)
        l0.close()

        l1 = ExitStack()
        faded = xn[:, 0:QT, :]
        twT = xn[0:E1 * R1, TPB:NT, :].rearrange("p (s n) c -> p s (n c)", s=2)
        oT = sb("oT", [P, 2, QT, SPAN], F32, l1)
        fT = sb("fT", [P, SPAN], F32, l1)
        vdec = sb("vdec", [P, 2, KV1, HPG, D1], F32, l1)
        vk = sb("vk", [P, 2, 2 * KV1 * D1], F32, l1)
        sm = sb("sm", [P, 4, SPAN], F32, l1)
        by_sin = sb("by_sin", [P, SIN_SLOTS, SPAN], F32, l1)
        turned = sb("turned", [P, TURN_SLOTS, SPAN], F32, l1)
        qr = sb("qr", [P, 2, QT, SPAN], F32, l1)
        kr = sb("kr", [P, 2, 2, SPAN], F32, l1)
        q_hi = sb("q_hi", [P, 2, QT, P], F32R, l1)
        q_lo = sb("q_lo", [P, 2, QT, P], F32R, l1)
        k_hi = sb("k_hi", [P, 2, 2, 2, P], F32R, l1)
        k_lo = sb("k_lo", [P, 2, 2, 2, P], F32R, l1)
        qd = sb("qd", [P, 2, QT, P], F32, l1)
        state = sb("state", [P, 2, QT, P], F32, l1)
        l1.close()
        spare, taken = oT[:, 1, :, :].rearrange("p k t -> p (k t)"), [0]

        def of_spare(n, c):
            taken[0] += n * c
            return spare[:, taken[0] - n * c:taken[0]].rearrange("p (n c) -> p n c", n=n)

        gl_sb, ex = of_spare(NT, GL), of_spare(NT, E1)
        sc = of_spare(NT, 2 * E1)
        kept, top, col = of_spare(NT, 2 * E1), of_spare(NT, 8), of_spare(3, NT)
        tw = w_sb[:, WCOLS["attn"][0]:WCOLS["attn"][0] + NT * E1 * R1].rearrange("p (n c) -> p n c", n=NT)

        q_scr = nc.dram_tensor("q_scr", [B, H0, 3 * D0, T], BF16, kind="Internal").ap()
        k_scr = nc.dram_tensor("k_scr", [B, H0, 5 * D0, T], BF16, kind="Internal").ap()
        s_front = sem("s_front")
        s_masks = sem("s_masks")
        s_big = sem("s_big")
        s_x = [sem(f"s_x{i}") for i in range(NSPAN)]
        dve = sem("dve")
        s_clear = sem("s_clear")
        s_var = sem("s_var")
        s_std = sem("s_std")
        s_xn = sem("s_xn")
        fillA, freeA = sem("fillA"), sem("freeA")
        fillD, freeD = sem("fillD"), sem("freeD")
        s_bq = sem("s_bq")
        s_part = [sem(f"s_part{i}") for i in range(3)]
        s_left = sem("s_left")
        s_unit, s_unit_used = sem("s_unit"), sem("s_unit_used")
        s_scr = [sem(f"s_scr{i}") for i in range(B)]
        s_rstd2 = sem("s_rstd2")
        s_xn2 = sem("s_xn2")
        s_kconst = sem("s_kconst")
        s_op = [sem(f"s_op{i}") for i in range(OP_SLOTS)]
        s_vaug = sem("s_vaug")
        s_gmax = sem("s_gmax")
        s_gall = sem("s_gall")
        s_ffn = sem("s_ffn")
        s_clip = sem("s_clip")
        s_item, s_item_used = sem("s_item"), sem("s_item_used")
        s_mpart = sem("s_mpart")
        s_mop = [sem(f"s_mop{i}") for i in range(2)]
        s_st = sem("s_st")
        s_exp = sem("s_exp")
        s_tri = sem("s_tri")
        s_pv = sem("s_pv")
        s_acc = sem("s_acc")
        s_out = sem("s_out")
        s_glx = sem("s_glx"); s_ex = sem("s_ex"); s_tw = sem("s_tw")
        s_zero = sem("s_zero")
        s_pj, s_pj_free = sem("s_pj"), sem("s_pj_free")
        s_turned = [sem(f"s_turned{i}") for i in range(TURN_SLOTS)]
        s_qr = sem("s_qr"); s_kr = sem("s_kr"); s_hi, s_lo = sem("s_hi"), sem("s_lo")
        s_z, s_zf = sem("s_z"), sem("s_zf")
        s_vd = sem("s_vd")
        s_qd = sem("s_qd")
        s_sc, s_sm = sem("s_sc"), sem("s_sm")
        s_kv = sem("s_kv")
        s_state, s_faded = sem("s_state"), sem("s_faded")
        s_o, s_oT = sem("s_o"), sem("s_oT")

        RA, RD = [], []
        FIRST = range(NSPAN // B)
        RA += [("xnT", i) for i in FIRST] + [(name, i) for i in FIRST for name in "qk"]
        RD += [("v", i) for i in FIRST]
        SECOND = range(NSPAN // B, NSPAN)
        UB = [("xnT", i) for i in SECOND] + [(name, i) for i in SECOND for name in "qk"] + [("v", i) for i in SECOND]
        UB_AT = {n: k for k, n in enumerate(UB)}

        def parts_of(k):
            if k < NSPAN:
                return part_a[:, k, :, :]
            t = SPAN * ((k - NSPAN) // 2)
            return part_b[:, k % 2, :, t:t + SPAN]

        N_A = len(RA)
        N_D = len(RD)
        RD += [("yt", i, g) for i in SECOND for g in range(NG)] + [("back", i) for i in SECOND]
        for i in SECOND:
            RA += [("yT", i), ("proj", i)]
        POST = []
        for i, ms in zip(SECOND, (range(0, 3), range(0))):
            POST += [("yt", i, g) for g in range(NG)] + [("p", 0, m) for m in ms]
        i, j = SECOND
        POST += [("yT", i), ("p", 0, 3), ("p", 0, 4), ("proj", i), ("yT", j), ("p", 0, 5), ("back", i), ("p", 0, 6),
                 ("proj", j), ("p", 0, 7), ("back", j), ("p", 0, 8), ("p", 0, 9)]
        PJ = [("p", 0, m) for m in range(PROJ)]
        GATE_CHUNK = 1
        Z = [("vk", 0)]
        for c in range(NCH):
            i, ch = divmod(c, TPS)
            if i + 1 < NSPAN:
                PJ += [("p", i + 1, m) for m in PROJ_OF[ch]]
            if ch == 0 and i:
                Z += [("twT", i - 1), ("out", i - 1)]
            if ch == 1 and i:
                PJ.append(("back", i - 1))
            if c == GATE_CHUNK:
                PJ += [("gl", j) for j in range(NSPAN)]
                Z += [("xn1T", j) for j in SECOND]
            if c + 1 < NCH:
                Z.append(("vk", c + 1))
        Z += [("twT", NSPAN - 1), ("out", NSPAN - 1)]
        PJ.append(("back", NSPAN - 1))
        PJ_at = {n: k for k, n in enumerate(PJ)}
        Z_at = {n: k for k, n in enumerate(Z)}

        def sums(c):
            return c - c // TPB

        def later(c):
            return c - (c + TPB - 1) // TPB

        def fades(c):
            return c - (c + TPB - 1) // TPB - c // TPB

        def states(c):
            return 2 * sums(c)

        def bank_a(k):
            return (k % 4, 4) if k < N_A else (2 + k % 2, 2)

        def wait_rotated(engine, n):
            i, m = divmod(n, PROJ)
            engine.wait_ge(s_kr, 2 * i + min(m, 2))
            if QT * i + max(m - 2, 0):
                engine.wait_ge(s_qr, QT * i + max(m - 2, 0))

        A_at = {n: i for i, n in enumerate(RA)}
        D_at = {n: i for i, n in enumerate(RD)}

        block = ctx.enter_context(nc.Block())

        OP_EACH = 16 * (1 + 2 * GH)
        SCR_EACH = 16 * 8 * NSPAN // B

        @block.sync
        def _(sp):
            xt = x.rearrange("(n p) c -> p n c", p=P)
            for i in range(NSPAN):
                sp.dma_start(x_sb[:, TPS * i:TPS * i + TPS, :], xt[:, TPS * i:TPS * i + TPS, :]).then_inc(s_x[i], 16)
                if i == 0:
                    sp.dma_start(w_sb[:, 0:FRONT], w[:, 0:FRONT]).then_inc(s_front, 16)
            sp.dma_start(masks_sb[:, :, :], masks).then_inc(s_masks, 16)

            def store(b, n, a, src, cs):
                for at in ((a,) if n == 0 or a == 2 else (a, a + 3)):
                    dst = (q_scr, k_scr)[n][b, :, D0 * at:D0 * at + D0, cs]
                    sp.dma_start(dst, src).then_inc(s_scr[b], 16)

            def load_ops(n):
                b, g = GROUPS[n]
                slot = n % OP_SLOTS
                if n >= OP_SLOTS:
                    sp.wait_ge(s_st, GH * NU * (n - OP_SLOTS + 1))
                if n % NG == 0:
                    sp.wait_ge(s_scr[b], SCR_EACH)
                sp.dma_start(q_op[0:ALIBI_ROWS, slot, :, :],
                             alibi_q[g * GH:g * GH + GH].rearrange("h r t -> r h t")).then_inc(s_op[slot], 16)
                for h in range(GH):
                    hh = g * GH + h
                    sp.dma_start(q_op[ALIBI_ROWS:ALIBI_ROWS + QK_ROWS, slot, h, :],
                                 q_scr[b, hh].rearrange("(o r) t -> o r t", o=1).broadcast_to([3, 3 * D0, T])).then_inc(s_op[slot], 16)
                    parts = k_scr[b, hh]
                    windows = bass.AP(tensor=parts.tensor, offset=parts.offset, ap=[[D0 * T, 3], [T, 3 * D0], [1, T]])
                    sp.dma_start(k_op[ALIBI_ROWS:ALIBI_ROWS + QK_ROWS, slot, h, :], windows).then_inc(s_op[slot], 16)

            def load_m(n):
                slot = n % OP_SLOTS
                sp.wait_ge(s_item_used, TURN_AT[n] + 1)
                for h in range(GH):
                    sp.dma_start(q_op[MAX_K:MAX_K + 3, slot, h, :],
                                 mrow[MAX_K + 3 * h:MAX_K + 3 * h + 3, n % 2, :]).then_inc(s_mop[n % 2], 16)

            def store_parts(ks):
                for k in ks:
                    i, n = divmod(k, 2)
                    b, half = divmod(i, 2)
                    for a in range(3):
                        sp.wait_ge(s_part[a], k + 1)
                        store(b, n, a, parts_of(k)[:, a, :], slice(SPAN * half, SPAN * half + SPAN))

            store_parts(range(NSPAN))
            sp.wait_ge(s_clear, 2)
            for r0, r1, k0 in ((0, ALIBI_ROWS, 0), (MAX_K, EXP_K, ALIBI_ROWS)):
                rows = alibi_k[k0:k0 + r1 - r0].rearrange("r (o t) -> r o t", o=1)
                sp.dma_start(k_op[r0:r1, :, :, :].rearrange("r s h t -> r (s h) t"),
                             rows.broadcast_to([r1 - r0, OP_SLOTS * GH, T])).then_inc(s_kconst, 16)
            for n in range(OP_SLOTS):
                load_ops(n)
            store_parts(range(NSPAN, 2 * NSPAN))
            load_m(0)
            sp.dma_start(w_sb[:, FRONT:], w[:, FRONT:]).then_inc(s_big, 16)
            sp.dma_start(c_sb[:, :], consts).then_inc(s_big, 16)
            sp.dma_start(right_sb[:, :], wright).then_inc(s_big, 16)
            load_m(1)
            for n in range(2, len(GROUPS)):
                if n + 1 < len(GROUPS):
                    load_ops(n + 1)
                load_m(n)

            ot = out.rearrange("(n p) c -> p n c", p=P)

            def turn_halves(i, ms):
                if i == NSPAN:
                    return
                for m in ms:
                    n = PROJ * i + m
                    sp.wait_ge(s_pj_free, PJ_at[("p", i, m)] + 1)
                    if n >= TURN_SLOTS:
                        wait_rotated(sp, n - TURN_SLOTS + 1)
                    for odd in range(2):
                        sp.dma_start(turned[odd:P:2, n % TURN_SLOTS, :], by_sin[1 - odd:P:2, n % SIN_SLOTS, :]).then_inc(s_turned[n % TURN_SLOTS], 16)

            def store_out(i):
                sp.wait_ge(s_pj_free, PJ_at[("back", i)] + 1)
                sp.dma_start(ot[:, TPS * i:TPS * i + TPS, :], x_sb[:, TPS * i:TPS * i + TPS, :]).then_inc(s_out, 16)

            turn_halves(0, range(PROJ))
            for c in range(NCH):
                i, ch = divmod(c, TPS)
                turn_halves(i + 1, PROJ_OF[ch])
                if ch == 1 and i:
                    store_out(i - 1)
            store_out(NSPAN - 1)
            sp.wait_ge(s_out, 16 * NSPAN)


        @block.tensor
        def _(pe):
            mm, tr = nc.tensor.matmul, nc.tensor.transpose

            def unit_a(name):
                k = A_at[name]
                bank, banks = bank_a(k)
                if k >= banks:
                    pe.wait_ge(freeA, k - banks + 1)
                return PS[:, bank, :]

            def unit_d(name):
                k = D_at[name]
                if k >= 4:
                    pe.wait_ge(freeD, k - 3)
                return PS[:, 4 + k % 4, :]

            pe.wait_ge(s_front, 16)
            for i in FIRST:
                ps = unit_a(("xnT", i))
                pe.wait_ge(s_xn, TPS * (i + 1))
                for j in range(TPS):
                    last = tr(ps[:, P * j:P * j + P], xn[:, TPS * i + j, :], W["ident"])
                last.then_inc(fillA, 1)
            for i in FIRST:
                pe.wait_ge(freeA, A_at[("xnT", i)] + 1)
                cs = slice(SPAN * i, SPAN * i + SPAN)
                for n, name in enumerate("qk"):
                    mm(unit_a((name, i)), W["attn"][:, C * n:C * n + C], xnT[:, cs], start=True, stop=True).then_inc(fillA, 1)
                ps = unit_d(("v", i))
                for j in range(TPS):
                    last = mm(ps[:, P * j:P * j + P], xnT[:, SPAN * i + P * j:SPAN * i + P * j + P],
                              W["attn"][:, 2 * C:3 * C], start=True, stop=True)
                last.then_inc(fillD, 1)

            pe.wait_ge(freeA, N_A)
            pe.wait_ge(freeD, N_D)
            pe.wait_ge(s_masks, 16)
            pe.wait_ge(s_kconst, 32)

            def item(k):
                kind, n, u = ITEMS[k]
                if k >= 2:
                    pe.wait_ge(s_item_used, k - 1)
                ring = 3 + 2 * (k % 2)
                if kind == "max":
                    slot = n % OP_SLOTS
                    if u == 0:
                        pe.wait_ge(s_op[slot], OP_EACH * (n // OP_SLOTS + 1))
                    for h, i, at in MAXU[u]:
                        j = 0
                        while j <= i:
                            c0 = at + j
                            nb = min(i + 1 - j, 4 - c0 % 4)
                            o = PS[:, ring + c0 // 4, P * (c0 % 4):P * (c0 % 4 + nb)]
                            diag = j + nb == i + 1
                            last = mm(o, q_op[0:MAX_K, slot, h, P * i:P * i + P], k_op[0:MAX_K, slot, h, P * j:P * (j + nb)],
                                      start=True, stop=not diag, skip_group_check=True)
                            if diag:
                                last = mm(o[:, P * (nb - 1):P * nb], ident_b, causal_b, start=False, stop=True,
                                          skip_group_check=True)
                            j += nb
                    last.then_inc(s_item, 1)
                elif kind != "turn":
                    o = PS[:, ring:ring + 2, :]
                    if kind == "yt":
                        pe.wait_ge(s_acc, 1 + 2 * NG)
                        for m in range(2):
                            for j in range(TPS):
                                last = tr(o[:, m, P * j:P * j + P],
                                          yacc[:, 2 * u + m, SPAN * n + P * j:SPAN * n + P * j + P], W["ident"])
                    elif kind == "yT":
                        pe.wait_ge(s_item_used, max(j for j, it in enumerate(ITEMS) if it[:2] == ("yt", n)) + 1)
                        for j in range(TPS):
                            last = tr(o[:, 0, P * j:P * j + P], y[:, n % 2, j, :], W["ident"])
                    elif kind == "proj":
                        pe.wait_ge(s_ffn, 1)
                        pe.wait_ge(s_clip, 1)
                        mm(o[:, 0, :], wq_c[:, :], xn2T[:, SPAN * n:SPAN * n + SPAN], start=True, stop=False)
                        pe.wait_ge(s_item_used, ITEM_AT["yT", n] + 1)
                        last = mm(o[:, 0, :], W["proj"], yT[:, n % 2, :], start=False, stop=True)
                    elif kind == "back":
                        pe.wait_ge(s_item_used, ITEM_AT["proj", n] + 1)
                        for j in range(TPS):
                            last = tr(o[:, 0, P * j:P * j + P], sT[:, n % 2, P * j:P * j + P], W["ident"])
                    else:
                        if kind == "xn2T":
                            pe.wait_ge(s_xn2, TPB * (n + 1))
                        else:
                            pe.wait_ge(s_xn, NT + TPB * (n + 1))
                        for j in range(TPB):
                            last = tr(o[:, j // TPS, P * (j % TPS):P * (j % TPS) + P], xn[:, TPB * n + j, :], W["ident"])
                    last.then_inc(s_item, 1)
                else:
                    pe.wait_ge(s_mpart, n + 1)
                    o = PS[MAX_K:MAX_K + 3 * GH, ring, :].bitcast(BF16)
                    for i in range(TPB):
                        last = tr(o[:, P * i:P * i + P], mpart[:, i, :, :].rearrange("p h a -> p (h a)"), ident_b)
                    last.then_inc(s_item, 1)

            def scores(s, heads):
                n, u = divmod(s, NU)
                slot = n % OP_SLOTS
                if u == 0 and heads[0] == 0:
                    pe.wait_ge(s_mop[n % 2], 16 * GH * (n // 2 + 1))
                for h in heads:
                    k = GH * s + h
                    if k >= ST_BANKS:
                        pe.wait_ge(s_exp, k - ST_BANKS + 1)
                    at = 0
                    for j, i0, nn in UNITS[u][1]:
                        last = mm(PS[:, k % ST_BANKS, at:at + nn], k_op[0:EXP_K, slot, h, P * j:P * j + P],
                                  q_op[0:EXP_K, slot, h, P * i0:P * i0 + nn], start=True, stop=True)
                        at += nn
                    last.then_inc(s_st, 1)

            def pv(s):
                n, u = divmod(s, NU)
                b, g = GROUPS[n]
                half, segs = UNITS[u]
                pe.wait_ge(s_exp, GH * (s + 1))
                pe.wait_ge(s_tri, TRI[s])
                if u in (0, 3):
                    pe.wait_ge(s_acc, 1 + 2 * n + (u == 3))
                at = 0
                for j, i0, nn in segs:
                    c0 = P * i0 - SPAN * half
                    for h in range(GH):
                        last = mm(PS[STRIP * h:STRIP * h + VW, 7, c0:c0 + nn], vaug[:, TPB * b + j, g * GH + h, :],
                                  prob[:, s % P_SLOTS, h, at:at + nn], start=(j == 0),
                                  stop=(u in (2, 9)), skip_group_check=True)
                    at += nn
                last.then_inc(s_pv, 1)

            def unit_b(k):
                if k >= len(UB):
                    return
                name, i = UB[k]
                if k >= 3:
                    pe.wait_ge(s_unit_used, k - 2)
                ps = PS[:, k % 3, :]
                if name == "xnT":
                    pe.wait_ge(s_xn, TPS * (i + 1))
                    for j in range(TPS):
                        last = tr(ps[:, P * j:P * j + P], xn[:, TPS * i + j, :], W["ident"])
                else:
                    pe.wait_ge(s_unit_used, UB_AT["xnT", i] + 1)
                    if name == "v":
                        for j in range(TPS):
                            mm(ps[:, P * j:P * j + P], xnT[:, SPAN * i + P * j:SPAN * i + P * j + P],
                               W["attn"][:, 2 * C:3 * C], start=True, stop=False, skip_group_check=True)
                            last = mm(ps[:, P * j:P * j + P], W["ident"], W["bv"], start=False, stop=True,
                                      skip_group_check=True)
                    else:
                        cols = slice(C * "qk".index(name), C * "qk".index(name) + C)
                        last = mm(ps, W["attn"][:, cols], xnT[:, SPAN * i:SPAN * i + SPAN], start=True, stop=True)
                last.then_inc(s_unit, 1)

            for k in range(EARLY):
                unit_b(k)
            for k in items_of_step(0):
                item(k)
                if k % 3 == 2:
                    unit_b(EARLY + k // 3)
            pe.wait_ge(s_unit_used, len(UB))
            for s in range(NSTEP + 1):
                beside = items_of_step(s) if 0 < s < NSTEP else ()
                for half in range(2):
                    if s < NSTEP:
                        scores(s, range(GH // 2 * half, GH // 2 * (half + 1)))
                    for k in (beside[:len(beside) // 2], beside[len(beside) // 2:])[half]:
                        item(k)
                if s:
                    pv(s - 1)

            pe.wait_ge(s_exp, GH * NSTEP)
            pe.wait_ge(s_item_used, len(ITEMS))
            pe.wait_ge(s_acc, 1 + 2 * len(GROUPS))
            pe.wait_ge(s_ffn, 1)
            pe.wait_ge(s_clip, B)

            def turn_heads(i, g):
                b, half = divmod(i, 2)
                ps = unit_d(("yt", i, g))
                for j in range(TPS):
                    last = tr(ps[:, P * j:P * j + P],
                              yacc[:, NG * b + g, SPAN * half + P * j:SPAN * half + P * j + P], W["ident"])
                last.then_inc(fillD, 1)

            def outputs_turned(i):
                ps = unit_a(("yT", i))
                pe.wait_ge(freeD, D_at[("yt", i, NG - 1)] + 1)
                for j in range(TPS):
                    last = tr(ps[:, P * j:P * j + P], y[:, i % 2, j, :], W["ident"])
                last.then_inc(fillA, 1)

            def project(i):
                ps = unit_a(("proj", i))
                mm(ps, wq_c[:, :], xn2T[:, SPAN * i:SPAN * i + SPAN], start=True, stop=False)
                pe.wait_ge(freeA, A_at[("yT", i)] + 1)
                mm(ps, W["proj"], yT[:, i % 2, :], start=False, stop=True).then_inc(fillA, 1)

            def back(i):
                pe.wait_ge(freeA, A_at[("proj", i)] + 1)
                ps = unit_d(("back", i))
                for j in range(TPS):
                    last = tr(ps[:, P * j:P * j + P], sT[:, i % 2, P * j:P * j + P], W["ident"])
                last.then_inc(fillD, 1)

            def bank01(name):
                k = PJ_at[name]
                if k >= 2:
                    pe.wait_ge(s_pj_free, k - 1)
                return PS[:, k % 2, :]

            def bank7(name):
                k = Z_at[name]
                if k:
                    pe.wait_ge(s_zf, k)
                return PS[:, 7, :]

            def project1(i, ms):
                if i == NSPAN:
                    return
                for m in ms:
                    w = W["k1"][:, P * m:P * m + P] if m < 2 else W["q1"][:, P * (m - 2):P * (m - 2) + P]
                    mm(bank01(("p", i, m)), w, xnT[:, SPAN * i:SPAN * i + SPAN], start=True, stop=True).then_inc(s_pj, 1)

            def chunk_vk(c):
                if c == NCH:
                    return
                i, ch = divmod(c, TPS)
                ps = bank7(("vk", c))
                mm(ps[:, 0:KV1 * D1], xnT[:, P * c:P * c + P], W["v1"], start=True, stop=True)
                pe.wait_ge(s_kr, 2 * (i + 1))
                for pr in range(2):
                    last = tr(ps[:, KV1 * D1 + P * pr:KV1 * D1 + P * pr + P], kr[:, i % 2, pr, P * ch:P * ch + P], W["ident"])
                last.then_inc(s_z, 1)

            def score(c, g):
                i, ch = divmod(c, TPS)
                m = KV1 * c + g
                if m >= 2:
                    pe.wait_ge(s_sm, m - 1)
                if g % 2 == 0:
                    pe.wait_ge(s_hi, 4 * c + 3 + g // 2)
                    pe.wait_ge(s_lo, 4 * c + 3 + g // 2)
                out_ = PS[:, 2 + m % 2, :].rearrange("p (a t) -> p a t", a=HPG)
                tiles = slice(HPG * (g // 2), HPG * (g // 2) + HPG)
                for n, (k_part, q_part) in enumerate(((k_hi, q_hi), (k_hi, q_lo), (k_lo, q_hi))):
                    last = mm(out_, k_part[:, c % 2, g // 2, g % 2, :], q_part[:, c % 2, tiles, :], start=(n == 0), stop=(n == 2))
                last.then_inc(s_sc, 1)

            def mix(c, pr):
                first = c % TPB == 0
                if c:
                    pe.wait_ge(s_oT, 2 * c + pr - 1)
                pe.wait_ge(s_zf, Z_at[("vk", c)] + 1)
                for q in range(2):
                    g = 2 * pr + q
                    m = KV1 * c + g
                    pe.wait_ge(s_sm, m + 1)
                    last = mm(PS[D1 * q:D1 * q + D1, 4 + pr, :], vk[:, c % 2, D1 * g:D1 * g + D1], sm[:, m % 4, :],
                              start=True, stop=first, skip_group_check=True)
                if not first:
                    pe.wait_ge(s_qd, later(c + 1))
                    pe.wait_ge(s_state, states(c))
                    for a in range(HPG):
                        last = mm(PS[:, 4 + pr, P * a:P * a + P], state[:, c % 2, HPG * pr + a, :],
                                  qd[:, c % 2, HPG * pr + a, :], start=False, stop=True, skip_group_check=True)
                last.then_inc(s_o, 1)

            def kv_sums(c):
                if c % TPB == TPB - 1:
                    return
                pe.wait_ge(s_vd, KV1 * (sums(c) + 1))
                if c:
                    pe.wait_ge(s_state, states(c))
                for g in range(KV1):
                    pr, q = divmod(g, 2)
                    last = mm(PS[D1 * q:D1 * q + D1, 6, 256 * pr:256 * pr + 256],
                              vk[:, c % 2, KV1 * D1 + D1 * g:KV1 * D1 + D1 * g + D1],
                              vdec[:, c % 2, g, :, :].rearrange("p h e -> p (h e)"), start=True, stop=True,
                              skip_group_check=True)
                last.then_inc(s_kv, 1)

            def span_out(i):
                ps = bank7(("out", i))
                cs = slice(SPAN * i, SPAN * i + SPAN)
                mm(ps, W["lin1"], xnT[:, cs], start=True, stop=False)
                pe.wait_ge(s_zf, Z_at[("twT", i)] + 1)
                mm(ps, right_sb[:, :], twT[:, i % 2, :], start=False, stop=False)
                pe.wait_ge(s_oT, 2 * TPS * (i + 1))
                for kt in range(QT):
                    last = mm(ps, W["wo1"][:, C * kt:C * kt + C], oT[:, i % 2, kt, :], start=False, stop=(kt == QT - 1))
                last.then_inc(s_z, 1)

            def span_back(i):
                ps = bank01(("back", i))
                pe.wait_ge(s_zf, Z_at[("out", i)] + 1)
                for j in range(TPS):
                    last = tr(ps[:, P * j:P * j + P], fT[:, P * j:P * j + P], W["ident"])
                last.then_inc(s_pj, 1)

            def turn_late(i):
                ps = bank7(("xn1T", i))
                pe.wait_ge(s_xn, NT + TPS * (i + 1))
                for j in range(TPS):
                    last = tr(ps[:, P * j:P * j + P], xn[:, TPS * i + j, :], W["ident"])
                last.then_inc(s_z, 1)

            def gate(i):
                ps = bank01(("gl", i))
                if i in SECOND:
                    pe.wait_ge(s_zf, Z_at[("xn1T", i)] + 1)
                for j in range(TPS):
                    last = mm(ps[:, GL * j:GL * j + GL], xnT[:, SPAN * i + P * j:SPAN * i + P * j + P], W["gl1"],
                              start=True, stop=True)
                last.then_inc(s_pj, 1)

            def turn_weighted(i):
                ps = bank7(("twT", i))
                pe.wait_ge(s_tw, 1)
                for j in range(TPS):
                    last = tr(ps[0:E1 * R1, P * j:P * j + P], tw[:, TPS * i + j, :], W["ident"])
                last.then_inc(s_z, 1)

            pe.wait_ge(s_big, 48)
            for name in POST:
                if name[0] == "yt":
                    turn_heads(*name[1:])
                elif name[0] == "p":
                    project1(0, name[2:])
                else:
                    {"yT": outputs_turned, "proj": project, "back": back}[name[0]](name[1])
            pe.wait_ge(freeA, len(RA))
            pe.wait_ge(freeD, len(RD))
            pe.wait_ge(s_zero, 3)
            chunk_vk(0)
            for c in range(NCH):
                i, ch = divmod(c, TPS)
                f = PROJ_OF[ch]
                score(c, 0)
                if ch == 0 and i:
                    turn_weighted(i - 1)
                score(c, 1)
                if ch == 0 and i:
                    span_out(i - 1)
                if c == GATE_CHUNK:
                    turn_late(SECOND[0])
                project1(i + 1, f[0:1])
                score(c, 2)
                mix(c, 0)
                score(c, 3)
                if c == GATE_CHUNK:
                    turn_late(SECOND[1])
                project1(i + 1, f[1:3])
                mix(c, 1)
                kv_sums(c)
                project1(i + 1, f[3:])
                if ch == 1 and i:
                    span_back(i - 1)
                if c == GATE_CHUNK:
                    for j in range(NSPAN):
                        gate(j)
                chunk_vk(c + 1)
            turn_weighted(NSPAN - 1)
            span_out(NSPAN - 1)
            span_back(NSPAN - 1)

        @block.vector
        def _(v):
            n_dve = [0]
            vec = nc.vector

            def link(ins):
                n_dve[0] += 1
                ins.then_inc(dve, 1)
                v.wait_ge(dve, n_dve[0])

            def note(ins):
                n_dve[0] += 1
                return ins.then_inc(dve, 1)

            def settle():
                v.wait_ge(dve, n_dve[0])

            def moments(b, eps, load=False):
                tiles = range(TPB * b, TPB * b + TPB)
                for i in tiles:
                    if load and i % TPS == 0:
                        v.wait_ge(s_x[i // TPS], 16)
                    note(vec.bn_stats(out=stats[:, i, :], in_=x_sb[:, i, :]))
                settle()
                for i in tiles:
                    note(vec.bn_aggr(out=mv[:, i, :], in_=stats[:, i, :]))
                settle()
                t = slice(tiles[0], tiles[-1] + 1)
                vec.tensor_scalar(std[:, t], mv[:, t, 1], eps, None, ALU.add).then_inc(s_var, 1)

            def normalise(b, turn):
                v.wait_ge(s_std, turn + 1)
                t = slice(TPB * b, TPB * b + TPB)
                link(vec.reciprocal(rstd[:, t], rstd[:, t]))
                for i in range(TPB * b, TPB * b + TPB):
                    vec.tensor_scalar(xn[:, i, :], x_sb[:, i, :], mv[:, i, 0:1], rstd[:, i:i + 1],
                                      ALU.subtract, ALU.mult).then_inc(s_xn, 1)

            def wait_d(name):
                k = D_at[name]
                v.wait_ge(fillD, k + 1)
                return PS[:, 4 + k % 4, :]

            def left(k):
                v.wait_ge(s_part[0], k + 1)
                vec.tensor_tensor(rest[:, k, :], rest[:, k, :], part_a[:, k, 0, :], ALU.subtract).then_inc(s_left, 1)

            def third(k):
                v.wait_ge(s_part[1], k + 1)
                vec.tensor_tensor(part_a[:, k, 2, :], rest[:, k, :], part_a[:, k, 1, :], ALU.subtract).then_inc(s_part[2], 1)

            def bias_v(t0, ps):
                n = ps.shape[1]
                return vec.tensor_tensor(vaug[:, t0:t0 + n, :, 0:D0], ps.rearrange("p n (h d) -> p n h d", d=D0),
                                         W["bv"].rearrange("p (a h d) -> p a h d", a=1, d=D0).broadcast_to([P, n, H0, D0]),
                                         ALU.add)

            moments(0, 1e-5, load=True)
            normalise(0, 0)
            v.wait_ge(s_front, 16)
            vec.tensor_scalar(small[:, 7:8], W["bq"], float(D0) ** -0.5, None, ALU.mult).then_inc(s_bq, 1)
            for i in FIRST:
                for n in range(2):
                    left(2 * i + n)
                    if i or n:
                        third(2 * i + n - 1)
                ps = wait_d(("v", i))
                v.wait_ge(s_vaug, 2)
                bias_v(TPS * i, ps.rearrange("p (n c) -> p n c", n=TPS)).then_inc(freeD, 1)
            third(NSPAN - 1)
            moments(1, 1e-5, load=True)
            normalise(1, 1)
            link(vec.tensor_tensor(rstd2[:, :], rstd[:, :], rstd[:, :], ALU.mult))
            link(vec.tensor_tensor(rstd2[:, :], rstd2[:, :], mv[:, :, 1], ALU.mult))
            vec.tensor_scalar(std[:, :], rstd2[:, :], 1e-3, None, ALU.add).then_inc(s_var, 1)
            v.wait_ge(s_std, B + 1)
            vec.reciprocal(rstd2[:, :], rstd2[:, :]).then_inc(s_rstd2, 1)

            def largest():
                v.wait_ge(s_item_used, len(MAIN_ITEMS))
                link(vec.tensor_reduce(small[:, 0:1], W["ffn0"], AX.X, ALU.add, apply_absolute_value=True))
                vec.tensor_reduce(small[:, 1:2], xn2T[:, :], AX.X, ALU.max, apply_absolute_value=True).then_inc(s_gmax, 1)

            def ternary():
                v.wait_ge(s_gall, 2)
                link(vec.tensor_scalar(small[:, 0:1], small[:, 2:3], 1.0 / (C * C), None, ALU.mult))
                link(vec.tensor_scalar(small[:, 4:5], small[:, 0:1], 1e-5, None, ALU.add))
                link(vec.reciprocal(small[:, 4:5], small[:, 4:5]))
                link(vec.tensor_scalar(wq_a[:, :], W["ffn0"], small[:, 4:5], None, ALU.mult))
                link(vec.tensor_scalar(wq_b[:, :], wq_a[:, :], 0.5, None, ALU.is_gt))
                link(vec.tensor_scalar(wq_a[:, :], wq_a[:, :], -0.5, None, ALU.is_lt))
                link(vec.tensor_tensor(wq_b[:, :], wq_b[:, :], wq_a[:, :], ALU.subtract))
                link(vec.reciprocal(small[:, 5:6], small[:, 3:4]))
                link(vec.tensor_scalar(small[:, 6:7], small[:, 3:4], small[:, 0:1], 1.0 / 128.0, ALU.mult, ALU.mult))
                link(vec.tensor_scalar(small[:, 5:6], small[:, 5:6], 128.0, None, ALU.mult))
                vec.tensor_scalar(wq_c[:, :], wq_b[:, :], small[:, 6:7], None, ALU.mult).then_inc(s_ffn, 1)

            def quantise():
                top_q = 128.0 - 1e-5
                for h in range(B):
                    cs = slice(T * h, T * h + T)
                    link(vec.tensor_scalar(xn2T[:, cs], xn2T[:, cs], small[:, 5:6], top_q, ALU.mult, ALU.min))
                    vec.tensor_scalar(xn2T[:, cs], xn2T[:, cs], -top_q, None, ALU.max).then_inc(s_clip, 1)

            v.wait_ge(freeD, N_D)
            vec.memset(PS[:, 7, :], 0.0).then_inc(s_acc, 1)

            def item(k):
                kind, n, u = ITEMS[k]
                v.wait_ge(s_item, k + 1)
                ring = 3 + 2 * (k % 2)
                both = PS[:, ring:ring + 2, :]
                if kind == "max":
                    vec.tensor_reduce(pmax[:, u, :], PS[:, ring:ring + 2, :].rearrange("p a (b c) -> p (a b) c", c=P),
                                      AX.X, ALU.max).then_inc(s_item_used, 1)
                    if u == NMAX - 1:
                        v.wait_ge(s_item_used, k + 1)
                        four = pmax[:, 0:4 * GH, :].rearrange("p (h u) b -> p h u b", u=4)
                        for uu, (a, b_) in enumerate(((7, None), (6, 0), (5, 1), (4, 2))):
                            note(vec.tensor_reduce(rmax[:, :, a], four[:, :, uu, 0:a + 1], AX.X, ALU.max, negate=True))
                            if b_ is not None:
                                note(vec.tensor_reduce(rmax[:, :, b_], four[:, :, uu, a + 1:8], AX.X, ALU.max, negate=True))
                        note(vec.tensor_reduce(rmax[:, :, 3], pmax[:, 4 * GH:, :].rearrange("p u (h b) -> p (u h) b", h=2),
                                               AX.X, ALU.max, negate=True))
                        settle()
                        mp = mpart[:, :, :, :].rearrange("p i h a -> p h i a")
                        link(vec.tensor_copy(mp[:, :, :, 0], rmax[:, :, :]))
                        link(vec.tensor_tensor(rleft[:, 0], rmax[:, :, :], mp[:, :, :, 0], ALU.subtract))
                        link(vec.tensor_copy(mp[:, :, :, 1], rleft[:, 0]))
                        link(vec.tensor_tensor(rleft[:, 1], rleft[:, 0], mp[:, :, :, 1], ALU.subtract))
                        vec.tensor_copy(mp[:, :, :, 2], rleft[:, 1]).then_inc(s_mpart, 1)
                        v.wait_ge(s_mpart, n + 1)
                elif kind == "yt":
                    for m in range(2):
                        ins = normalise_heads(n, 2 * u + m, both[:, m, :])
                        if m == 0:
                            note(ins)
                    ins.then_inc(s_item_used, 1)
                elif kind == "yT":
                    vec.tensor_copy(yT[:, n % 2, :], both[:, 0, :]).then_inc(s_item_used, 1)
                elif kind == "proj":
                    vec.tensor_scalar(sT[:, n % 2, :], both[:, 0, :], W["bproj"], None, ALU.add).then_inc(s_item_used, 1)
                elif kind == "back":
                    add_to_x(n, both[:, 0, :]).then_inc(s_item_used, 1)
                elif kind == "xn1T":
                    vec.tensor_copy(xnT[:, T * n:T * n + T], both.rearrange("p a c -> p (a c)")).then_inc(s_item_used, 1)
                elif kind == "xn2T":
                    vec.tensor_scalar(xn2T[:, T * n:T * n + T], both.rearrange("p a c -> p (a c)"), W["lng"], W["lnb"],
                                      ALU.mult, ALU.add).then_inc(s_item_used, 1)
                else:
                    if n >= 2:
                        v.wait_ge(s_mop[n % 2], 16 * GH * (n // 2))
                    src = PS[MAX_K:MAX_K + 3 * GH, ring, :].bitcast(BF16)
                    vec.tensor_copy(mrow[MAX_K:MAX_K + 3 * GH, n % 2, :], src).then_inc(s_item_used, 1)

            def normalise_heads(i, g, ps):
                ps = ps.rearrange("p (m w) -> p m w", w=STRIP)
                link(vec.reciprocal(rden[:, g % 2, :], ps[:, :, D0]))
                return vec.tensor_tensor(y[:, i % 2, :, GH * D0 * g:GH * D0 * (g + 1)].rearrange("p n (h d) -> p n h d", d=D0),
                                         ps[:, :, 0:D0].rearrange("p (n h) d -> p n h d", h=GH),
                                         rden[:, g % 2, :].rearrange("p (n h a) -> p n h a", h=GH, a=1)
                                         .broadcast_to([P, TPS, GH, D0]), ALU.mult)

            def add_to_x(i, ps):
                xs = x_sb[:, TPS * i:TPS * i + TPS, :]
                return vec.tensor_tensor(xs, ps.rearrange("p (n c) -> p n c", n=TPS), xs, ALU.add)

            def acc(s):
                n, u = divmod(s, NU)
                if u in (2, 9):
                    v.wait_ge(s_pv, s + 1)
                    half = UNITS[u][0]
                    if u == 2 and n in (0, NSPAN - 1):
                        v.wait_ge(s_scr[n > 0], SCR_EACH)
                    vec.tensor_copy(yacc[:, n, SPAN * half:SPAN * half + SPAN], PS[:, 7, :]).then_inc(s_acc, 1)

            for k in items_of_step(0):
                item(k)
            for s in range(NSTEP + 1):
                if 0 < s < NSTEP:
                    for k in items_of_step(s):
                        item(k)
                if s == LN1_STEP:
                    v.wait_ge(s_item_used, len(ITEMS) - 1)
                    moments(0, 1e-5)
                if s == LN1_STEP + 1:
                    normalise(0, B + 1)
                if s:
                    acc(s - 1)
                if s == FFN_STEP:
                    largest()
                if s == FFN_STEP + 2:
                    ternary()
                    quantise()

            def after_attention():
                v.wait_ge(s_big, 48)
                for name in POST:
                    if name[0] == "yt":
                        normalise_heads(*name[1:], wait_d(name)).then_inc(freeD, 1)
                        v.wait_ge(freeD, D_at[name] + 1)
                    elif name[0] == "back":
                        add_to_x(name[1], wait_d(name)).then_inc(freeD, 1)
                    elif name[0] == "p":
                        rope(0, name[2:])
                v.wait_ge(freeD, len(RD))

            wide = lambda a: a.rearrange("p (n o) -> p n o", o=1).broadcast_to([P, NT, E1])

            def gate_logits():
                for i in range(NSPAN):
                    k = PJ_at[("gl", i)]
                    v.wait_ge(s_pj, k + 1)
                    vec.tensor_copy(gl_sb[:, TPS * i:TPS * i + TPS, :],
                                    PS[:, k % 2, 0:TPS * GL].rearrange("p (n c) -> p n c", n=TPS)).then_inc(s_pj_free, 1)
                v.wait_ge(s_pj_free, PJ_at[("gl", NSPAN - 1)] + 1)
                link(vec.tensor_reduce(col[:, 0, :], gl_sb[:, :, 0:E1], AX.X, ALU.max))
                vec.tensor_tensor(ex[:, :, :], gl_sb[:, :, 0:E1], wide(col[:, 0, :]), ALU.subtract).then_inc(s_glx, 1)

            def gate_weights():
                v.wait_ge(s_ex, 1)
                link(vec.tensor_reduce(col[:, 1, :], ex[:, :, :], AX.X, ALU.add))
                link(vec.reciprocal(col[:, 2, :], col[:, 1, :]))
                link(vec.memset(sc[:, :, E1:], -1.0))
                link(vec.tensor_tensor(sc[:, :, 0:E1], ex[:, :, :], wide(col[:, 2, :]), ALU.mult))
                for i in range(NT):
                    note(vec.max(top[:, i, :], sc[:, i, :]))
                settle()

            def gate_products():
                link(vec.memset(top[:, :, TOPK:8], -1.0))
                for i in range(NT):
                    note(vec.match_replace(kept[:, i, :], top[:, i, :], sc[:, i, :], 0.0))
                settle()
                link(vec.tensor_tensor(kept[:, :, 0:E1], sc[:, :, 0:E1], kept[:, :, 0:E1], ALU.subtract))
                vec.tensor_tensor(tw[:, :, :].rearrange("p n (e r) -> p n e r", r=R1),
                                  gl_sb[:, :, E1:].rearrange("p n (e r) -> p n e r", r=R1),
                                  kept[:, :, 0:E1].rearrange("p n (e o) -> p n e o", o=1).broadcast_to([P, NT, E1, R1]),
                                  ALU.mult).then_inc(s_tw, 1)

            def rope(i, ms):
                if i == NSPAN:
                    return
                for m in ms:
                    n = PROJ * i + m
                    k = PJ_at[("p", i, m)]
                    v.wait_ge(s_pj, k + 1)
                    if i >= 2 and m == 0:
                        v.wait_ge(s_o, 2 * TPS * (i - 1))
                        v.wait_ge(s_z, Z_at[("vk", TPS * (i - 1) - 1)] + 1)
                        v.wait_ge(s_hi, 4 * TPS * (i - 1))
                        v.wait_ge(s_lo, 4 * TPS * (i - 1))
                    t = slice(SPAN * (i % 2), SPAN * (i % 2) + SPAN)
                    dst = kr[:, i % 2, m, :] if m < 2 else qr[:, i % 2, m - 2, :]
                    note(vec.tensor_tensor(dst, PS[:, k % 2, :], K["cos"][:, t], ALU.mult))
                    if n >= SIN_SLOTS:
                        q, slot = divmod(n - SIN_SLOTS, TURN_SLOTS)
                        v.wait_ge(s_turned[slot], 32 * (q + 1))
                    vec.tensor_tensor(by_sin[:, n % SIN_SLOTS, :], PS[:, k % 2, :], K["sin"][:, t],
                                      ALU.mult).then_inc(s_pj_free, 1)

            def masked(c, g):
                m = KV1 * c + g
                v.wait_ge(s_sc, m + 1)
                if m >= 4:
                    v.wait_ge(s_o, (m - 4) // 2 + 1)
                vec.tensor_tensor(sm[:, m % 4, :], PS[:, 2 + m % 2, :], K["decay"][:, SPAN * g:SPAN * g + SPAN], ALU.mult).then_inc(s_sm, 1)

            def low_parts(c, pairs):
                if c == NCH:
                    return
                i, ch = divmod(c, TPS)
                t = slice(P * ch, P * ch + P)
                for pr in pairs:
                    v.wait_ge(s_hi, 4 * c + 3 + pr)
                    if c >= 2:
                        v.wait_ge(s_sc, KV1 * (c - 1))
                    tiles = slice(HPG * pr, HPG * pr + HPG)
                    vec.tensor_tensor(q_lo[:, c % 2, tiles, :], qr[:, i % 2, tiles, t], q_hi[:, c % 2, tiles, :].bitcast(F32),
                                      ALU.subtract).then_inc(s_lo, 1)
                    for q in range(2 if pr == 0 else 0):
                        rows = slice(D1 * q, D1 * q + D1)
                        vec.tensor_tensor(k_lo[rows, c % 2, :, q, :], kr[rows, i % 2, :, t],
                                          k_hi[rows, c % 2, :, q, :].bitcast(F32), ALU.subtract).then_inc(s_lo, 1)

            def advance(c):
                if c % TPB == TPB - 1:
                    return
                v.wait_ge(s_kv, sums(c + 1))
                v.wait_ge(s_o, 2 * (c + 1))
                if c % TPB:
                    v.wait_ge(s_faded, fades(c + 1))
                for q in range(2):
                    rows = slice(D1 * q, D1 * q + D1)
                    new = PS[rows, 6, :].rearrange("p (k e) -> p k e", e=D1)
                    dst = state[rows, (c + 1) % 2, :, rows]
                    if c % TPB == 0:
                        vec.tensor_copy(dst, new).then_inc(s_state, 1)
                    else:
                        vec.tensor_tensor(dst, new, faded[rows, :, rows], ALU.add).then_inc(s_state, 1)

            def span_back(i):
                k = PJ_at[("back", i)]
                v.wait_ge(s_pj, k + 1)
                xs = x_sb[:, TPS * i:TPS * i + TPS, :]
                vec.tensor_tensor(xs, PS[:, k % 2, :].rearrange("p (n c) -> p n c", n=TPS), xs, ALU.add).then_inc(s_pj_free, 1)

            after_attention()
            v.wait_ge(s_zero, 3)
            low_parts(0, (0,))
            for c in range(NCH):
                i, ch = divmod(c, TPS)
                f = PROJ_OF[ch]
                masked(c, 0)
                masked(c, 1)
                if ch == 0:
                    low_parts(c, (1,))
                rope(i + 1, f[0:1])
                masked(c, 2)
                if ch < TPS - 1:
                    low_parts(c + 1, (0, 1))
                masked(c, 3)
                rope(i + 1, f[1:3])
                advance(c)
                rope(i + 1, f[3:])
                if ch == TPS - 1:
                    low_parts(c + 1, (0,))
                if ch == 1 and i:
                    span_back(i - 1)
                if c == GATE_CHUNK - 1:
                    moments(1, 1e-5)
                    normalise(1, B + 2)
                if c == GATE_CHUNK:
                    gate_logits()
                if c == GATE_CHUNK + 1:
                    gate_weights()
                if c == GATE_CHUNK + 2:
                    gate_products()
            span_back(NSPAN - 1)

        @block.scalar
        def _(a):
            sca = nc.scalar

            def wait_a(name):
                k = A_at[name]
                a.wait_ge(fillA, k + 1)
                return PS[:, bank_a(k)[0], :]

            def root(turn, dst=rstd, tiles=range(NT)):
                a.wait_ge(s_var, turn + 1)
                part_ = slice(tiles[0], tiles[-1] + 1)
                sca.activation(dst[:, part_], std[:, part_], ACT.Sqrt).then_inc(s_std, 1)

            def second(k):
                a.wait_ge(s_left, k + 1)
                sca.copy(parts_of(k)[:, 1, :], rest[:, k % NSPAN, :]).then_inc(s_part[1], 1)

            def split_first(k, ps):
                return sca.activation(rest[:, k % NSPAN, :], ps, ACT.Identity, bias=W["bk"] if k % 2 else small[:, 7:8],
                                      scale=1.0 if k % 2 else float(D0) ** -0.5)

            root(0, tiles=range(TPB))
            for i in FIRST:
                sca.copy(xnT[:, SPAN * i:SPAN * i + SPAN], wait_a(("xnT", i))).then_inc(freeA, 1)
            a.wait_ge(s_front, 16)
            a.wait_ge(s_bq, 1)
            for k in range(NSPAN):
                i, n = divmod(k, 2)
                ps = wait_a(("qk"[n], i))
                split_first(k, ps).then_inc(freeA, 1)
                a.wait_ge(freeA, A_at[("qk"[n], i)] + 1)
                sca.copy(part_a[:, k, 0, :], rest[:, k, :]).then_inc(s_part[0], 1)
                if k:
                    second(k - 1)
            second(NSPAN - 1)
            root(1, tiles=range(TPB, NT))
            root(B, rstd2)

            for k, (name, i) in enumerate(UB):
                a.wait_ge(s_unit, k + 1)
                ps = PS[:, k % 3, :]
                if name == "xnT":
                    sca.copy(xnT[:, SPAN * i:SPAN * i + SPAN], ps).then_inc(s_unit_used, 1)
                elif name == "v":
                    a.wait_ge(s_vaug, 2)
                    sca.copy(vaug[:, TPS * i:TPS * i + TPS, :, 0:D0],
                             ps.rearrange("p (n h d) -> p n h d", n=TPS, d=D0)).then_inc(s_unit_used, 1)
                else:
                    m = 2 * i + "qk".index(name)
                    a.wait_ge(s_part[2], NSPAN)
                    split_first(m, ps).then_inc(s_unit_used, 1)
                    a.wait_ge(s_unit_used, k + 1)
                    sca.copy(parts_of(m)[:, 0, :], rest[:, m - NSPAN, :]).then_inc(s_part[0], 1)
                    if m > NSPAN:
                        second(m - 1)
                    if m == 2 * NSPAN - 1:
                        second(m)

            for s in range(NSTEP):
                u = s % NU
                if s >= P_SLOTS:
                    a.wait_ge(s_pv, s - P_SLOTS + 1)
                for h in range(GH):
                    k = GH * s + h
                    a.wait_ge(s_st, k + 1)
                    sca.activation(prob[:, s % P_SLOTS, h, 0:UNIT_W[u]], PS[:, k % ST_BANKS, 0:UNIT_W[u]],
                                   ACT.Exp).then_inc(s_exp, 1)
                if s == LN1_STEP:
                    root(B + 1, tiles=range(TPB))
            for i in SECOND:
                sca.copy(yT[:, i % 2, :], wait_a(("yT", i))).then_inc(freeA, 1)
                sca.activation(sT[:, i % 2, :], wait_a(("proj", i)), ACT.Identity, bias=W["bproj"]).then_inc(freeA, 1)
            a.wait_ge(s_big, 48)
            def high_parts(c, pairs):
                if c == NCH:
                    return
                i, ch = divmod(c, TPS)
                t = slice(P * ch, P * ch + P)
                for pr in pairs:
                    if ch == 0:
                        a.wait_ge(s_kr, 2 * (i + 1))
                        a.wait_ge(s_qr, QT * i + HPG * (pr + 1))
                    if c >= 2:
                        a.wait_ge(s_sc, KV1 * (c - 1))
                        a.wait_ge(s_lo, 4 * (c - 1))
                    tiles = slice(HPG * pr, HPG * pr + HPG)
                    sca.copy(q_hi[:, c % 2, tiles, :], qr[:, i % 2, tiles, t]).then_inc(s_hi, 1)
                    for q in range(2 if pr == 0 else 0):
                        rows = slice(D1 * q, D1 * q + D1)
                        sca.copy(k_hi[rows, c % 2, :, q, :], kr[rows, i % 2, :, t]).then_inc(s_hi, 1)

            def chunk_vk(c):
                if c == NCH:
                    return
                k = Z_at[("vk", c)]
                a.wait_ge(s_z, k + 1)
                if c >= 2:
                    a.wait_ge(s_vd, KV1 * sums(c - 1))
                    a.wait_ge(s_kv, sums(c - 1))
                    a.wait_ge(s_o, 2 * (c - 1))
                sca.copy(vk[:, c % 2, :], PS[:, 7, :]).then_inc(s_zf, 1)

            def span_out(i):
                k = Z_at[("out", i)]
                a.wait_ge(s_z, k + 1)
                if i:
                    a.wait_ge(s_pj, PJ_at[("back", i - 1)] + 1)
                sca.activation(fT[:, :], PS[:, 7, :], ACT.Identity, bias=W["blin"]).then_inc(s_zf, 1)

            def bank7_to(name, dst, rows=P):
                a.wait_ge(s_z, Z_at[name] + 1)
                sca.copy(dst, PS[0:rows, 7, :]).then_inc(s_zf, 1)

            def weighted(i):
                bank7_to(("twT", i), twT[:, i % 2, :], rows=E1 * R1)

            a.wait_ge(s_zero, 1)
            for op in (k_hi, k_lo):
                sca.copy(op[:, :, :, :, :].rearrange("p s a q t -> p (s a q t)"),
                         state[:, 0, :, :].rearrange("p k t -> p (k t)")).then_inc(s_zero, 1)
            a.wait_ge(s_zero, 3)
            high_parts(0, (0,))
            chunk_vk(0)
            for c in range(NCH):
                i, ch = divmod(c, TPS)
                if ch == 0:
                    high_parts(c, (1,))
                if ch == 0 and i:
                    weighted(i - 1)
                    span_out(i - 1)
                if ch < TPS - 1:
                    high_parts(c + 1, (0, 1))
                for pr in range(2):
                    if pr == 1 and ch == TPS - 1:
                        high_parts(c + 1, (0,))
                    if c == GATE_CHUNK:
                        j = SECOND[pr]
                        bank7_to(("xn1T", j), xnT[:, SPAN * j:SPAN * j + SPAN])
                    a.wait_ge(s_o, 2 * c + pr + 1)
                    if i >= 2 and ch == 0 and pr == 0:
                        a.wait_ge(s_z, Z_at[("out", i - 2)] + 1)
                    sca.copy(oT[:, i % 2, HPG * pr:HPG * pr + HPG, P * ch:P * ch + P],
                             PS[:, 4 + pr, :].rearrange("p (k t) -> p k t", k=HPG)).then_inc(s_oT, 1)
                if c == GATE_CHUNK - 1:
                    root(B + 2, tiles=range(TPB, NT))
                if c == GATE_CHUNK:
                    a.wait_ge(s_glx, 1)
                    sca.activation(ex[:, :, :], ex[:, :, :], ACT.Exp).then_inc(s_ex, 1)
                chunk_vk(c + 1)
            weighted(NSPAN - 1)
            span_out(NSPAN - 1)

        @block.gpsimd
        def _(g_):
            po = nc.gpsimd
            po.memset(vaug[:, :, :, :], 0.0).then_inc(s_vaug, 1)
            g_.wait_ge(s_vaug, 1)
            po.memset(vaug[:, :, :, D0:D0 + 1], 1.0).then_inc(s_vaug, 1)
            for op in (q_op, k_op):
                po.memset(op[:, :, :, :].rearrange("p s h t -> p (s h t)").bitcast(F32), 0.0).then_inc(s_clear, 1)

            for k in range(NSPAN, 2 * NSPAN):
                left = rest[:, k - NSPAN, :]
                g_.wait_ge(s_part[0], k + 1)
                po.tensor_tensor(left, left, parts_of(k)[:, 0, :], ALU.subtract).then_inc(s_left, 1)
                g_.wait_ge(s_part[1], k + 1)
                g_.wait_ge(s_left, k + 1)
                po.tensor_tensor(parts_of(k)[:, 2, :], left, parts_of(k)[:, 1, :], ALU.subtract).then_inc(s_part[2], 1)

            def normalise_again(j):
                if j == 0:
                    g_.wait_ge(s_rstd2, 1)
                    g_.wait_ge(s_unit, UB_AT["xnT", SECOND[-1]] + 1)
                po.tensor_scalar(xn[:, j, :], xn[:, j, :], rstd2[:, j:j + 1], None, ALU.mult).then_inc(s_xn2, 1)

            def whole_sums():
                g_.wait_ge(s_gmax, 1)
                po.partition_all_reduce(small[:, 2:3], small[:, 0:1], P, RED.add).then_inc(s_gall, 1)
                po.partition_all_reduce(small[:, 3:4], small[:, 1:2], P, RED.max).then_inc(s_gall, 1)

            for s in range(NSTEP):
                at = 0
                for j, i0, nn in UNITS[s % NU][1]:
                    if i0 == j:
                        if at == 0:
                            g_.wait_ge(s_exp, GH * (s + 1))
                        blk = prob[:, s % P_SLOTS, :, at:at + P]
                        po.affine_select(out=blk, in_=blk, compare_op=ALU.is_ge, fill=0.0, base=0,
                                         pattern=[[0, GH], [1, P]], channel_multiplier=-1).then_inc(s_tri, 1)
                    at += nn
                if X2_STEP <= s < X2_STEP + NT:
                    normalise_again(s - X2_STEP)
                if s == FFN_STEP:
                    whole_sums()
            g_.wait_ge(s_acc, 1 + 2 * len(GROUPS))
            g_.wait_ge(s_big, 48)
            po.memset(state[:, :, :, :], 0.0).then_inc(s_zero, 1)

            def rotate(i, ms):
                if i == NSPAN:
                    return
                for m in ms:
                    n = PROJ * i + m
                    g_.wait_ge(s_turned[n % TURN_SLOTS], 32 * (n // TURN_SLOTS + 1))
                    dst, done = (kr[:, i % 2, m, :], s_kr) if m < 2 else (qr[:, i % 2, m - 2, :], s_qr)
                    po.tensor_tensor(dst, dst, turned[:, n % TURN_SLOTS, :], ALU.add).then_inc(done, 1)

            def fade_q(c):
                if c % TPB == 0:
                    return
                i, ch = divmod(c, TPS)
                g_.wait_ge(s_qr, QT * (i + 1))
                if c >= 2:
                    g_.wait_ge(s_o, 2 * (c - 1))
                po.tensor_tensor(qd[:, c % 2, :, :], qr[:, i % 2, :, P * ch:P * ch + P],
                                 K["qdec"].rearrange("p (k t) -> p k t", k=QT), ALU.mult).then_inc(s_qd, 1)

            def fade_v(c):
                if c % TPB == TPB - 1:
                    return
                kdec = K["kdec"].rearrange("p (g h o) -> p g h o", g=KV1, o=1)
                g_.wait_ge(s_zf, Z_at[("vk", c)] + 1)
                if c >= 2:
                    g_.wait_ge(s_kv, sums(c - 1))
                for g in range(KV1):
                    po.tensor_tensor(vdec[:, c % 2, g, :, :],
                                     vk[:, c % 2, D1 * g:D1 * g + D1].rearrange("p (o e) -> p o e", o=1).broadcast_to([P, HPG, D1]),
                                     kdec[:, g, :, :].broadcast_to([P, HPG, D1]), ALU.mult).then_inc(s_vd, 1)

            def fade_state(c):
                if c % TPB in (0, TPB - 1):
                    return
                g_.wait_ge(s_state, states(c))
                fade = K["blkdec"].rearrange("p (m o) -> p m o", o=1).broadcast_to([P, 2 * QT, D1])
                po.tensor_tensor(faded[:, :, :].rearrange("p k (q e) -> p (k q) e", q=2),
                                 state[:, c % 2, :, :].rearrange("p k (q e) -> p (k q) e", q=2), fade, ALU.mult).then_inc(s_faded, 1)

            rotate(0, range(PROJ))
            fade_v(0)
            for c in range(NCH):
                i, ch = divmod(c, TPS)
                if ch < TPS - 1 and c + 1 < NCH:
                    fade_q(c + 1)
                if ch:
                    rotate(i + 1, PROJ_OF[ch - 1])
                if ch == TPS - 1 and c + 1 < NCH:
                    fade_q(c + 1)
                if c + 1 < NCH:
                    fade_v(c + 1)
                    fade_state(c + 1)


def _tile_heads():
    import numpy as np
    return np.arange(H1).reshape(KV1 // 2, 2, HPG).transpose(0, 2, 1).reshape(QT, 2)


def _layer_1_constants():
    import numpy as np
    inv = 1.0 / 10000.0 ** (np.arange(0, D1, 2, dtype=np.float64) / D1)
    angle = np.outer(inv, np.arange(T, dtype=np.float64))
    cos = np.tile(np.repeat(np.cos(angle), 2, axis=0), (2, 1))
    sin = np.sin(angle)
    sin = np.tile(np.stack([sin, -sin], axis=1).reshape(D1, T), (2, 1))
    slope = (2.0 ** (-8.0 / H1 * np.arange(1, H1 + 1))).astype(np.float32).astype(np.float64)
    t = np.arange(P, dtype=np.float64)
    late = t[None, :] - t[:, None]
    decay = np.concatenate([np.where(late >= 0, np.exp(-slope[h] * np.maximum(late, 0)), 0.0) for h in range(H1)], axis=1)
    tiles = _tile_heads()
    qdec = np.concatenate([np.repeat(np.exp(-slope[tiles[k]][:, None] * (t + 1.0)), D1, axis=0) for k in range(QT)], axis=1)
    kdec = np.exp(-slope[None, :] * (P - 1.0 - t)[:, None])
    blkdec = np.broadcast_to(np.exp(-slope * P)[tiles].reshape(1, -1), (P, 2 * QT))
    parts = {"cos": cos, "sin": sin, "decay": decay, "qdec": qdec, "kdec": kdec, "blkdec": blkdec, }
    return np.concatenate([parts[n].astype(np.float32) for n in CCOLS], axis=1)


def _layer_0_constants():
    import numpy as np
    bf = lambda v: (v.astype(np.float32).view(np.uint32) >> 16).astype(np.uint16)
    t = np.arange(T)
    coarse, fine = t // 4 * 4, t % 4
    one = np.ones(T)
    k_rows = np.stack([coarse, fine, one, one, one, one, one])
    q_rows = np.stack([[s * one, s * one, -s * coarse, -s * fine] for s in 0.5 ** np.arange(1, H0 + 1)])
    row = np.arange(P)
    masks = np.stack([np.eye(P), np.where(row[None, :] > row[:, None], -1e30, 0.0)], axis=1)
    return bf(q_rows), bf(k_rows), bf(masks)


def kernel(**inputs):
    import numpy as np
    import concourse.bacc as bacc
    from concourse.bass_utils import run_bass_kernel_spmd

    a = {k: np.asarray(v) for k, v in inputs.items()}
    wq, wk, wv, wo = (a["L1_attn_" + n] for n in ("Wq", "Wk", "Wv", "Wo"))

    def paired(wt, heads):
        return wt.reshape(heads, 2, D1 // 2, C).transpose(0, 2, 1, 3).reshape(heads * D1, C)

    heads = _tile_heads().reshape(-1)
    by_tile = lambda wt: wt.reshape(H1, D1, -1)[heads].reshape(H1 * D1, -1)
    col = lambda v: v.reshape(C, 1)
    parts = {
        "ident": np.eye(P, dtype=np.float32), "attn": a["L0_attn_W_attn"], "proj": a["L0_attn_W_proj"], "ffn0": a["L0_ffn_weight"],
        "q1": by_tile(paired(wq, H1)).T, "k1": paired(wk, KV1).T, "v1": wv.T,
        "wo1": by_tile(wo.T).reshape(QT, P, C).transpose(1, 0, 2).reshape(P, QT * C),
        "lin1": a["L1_ffn_W_lin"].T,
        "gl1": np.concatenate([a["L1_ffn_gate_w"].T, a["L1_ffn_left"].transpose(1, 0, 2).reshape(C, E1 * R1)], axis=1),
        "bq": col(a["L0_attn_b_attn"][:C]), "bk": col(a["L0_attn_b_attn"][C:2 * C]),
        "bproj": col(a["L0_attn_b_proj"]), "lng": col(a["L0_ffn_ln_gamma"]), "lnb": col(a["L0_ffn_ln_beta"]),
        "blin": col(a["L1_ffn_b_lin"]), "bv": np.broadcast_to(a["L0_attn_b_attn"][2 * C:], (P, C)),
    }
    q_rows, k_rows, masks = _layer_0_constants()
    arrays = {
        "x_dram": np.ascontiguousarray(a["L0_attn_x"].reshape(B * T, C)),
        "w_dram": np.ascontiguousarray(np.concatenate([parts[n] for n in WCOLS], axis=1)),
        "right_dram": np.ascontiguousarray(a["L1_ffn_right"].reshape(E1 * R1, C)),
        "const_dram": _layer_1_constants(), "alibi_q_dram": q_rows, "alibi_k_dram": k_rows, "masks_dram": masks,
    }
    nc = bacc.Bacc("TRN2", target_bir_lowering=False, num_devices=1)
    args = [nc.dram_tensor(n, v.shape, mybir.dt.from_np(v.dtype), kind="ExternalInput").ap() for n, v in arrays.items()]
    args.append(nc.dram_tensor("out_dram", (B * T, C), F32, kind="ExternalOutput").ap())
    build(nc, *args)
    r = run_bass_kernel_spmd(nc, [arrays], core_ids=[0])
    return r.results[0]["out_dram"].reshape(B, T, C)
```
